# Optimizing a Trainium2 kernel written in Bass

```python
import numpy as np
import jax
import jax.numpy as jnp

def _softmax(x, axis=-1):
    return jax.nn.softmax(x, axis=axis)

def _gelu(x):
    return jax.nn.gelu(x, approximate=True)

def _silu(x):
    return jax.nn.silu(x)

def _sigmoid(x):
    return jax.nn.sigmoid(x)

def _layernorm(x, axis=-1, eps=1e-05):
    m = jnp.mean(x, axis=axis, keepdims=True)
    v = jnp.var(x, axis=axis, keepdims=True)
    return (x - m) / jnp.sqrt(v + eps)

def _scatter_add(tgt, idx, src, axis=0):
    return tgt.at[idx].add(src)

def _segment_sum(src, seg, n):
    return jax.ops.segment_sum(src, seg, n)
kernel_name = 'mk_decoder_postln_d2_seqx_r8_daf48c'

def setup_inputs(seed: int=0):
    np.random.seed(seed)
    _w = jnp.asarray

    def _rec_inputs():
        import jax
        import jax.numpy as jnp
        _rk = jax.random.key(seed)
        x = -0.000125 + 0.9999 * jax.random.normal(jax.random.fold_in(_rk, 1), (4, 256, 256), jnp.float32)
        _lenS = 256 - jax.random.randint(jax.random.fold_in(_rk, 7), (4,), 0, max(1, 256 // 4) + 1, jnp.int32)
        _lenS2 = 256 - jax.random.randint(jax.random.fold_in(_rk, 8), (4,), 0, max(1, 256 // 4) + 1, jnp.int32)
        itok_BxS_13_99985 = jax.random.randint(jax.random.fold_in(_rk, 11), (4, 256), 13, 99986, jnp.int32)
        _ctx_2048P = jax.random.normal(jax.random.fold_in(_rk, 12), (4, 16, 256), jnp.float32)
        _ctx_2048c = jax.random.dirichlet(jax.random.fold_in(_rk, 512), 0.3 * jnp.ones((16,), jnp.float32), (4, 256))
        _ctx_2048t = jnp.einsum('bsk,bkd->bsd', _ctx_2048c, _ctx_2048P)
        _ctx_2048t = _ctx_2048t * jax.lax.rsqrt(jnp.mean(jnp.square(_ctx_2048t)) + 1e-12) * 0.953939
        ctx_2048 = 6.82029e-06 + 0.0200006 * (_ctx_2048t + 0.3 * jax.random.normal(jax.random.fold_in(_rk, 612), (4, 256, 256), jnp.float32))
        _validS = jnp.arange(256)[None, :] < _lenS[:, None]
        _validS2 = jnp.arange(256)[None, :] < _lenS2[:, None]
        _causal = jnp.tril(jnp.ones((256, 256), dtype=bool))
        mask_BxS2_bk0 = jnp.logical_not(jnp.broadcast_to(_validS2[:, :], (4, 256)))
        return (x, itok_BxS_13_99985, ctx_2048, mask_BxS2_bk0)
    x, itok_BxS_13_99985, ctx_2048, mask_BxS2_bk0 = _rec_inputs()

    def _L0_attn_setup():
        import jax, jax.numpy as jnp
        import numpy as np
        HID = 256
        HEADS = 16
        HD = HID // HEADS
        EPS = 1e-06

        def _heads(x, b, s):
            return x.reshape(b, s, HEADS, HD).transpose(0, 2, 1, 3)
        key = jax.random.key(seed)
        ks = jax.random.split(key, 9)
        s = 1.0 / np.sqrt(HID)
        return {'hidden_states': jax.random.normal(ks[0], (4, 512, HID), jnp.float32), 'q_w': jax.random.normal(ks[1], (HID, HID), jnp.float32) * s, 'q_b': jnp.zeros((HID,), jnp.float32), 'k_w': jax.random.normal(ks[2], (HID, HID), jnp.float32) * s, 'k_b': jnp.zeros((HID,), jnp.float32), 'v_w': jax.random.normal(ks[3], (HID, HID), jnp.float32) * s, 'v_b': jnp.zeros((HID,), jnp.float32), 'o_w': jax.random.normal(ks[4], (HID, HID), jnp.float32) * s, 'o_b': jnp.zeros((HID,), jnp.float32)}
    _L0_attn_all = _L0_attn_setup()
    _L0_attn_in = {k: v for k, v in _L0_attn_all.items() if k in ('q_w', 'q_b', 'k_w', 'k_b', 'v_w', 'v_b', 'o_w', 'o_b')}
    del _L0_attn_all

    def _L0_xattn_setup():
        import jax, jax.numpy as jnp
        import numpy as np
        B, S, D = (4, 512, 256)
        E = 4
        F = 1024 // E
        VOCAB = 12500
        key = jax.random.key(seed)
        k1, k2, k3, k4, k5 = jax.random.split(key, 5)
        hidden_states = jax.random.normal(k1, (B, S, D), dtype=jnp.float32)
        token_ids = jax.random.randint(k2, (B, S), 0, VOCAB, dtype=jnp.int64)
        Wg = jax.random.normal(k3, (E, F, D), dtype=jnp.float32) * 0.02
        Wu = jax.random.normal(k4, (E, F, D), dtype=jnp.float32) * 0.02
        Wd = jax.random.normal(k5, (E, D, F), dtype=jnp.float32) * 0.02
        return {'hidden_states': hidden_states, 'token_ids': token_ids, 'Wg': Wg, 'Wu': Wu, 'Wd': Wd}
    _L0_xattn_all = _L0_xattn_setup()
    _L0_xattn_in = {k: v for k, v in _L0_xattn_all.items() if k in ()}
    del _L0_xattn_all

    def _L0_ffn_setup():
        import jax, jax.numpy as jnp
        import numpy as np
        GOLDEN_CENTER = 1.0 / np.e
        GOLDEN_LOWER = 0.5 - np.log(4.0 / 3.0)
        GOLDEN_UPPER = 0.5

        def _golden_weights(x, Wr, temperature):
            inh = jax.nn.sigmoid(x @ Wr / temperature)
            in_zone = (inh >= GOLDEN_LOWER) & (inh <= GOLDEN_UPPER)
            distance = jnp.abs(inh - GOLDEN_CENTER)
            weights = jnp.exp(-distance / 0.1) * in_zone.astype(x.dtype)
            wsum = jnp.sum(weights, axis=-1, keepdims=True)
            no_expert = wsum < 1e-08
            fb = jnp.exp(-distance / 0.3)
            _, top2 = jax.lax.top_k(fb, 2)
            fb_mask = jnp.sum(jax.nn.one_hot(top2, weights.shape[-1], dtype=x.dtype), axis=-2)
            fb_w = fb * fb_mask
            fb_w = fb_w / jnp.maximum(jnp.sum(fb_w, axis=-1, keepdims=True), 1e-08)
            weights = jnp.where(no_expert, fb_w, weights)
            weights = weights / jnp.maximum(jnp.sum(weights, axis=-1, keepdims=True), 1e-08)
            return weights
        key = jax.random.key(seed)
        ks = jax.random.split(key, 5)
        B, T, D, E, F = (2, 256, 256, 8, 256)
        s_in = 1.0 / np.sqrt(D)
        s_f = 1.0 / np.sqrt(F)
        return {'x': jax.random.normal(ks[0], (B, T, D), dtype=jnp.float32), 'Wg': jax.random.normal(ks[1], (E, D, F), dtype=jnp.float32) * s_in, 'Wu': jax.random.normal(ks[2], (E, D, F), dtype=jnp.float32) * s_in, 'Wd': jax.random.normal(ks[3], (E, F, D), dtype=jnp.float32) * s_f, 'Wr': jax.random.normal(ks[4], (D, E), dtype=jnp.float32) * s_in, 'temperature': jnp.ones((1,), dtype=jnp.float32)}
    _L0_ffn_all = _L0_ffn_setup()
    _L0_ffn_in = {k: v for k, v in _L0_ffn_all.items() if k in ('Wg', 'Wu', 'Wd', 'Wr', 'temperature')}
    del _L0_ffn_all

    def _L1_attn_setup():
        import jax, jax.numpy as jnp
        import numpy as np
        EMBED_DIM = 256
        NUM_HEADS = 16
        HEAD_DIM = EMBED_DIM // NUM_HEADS
        GROUP = 32
        NEG = -1000000000.0

        def _s2_attn(x, Wq, bq, Wk, bk, Wv, bv):
            B, N, C = x.shape
            H, hd, gs = (NUM_HEADS, HEAD_DIM, GROUP)
            G = N // gs
            half = H // 2

            def heads(t):
                return t.reshape(B, N, H, hd).transpose(0, 2, 1, 3)
            q = heads(x @ Wq.T + bq)
            k = heads(x @ Wk.T + bk)
            v = heads(x @ Wv.T + bv)

            def shift(t, s):
                return jnp.concatenate([t[:, :half], jnp.roll(t[:, half:], s, axis=2)], axis=1)
            q, k, v = (shift(q, -(gs // 2)), shift(k, -(gs // 2)), shift(v, -(gs // 2)))
            qg = q.reshape(B, H, G, gs, hd)
            kg = k.reshape(B, H, G, gs, hd)
            vg = v.reshape(B, H, G, gs, hd)
            scores = jnp.einsum('bhgqd,bhgkd->bhgqk', qg, kg) / np.sqrt(hd).astype(x.dtype)
            causal = jnp.triu(jnp.ones((gs, gs), bool), 1)
            scores = jnp.where(causal, NEG, scores)
            attn = jax.nn.softmax(scores, axis=-1)
            out = jnp.einsum('bhgqk,bhgkd->bhgqd', attn, vg).reshape(B, H, N, hd)
            out = shift(out, gs // 2)
            return out.transpose(0, 2, 1, 3).reshape(B, N, C)
        key = jax.random.key(seed)
        ks = jax.random.split(key, 4)
        B, N, C = (2, 1024, EMBED_DIM)
        s = 1.0 / np.sqrt(C).astype(np.float32)
        return {'x': jax.random.normal(ks[0], (B, N, C), jnp.float32), 'Wq': jax.random.normal(ks[1], (C, C), jnp.float32) * s, 'bq': jnp.zeros((C,), jnp.float32), 'Wk': jax.random.normal(ks[2], (C, C), jnp.float32) * s, 'bk': jnp.zeros((C,), jnp.float32), 'Wv': jax.random.normal(ks[3], (C, C), jnp.float32) * s, 'bv': jnp.zeros((C,), jnp.float32)}
    _L1_attn_all = _L1_attn_setup()
    _L1_attn_in = {k: v for k, v in _L1_attn_all.items() if k in ('Wq', 'bq', 'Wk', 'bk', 'Wv', 'bv')}
    del _L1_attn_all

    def _L1_xattn_setup():
        import jax, jax.numpy as jnp
        import numpy as np
        key = jax.random.key(seed)
        k1, k2, k3 = jax.random.split(key, 3)
        B, S, D, M = (8, 256, 256, 128)
        hidden_states = jax.random.normal(k1, (B, S, D), dtype=jnp.float32)
        memory_tokens = jax.random.normal(k2, (B, M, D), dtype=jnp.float32)
        memory_mask = jax.random.randint(k3, (B, M), 0, 2).astype(jnp.bool_)
        return {'hidden_states': hidden_states, 'memory_tokens': memory_tokens, 'memory_mask': memory_mask}
    _L1_xattn_all = _L1_xattn_setup()
    _L1_xattn_in = {k: v for k, v in _L1_xattn_all.items() if k in ()}
    del _L1_xattn_all

    def _L1_ffn_setup():
        import jax, jax.numpy as jnp
        import numpy as np
        TOP_K = 2
        key = jax.random.key(seed)
        ks = jax.random.split(key, 6)
        B, S, H, F, E = (1, 256, 256, 176, 8)
        Fs = 2 * F
        std = jnp.float32(0.02)
        return {'hidden_states': jax.random.normal(ks[0], (B, S, H), jnp.float32), 'gate_weight': jax.random.normal(ks[1], (E, H), jnp.float32) * std, 'gate_up_weights': jax.random.normal(ks[2], (E, 2 * F, H), jnp.float32) * std, 'down_weights': jax.random.normal(ks[3], (E, H, F), jnp.float32) * std, 'shared_gate_up': jax.random.normal(ks[4], (2 * Fs, H), jnp.float32) * std, 'shared_down': jax.random.normal(ks[5], (H, Fs), jnp.float32) * std}
    _L1_ffn_all = _L1_ffn_setup()
    _L1_ffn_in = {k: v for k, v in _L1_ffn_all.items() if k in ('gate_weight', 'gate_up_weights', 'down_weights', 'shared_gate_up', 'shared_down')}
    del _L1_ffn_all
    return {'x': x, 'itok_BxS_13_99985': itok_BxS_13_99985, 'ctx_2048': ctx_2048, 'mask_BxS2_bk0': mask_BxS2_bk0, 'L0_attn_q_w': _L0_attn_in['q_w'], 'L0_attn_q_b': _L0_attn_in['q_b'], 'L0_attn_k_w': _L0_attn_in['k_w'], 'L0_attn_k_b': _L0_attn_in['k_b'], 'L0_attn_v_w': _L0_attn_in['v_w'], 'L0_attn_v_b': _L0_attn_in['v_b'], 'L0_attn_o_w': _L0_attn_in['o_w'], 'L0_attn_o_b': _L0_attn_in['o_b'], 'L0_ffn_Wg': _L0_ffn_in['Wg'], 'L0_ffn_Wu': _L0_ffn_in['Wu'], 'L0_ffn_Wd': _L0_ffn_in['Wd'], 'L0_ffn_Wr': _L0_ffn_in['Wr'], 'L0_ffn_temperature': _L0_ffn_in['temperature'], 'L1_attn_Wq': _L1_attn_in['Wq'], 'L1_attn_bq': _L1_attn_in['bq'], 'L1_attn_Wk': _L1_attn_in['Wk'], 'L1_attn_bk': _L1_attn_in['bk'], 'L1_attn_Wv': _L1_attn_in['Wv'], 'L1_attn_bv': _L1_attn_in['bv'], 'L1_ffn_gate_weight': _L1_ffn_in['gate_weight'], 'L1_ffn_gate_up_weights': _L1_ffn_in['gate_up_weights'], 'L1_ffn_down_weights': _L1_ffn_in['down_weights'], 'L1_ffn_shared_gate_up': _L1_ffn_in['shared_gate_up'], 'L1_ffn_shared_down': _L1_ffn_in['shared_down']}

def reference(x, itok_BxS_13_99985, ctx_2048, mask_BxS2_bk0, L0_attn_q_w, L0_attn_q_b, L0_attn_k_w, L0_attn_k_b, L0_attn_v_w, L0_attn_v_b, L0_attn_o_w, L0_attn_o_b, L0_ffn_Wg, L0_ffn_Wu, L0_ffn_Wd, L0_ffn_Wr, L0_ffn_temperature, L1_attn_Wq, L1_attn_bq, L1_attn_Wk, L1_attn_bk, L1_attn_Wv, L1_attn_bv, L1_ffn_gate_weight, L1_ffn_gate_up_weights, L1_ffn_down_weights, L1_ffn_shared_gate_up, L1_ffn_shared_down):
    import jax
    import jax.numpy as jnp

    def _L0_attn_ref(hidden_states, q_w, q_b, k_w, k_b, v_w, v_b, o_w, o_b):
        import jax, jax.numpy as jnp
        import numpy as np
        HID = 256
        HEADS = 16
        HD = HID // HEADS
        EPS = 1e-06

        def _heads(x, b, s):
            return x.reshape(b, s, HEADS, HD).transpose(0, 2, 1, 3)
        b, s, _ = hidden_states.shape
        q = _heads(hidden_states @ q_w.T + q_b, b, s)
        k = _heads(hidden_states @ k_w.T + k_b, b, s)
        v = _heads(hidden_states @ v_w.T + v_b, b, s)
        qp = jax.nn.elu(q) + 1.0
        kp = jax.nn.elu(k) + 1.0
        kv = jnp.einsum('bhsd,bhse->bhde', kp, v)
        z = jnp.einsum('bhsd,bhd->bhs', qp, kp.sum(axis=2))[..., None]
        attn = jnp.einsum('bhsd,bhde->bhse', qp, kv) / (z + EPS)
        out = attn.transpose(0, 2, 1, 3).reshape(b, s, HID)
        return out @ o_w.T + o_b

    def _L0_xattn_ref(hidden_states, token_ids, Wg, Wu, Wd):
        import jax, jax.numpy as jnp
        import numpy as np
        B, S, D = (4, 512, 256)
        E = 4
        F = 1024 // E
        VOCAB = 12500
        tokens_per_expert = VOCAB // E
        tid = jnp.clip(token_ids, 0, VOCAB - 1)
        expert_ids = jnp.minimum(tid // tokens_per_expert, E - 1)
        out = jnp.zeros_like(hidden_states)
        for e in range(E):
            g = jax.nn.silu(jnp.einsum('bsd,fd->bsf', hidden_states, Wg[e]))
            u = jnp.einsum('bsd,fd->bsf', hidden_states, Wu[e])
            y = jnp.einsum('bsf,df->bsd', g * u, Wd[e])
            out = jnp.where((expert_ids == e)[..., None], y, out)
        return out

    def _L0_ffn_ref(x, Wg, Wu, Wd, Wr, temperature):
        import jax, jax.numpy as jnp
        import numpy as np
        GOLDEN_CENTER = 1.0 / np.e
        GOLDEN_LOWER = 0.5 - np.log(4.0 / 3.0)
        GOLDEN_UPPER = 0.5

        def _golden_weights(x, Wr, temperature):
            inh = jax.nn.sigmoid(x @ Wr / temperature)
            in_zone = (inh >= GOLDEN_LOWER) & (inh <= GOLDEN_UPPER)
            distance = jnp.abs(inh - GOLDEN_CENTER)
            weights = jnp.exp(-distance / 0.1) * in_zone.astype(x.dtype)
            wsum = jnp.sum(weights, axis=-1, keepdims=True)
            no_expert = wsum < 1e-08
            fb = jnp.exp(-distance / 0.3)
            _, top2 = jax.lax.top_k(fb, 2)
            fb_mask = jnp.sum(jax.nn.one_hot(top2, weights.shape[-1], dtype=x.dtype), axis=-2)
            fb_w = fb * fb_mask
            fb_w = fb_w / jnp.maximum(jnp.sum(fb_w, axis=-1, keepdims=True), 1e-08)
            weights = jnp.where(no_expert, fb_w, weights)
            weights = weights / jnp.maximum(jnp.sum(weights, axis=-1, keepdims=True), 1e-08)
            return weights
        weights = _golden_weights(x, Wr, temperature)
        gate = jnp.einsum('btd,edf->betf', x, Wg)
        up = jnp.einsum('btd,edf->betf', x, Wu)
        h = jax.nn.silu(gate) * up
        e_out = jnp.einsum('betf,efd->betd', h, Wd)
        out = jnp.einsum('bte,betd->btd', weights, e_out)
        return out

    def _L1_attn_ref(x, Wq, bq, Wk, bk, Wv, bv):
        import jax, jax.numpy as jnp
        import numpy as np
        EMBED_DIM = 256
        NUM_HEADS = 16
        HEAD_DIM = EMBED_DIM // NUM_HEADS
        GROUP = 32
        NEG = -1000000000.0

        def _s2_attn(x, Wq, bq, Wk, bk, Wv, bv):
            B, N, C = x.shape
            H, hd, gs = (NUM_HEADS, HEAD_DIM, GROUP)
            G = N // gs
            half = H // 2

            def heads(t):
                return t.reshape(B, N, H, hd).transpose(0, 2, 1, 3)
            q = heads(x @ Wq.T + bq)
            k = heads(x @ Wk.T + bk)
            v = heads(x @ Wv.T + bv)

            def shift(t, s):
                return jnp.concatenate([t[:, :half], jnp.roll(t[:, half:], s, axis=2)], axis=1)
            q, k, v = (shift(q, -(gs // 2)), shift(k, -(gs // 2)), shift(v, -(gs // 2)))
            qg = q.reshape(B, H, G, gs, hd)
            kg = k.reshape(B, H, G, gs, hd)
            vg = v.reshape(B, H, G, gs, hd)
            scores = jnp.einsum('bhgqd,bhgkd->bhgqk', qg, kg) / np.sqrt(hd).astype(x.dtype)
            causal = jnp.triu(jnp.ones((gs, gs), bool), 1)
            scores = jnp.where(causal, NEG, scores)
            attn = jax.nn.softmax(scores, axis=-1)
            out = jnp.einsum('bhgqk,bhgkd->bhgqd', attn, vg).reshape(B, H, N, hd)
            out = shift(out, gs // 2)
            return out.transpose(0, 2, 1, 3).reshape(B, N, C)
        return _s2_attn(x, Wq, bq, Wk, bk, Wv, bv)

    def _L1_xattn_ref(hidden_states, memory_tokens, memory_mask):
        import jax, jax.numpy as jnp
        import numpy as np
        B, S, D = hidden_states.shape
        scale = 1.0 / jnp.sqrt(jnp.asarray(D, hidden_states.dtype))
        scores = jnp.einsum('bsd,bmd->bsm', hidden_states, memory_tokens) * scale
        neg_inf = jnp.asarray(-1e+30, scores.dtype)
        scores = jnp.where(memory_mask[:, None, :], scores, neg_inf)
        attn = jax.nn.softmax(scores, axis=-1)
        readout = jnp.einsum('bsm,bmd->bsd', attn, memory_tokens)
        valid_b = jnp.any(memory_mask, axis=-1)
        out = jnp.where(valid_b[:, None, None], readout, jnp.zeros_like(readout))
        return out

    def _L1_ffn_ref(hidden_states, gate_weight, gate_up_weights, down_weights, shared_gate_up, shared_down):
        import jax, jax.numpy as jnp
        import numpy as np
        TOP_K = 2
        B, S, H = hidden_states.shape
        E, twoF, _ = gate_up_weights.shape
        F = twoF // 2
        T = B * S
        x = hidden_states.reshape(T, H)
        logits = x @ gate_weight.T
        scores = jax.nn.softmax(logits, axis=-1)
        topk_w, topk_idx = jax.lax.top_k(scores, TOP_K)
        combine = jnp.zeros((T, E), x.dtype).at[jnp.arange(T)[:, None], topk_idx].add(topk_w)
        gu = jnp.einsum('th,efh->tef', x, gate_up_weights)
        act = jax.nn.silu(gu[..., :F]) * gu[..., F:]
        y = jnp.einsum('tef,te,ehf->th', act, combine, down_weights)
        Fs = shared_gate_up.shape[0] // 2
        sgu = x @ shared_gate_up.T
        sact = jax.nn.silu(sgu[:, :Fs]) * sgu[:, Fs:]
        y = y + sact @ shared_down.T
        return y.reshape(B, S, H)
    x = _layernorm(x + _L0_attn_ref(x, L0_attn_q_w, L0_attn_q_b, L0_attn_k_w, L0_attn_k_b, L0_attn_v_w, L0_attn_v_b, L0_attn_o_w, L0_attn_o_b), axis=-1)
    x = _layernorm(x + _L0_xattn_ref(x, itok_BxS_13_99985, ctx_2048, ctx_2048, ctx_2048), axis=-1)
    x = _layernorm(x + _L0_ffn_ref(x, L0_ffn_Wg, L0_ffn_Wu, L0_ffn_Wd, L0_ffn_Wr, L0_ffn_temperature), axis=-1)
    x = _layernorm(x + _L1_attn_ref(x, L1_attn_Wq, L1_attn_bq, L1_attn_Wk, L1_attn_bk, L1_attn_Wv, L1_attn_bv), axis=-1)
    x = _layernorm(x + _L1_xattn_ref(x, ctx_2048, mask_BxS2_bk0), axis=-1)
    x = _layernorm(x + _L1_ffn_ref(x, L1_ffn_gate_weight, L1_ffn_gate_up_weights, L1_ffn_down_weights, L1_ffn_shared_gate_up, L1_ffn_shared_down), axis=-1)
    return x

_drawn_inputs = setup_inputs


def setup_inputs(seed=0):
    import zlib

    import numpy as np

    out = dict(_drawn_inputs(seed))
    spreads = {'L0_attn_q_b': (0.0, 0.8),
     'L0_attn_k_b': (0.0, 0.601),
     'L0_attn_v_b': (0.0, 0.1),
     'L0_attn_o_b': (0.0, 0.1),
     'L1_attn_bq': (0.0, 0.269),
     'L1_attn_bk': (0.0, 0.8),
     'L1_attn_bv': (0.0, 0.1)}
    factors = {'L1_ffn_gate_weight': 8.0,
     'L1_ffn_gate_up_weights': 8.0,
     'L1_ffn_down_weights': 8.0,
     'L1_ffn_shared_gate_up': 2.847,
     'L1_ffn_shared_down': 2.85}
    for name, (base, spread) in spreads.items():
        noise = np.random.default_rng([zlib.crc32(name.encode()), seed]).standard_normal(out[name].shape)
        drawn = base * np.exp(spread * noise) if base else spread * noise
        out[name] = jnp.asarray(drawn.astype(out[name].dtype))
    for name, factor in factors.items():
        out[name] = (out[name] * factor).astype(out[name].dtype)
    return out
```

```python
from contextlib import ExitStack

import numpy as np

import concourse.bass as bass
from concourse import mybir

F32 = mybir.dt.float32
F32R = mybir.dt.float32r
I32 = mybir.dt.int32
U32 = mybir.dt.uint32
U8 = mybir.dt.uint8
ALU = mybir.AluOpType
ACT = mybir.ActivationFunctionType
AXX = mybir.AxisListType.X

P = 128
B, S, D = 4, 256, 256
TILES = B * S // P
HT = TILES // 2
KC = D // P
HEADS, HD = 16, 16
HC = HEADS // KC
GS = 32
ROLL = GS // 2
SX = S + ROLL
NG = P // GS
E0, EX, E1, F1 = 8, 4, 8, 176
CH_R = E1 * F1 // P
FS = 2 * F1
CH_S = -(-FS // P)
PACKS_X0, PACKS_F0, PACKS_X1, PACKS_F1 = EX, E0, B, CH_R + CH_S
W_X0, W_F0, W_X1, W_F1 = KC * D, 3 * KC * D, 2 * KC * D, 3 * D + P
BASE_X0, BASE_F0 = 0, PACKS_X0
BASE_X1 = BASE_F0 + PACKS_F0
BASE_F1 = BASE_X1 + PACKS_X1
WMAX = W_F0
VOCAB_CUT = 12500 // EX
LN_EPS = 1e-5
GOLD_C = 1.0 / np.e
GOLD_LO = 0.5 - np.log(4.0 / 3.0)
GOLD_HI = 0.5
NEG = -1e9
NEG_X = -1e30
DOWN_0, M1_0 = 2, 1
BLK = P + HC
CONST_W = P + BLK + GS + 8


def decoder_program(nc, x_rows, x_cols, ids, pad_mask, w_attn0, w_attn1, bias_cols, bias_rows,
                    w_route, temperature, consts, pk_x0, pk_f0, pk_x1, pk_f1, out):
    with ExitStack() as ctx:
        def sb(name, shape, dt=F32):
            return ctx.enter_context(nc.sbuf_tensor(name, shape, dt))

        def sem(name):
            return ctx.enter_context(nc.semaphore(name))

        bank = [ctx.enter_context(nc.psum_tensor(f"bank{i}", [P, 512], F32)) for i in range(8)]

        x_tok = sb("x_tok", [P, TILES, D])
        xT_hi = sb("xT_hi", [P, KC, B, SX], F32R)
        xT_lo = sb("xT_lo", [P, KC, B, SX], F32R)
        wa_raw = sb("wa_raw", [P, KC, 4 * D])
        wa_hi = sb("wa_hi", [P, KC, 4 * D], F32R)
        wa_lo = sb("wa_lo", [P, KC, 4 * D], F32R)
        pk_raw = sb("pk_raw", [P, 2, WMAX])
        pk_hi = sb("pk_hi", [P, 2, WMAX], F32R)
        pk_lo = sb("pk_lo", [P, 2, WMAX], F32R)
        q_buf = sb("q_buf", [P, KC, TILES * P])
        k_buf = sb("k_buf", [P, 2048])
        k_tok = k_buf[:, :].rearrange("p (t d) -> p t d", t=TILES)
        k_T = k_buf[:, :].rearrange("p (c s) -> p c s", c=KC)
        v_buf = sb("v_buf", [P, TILES, KC, P + 1])
        v1 = v_buf[:, :, :, :].rearrange("p t c d -> p t (c d)")
        kx = sb("kx", [P, 4, 4 * D])
        ek = kx[:, 0:2, :].rearrange("p a (t d) -> p (a t) d", d=D)
        eq = kx[:, 2:4, :]
        state = sb("state", [P, B * KC, BLK])
        o_roll = state[:, :, 0:P]
        sm = sb("sm", [P, 4, 512])
        pT = sb("pT", [P, 2, 512])
        p_bd = sb("p_bd", [P, 2, HEADS, P])
        h_hi = sb("h_hi", [P, 2, 1024], F32R)
        h_lo = sb("h_lo", [P, 2, 1024], F32R)
        scratch = sb("scratch", [P, 2048])
        sil = scratch[:, 0:1024].rearrange("p (r n) -> p r n", r=2)
        hraw = scratch[:, 1024:2048].rearrange("p (r n) -> p r n", r=2)
        o_tok = scratch[:, :].rearrange("p (t d) -> p t d", t=TILES)
        keep = sb("keep", [P, B, S])
        fill = sb("fill", [P, B, S])
        mask_w = sb("mask_w", [P, B * S // 4], U32)
        valid = sb("valid", [P, B])
        brow = sb("brow", [P, 4 * D])
        bcol = sb("bcol", [P, 6])
        con = sb("con", [P, CONST_W])
        ident = con[:, 0:P]
        headmask = con[:, P:2 * P]
        head8 = con[:, 2 * P:2 * P + HC]
        causal = con[:, P + BLK:P + BLK + GS]
        iota8 = con[:, P + BLK + GS:CONST_W]
        zero_r = sb("zero_r", [P, 512], F32R)
        rw_raw = sb("rw_raw", [P, KC, 2 * E0])
        rw_hi = sb("rw_hi", [P, KC, 2 * E0], F32R)
        rw_lo = sb("rw_lo", [P, KC, 2 * E0], F32R)
        temp = sb("temp", [P, 2])
        ids_i = sb("ids_i", [P, TILES], I32)
        ids_f = sb("ids_f", [P, TILES])
        route0 = sb("route0", [P, TILES, EX])
        gold = sb("gold", [P, TILES, E0])
        stats = sb("stats", [P, HT, 6])
        mv = sb("mv", [P, TILES, 2])
        var_e = sb("var_e", [P, TILES])
        rstd = sb("rstd", [P, TILES])
        mhalf = sb("mhalf", [P, HT])
        mx = sb("mx", [P, TILES, HEADS])
        rs = sb("rs", [P, TILES, HEADS])
        lg = sb("lg", [P, TILES, E0])
        inh = sb("inh", [P, TILES, E0])
        dist = sb("dist", [P, TILES, E0])
        wz = sb("wz", [P, TILES, E0])
        fb = sb("fb", [P, TILES, E0])
        zone = sb("zone", [P, TILES, E0])
        pick = sb("pick", [P, TILES, E0])
        top = sb("top", [P, TILES, 8])
        top_i = sb("top_i", [P, TILES, 8], U32)
        top_f = sb("top_f", [P, TILES, 8])
        s1 = sb("s1", [P, TILES])
        s2 = sb("s2", [P, TILES])
        none_in = sb("none_in", [P, TILES])
        stack = sb("stack", [P, TILES, 32])
        cw_r = sb("cw_r", [P, HT, E1], F32R)
        cwT = sb("cwT", [32, TILES * P], F32R)

        sems = {}

        def sm_(name):
            if name not in sems:
                sems[name] = sem(name)
            return sems[name]

        names = """in_x in_xT in_w0 in_w1 in_small out_done
            xraw_hi wa_hi_done wa_lo_done small_ready ones_ready
            a0_q_ps a0_eq a0_q a0_kv_ps a0_kv a0_ek a0_ek1 a0_kp a0_st_ps a0_state a0_at_ps
            a0_attn a0_aT_ps a0_aT_hi a0_aT_lo a0_o_ps a0_res a0_xb
            ln_var ln_rstd ln_done xt_ps xt_hi xt_lo
            gate_ready up_ready cw_ready silu_done m1_done hid_mul hid_hi hid_lo
            out_ready acc_done down_done pack_hi pack_lo
            rt_ps rt_lg rt_sig rt_dist rt_exp rt_done rt_exp1 rt_stack cwT_ps cwT_done
            a1_q_ps a1_k_ps a1_q a1_k a1_v_ps a1_v a1_kx a1_s_ps a1_s a1_sub a1_exp a1_pT a1_bd
            a1_o_ps a1_o a1_oroll0 a1_oroll1 a1_res a1_max bd_zero
            x1_s_ps x1_s x1_add x1_max x1_exp x1_pT_ps x1_pT_hi x1_pT_lo x1_o_ps x1_w x1_out
            dve_link pool_link mask_ready acc_open raw0 raw1 fin""".split()
        for n in names:
            sm_(n)
        raw_loaded = [sems["raw0"], sems["raw1"]]

        def tile_cols(T):
            return T // 2, (T % 2) * P

        def x_half(buf, c, h, roll=0):
            return buf[:, c, 2 * h:2 * h + 2, roll:roll + S]

        def x_tile(buf, c, T, roll=0):
            b, o = tile_cols(T)
            return buf[:, c, b, roll + o:roll + o + P]

        block = ctx.enter_context(nc.Block())

        @block.sync
        def _(sp):
            sp.dma_start(q_buf[:, :, :], x_cols.rearrange("(c p) t -> p c t", p=P)).then_inc(sems["in_xT"], 16)
            sp.dma_start(wa_raw[:, :, :], w_attn0).then_inc(sems["in_w0"], 16)
            sp.dma_start(con[:, :], consts).then_inc(sems["in_small"], 16)
            sp.dma_start(bcol[:, :], bias_cols).then_inc(sems["in_small"], 16)
            sp.dma_start(brow[:, :], bias_rows.partition_broadcast(P)).then_inc(sems["in_small"], 16)
            sp.dma_start(x_tok[:, :, :], x_rows.rearrange("(t p) d -> p t d", p=P)).then_inc(sems["in_x"], 16)
            sp.dma_start(rw_raw[:, :, :], w_route).then_inc(sems["in_small"], 16)
            sp.dma_start(temp[:, 0:1], temperature.partition_broadcast(P)).then_inc(sems["in_small"], 16)
            sp.dma_start(ids_i[:, :], ids).then_inc(sems["in_small"], 16)
            sp.dma_start(mask_w[:, :], pad_mask.partition_broadcast(P)).then_inc(sems["in_small"], 16)

            def load(p, slot, src, width):
                if not (isinstance(p, int) and p < 2):
                    sp.wait_ge(sems["pack_lo"], p - 1)
                sp.dma_start(pk_raw[:, slot, 0:width], src).then_inc(raw_loaded[slot], 16)

            for p in range(PACKS_X0):
                load(p, p % 2, pk_x0[p, :, :], W_X0)
            sp.wait_ge(sems["wa_lo_done"], 1)
            sp.dma_start(wa_raw[:, :, 0:3 * D], w_attn1).then_inc(sems["in_w1"], 16)
            with sp.Fori(0, PACKS_F0 // 2) as i:
                for k in range(2):
                    load(i * 2 + (BASE_F0 + k), k, pk_f0[bass.ds(i * 2 + k, 1), :, :].rearrange("a p n -> (a p) n"), W_F0)
            for b in range(PACKS_X1):
                load(BASE_X1 + b, b % 2, pk_x1[b, :, :], W_X1)
            for h in range(2):
                sp.wait_ge(sems["a1_o"], HT * (h + 1))
                a, z = HT * h, HT * (h + 1)
                sp.dma_start(o_roll[ROLL:P, a:z, :], o_tok[0:P - ROLL, a:z, P:D]).then_inc(sems[f"a1_oroll{h}"], 16)
                sp.dma_start(o_roll[0:ROLL, a:z:2, :], o_tok[P - ROLL:P, a + 1:z:2, P:D]).then_inc(sems[f"a1_oroll{h}"], 16)
                sp.dma_start(o_roll[0:ROLL, a + 1:z:2, :], o_tok[P - ROLL:P, a:z:2, P:D]).then_inc(sems[f"a1_oroll{h}"], 16)
            with sp.Fori(0, PACKS_F1 // 2) as i:
                for k in range(2):
                    load(i * 2 + (BASE_F1 + k), k, pk_f1[bass.ds(i * 2 + k, 1), :, :].rearrange("a p n -> (a p) n"), W_F1)
            out_v = out.rearrange("(t p) d -> p t d", p=P)
            for h in range(2):
                for t in range(0, HT, 2):
                    T = HT * h + t
                    sp.wait_ge(sems["ln_done"], 4 * (10 + h) + t + 2)
                    sp.dma_start(out_v[:, T:T + 2, :], x_tok[:, T:T + 2, :]).then_inc(sems["out_done"], 16)
            sp.wait_ge(sems["out_done"], 16 * 4)

        @block.tensor
        def _(pe):
            def split_mm(o, w, x, first, last, skip=False):
                (wh, wl), (xh, xl) = w, x
                pe.matmul(o, wh, xh, start=first, stop=False, skip_group_check=skip)
                pe.matmul(o, wh, xl, start=False, stop=False, skip_group_check=skip)
                return pe.matmul(o, wl, xh, start=False, stop=last, skip_group_check=skip)

            def transposes(n):
                h = n % 2
                for t in range(HT):
                    pe.wait_ge(sems["ln_done"], 4 * n + t + 1)
                    for c in range(KC):
                        m = pe.transpose(bank[4 + 2 * h + c][:, t * P:(t + 1) * P],
                                         x_tok[:, HT * h + t, c * P:(c + 1) * P], ident)
                        if t == HT - 1:
                            m.then_inc(sems["xt_ps"], 1)

            def wait_xT(n):
                pe.wait_ge(sems["xt_hi"], KC * (n + 1))
                pe.wait_ge(sems["xt_lo"], KC * (n + 1))

            pe.wait_ge(sems["in_small"], 16 * 7)
            pe.wait_ge(sems["wa_lo_done"], 1)
            wa = lambda c, a, z: (wa_hi[:, c, a:z], wa_lo[:, c, a:z])
            for h in range(2):
                pe.wait_ge(sems["xt_lo"], h + 1)
                for c in range(KC):
                    for kc in range(KC):
                        m = split_mm(bank[2 * h + c][:, :], wa(kc, c * P, (c + 1) * P),
                                     (x_half(xT_hi, kc, h), x_half(xT_lo, kc, h)), kc == 0, kc == KC - 1)
                    m.then_inc(sems["a0_q_ps"], 1)
                for t in range(HT):
                    T = HT * h + t
                    if h:
                        pe.wait_ge(sems["a0_kv"], t + 1)
                    for kc in range(KC):
                        xh, xl = x_tile(xT_hi, kc, T), x_tile(xT_lo, kc, T)
                        wh, wl = wa(kc, D, 3 * D)
                        pe.matmul(bank[4 + t][:, :], xh, wh, start=kc == 0, stop=False)
                        pe.matmul(bank[4 + t][:, :], xh, wl, start=False, stop=False)
                        m = pe.matmul(bank[4 + t][:, :], xl, wh, start=False, stop=kc == KC - 1)
                    m.then_inc(sems["a0_kv_ps"], 1)

            def a0_state(h):
                pe.wait_ge(sems["a0_kp"], h + 1)
                pe.wait_ge(sems["a0_q"], KC * (h + 1))
                for b in range(2):
                    for c in range(KC):
                        for t in range(2):
                            T = HT * h + 2 * b + t
                            m = pe.matmul(bank[2 * h + b][:, c * 256:c * 256 + P + 1],
                                          k_tok[:, T, c * P:(c + 1) * P], v_buf[:, T, c, :],
                                          start=t == 0, stop=t == 1)
                    m.then_inc(sems["a0_st_ps"], 1)

            def a0_attend(h):
                pe.wait_ge(sems["a0_state"], 2 * (h + 1))
                for t in range(HT):
                    T = HT * h + t
                    if h:
                        pe.wait_ge(sems["a0_attn"], t + 1)
                    else:
                        pe.wait_ge(sems["a0_kv"], HT + t + 1)
                    for c in range(KC):
                        m = pe.matmul(bank[4 + t][:, c * 256:c * 256 + BLK], q_buf[:, c, T * P:(T + 1) * P],
                                      state[:, KC * (T // 2) + c, :], start=True, stop=True)
                    m.then_inc(sems["a0_at_ps"], 1)

            def a0_transpose(h):
                for t in range(HT):
                    T = HT * h + t
                    pe.wait_ge(sems["a0_attn"], T + 1)
                    for c in range(KC):
                        m = pe.transpose(bank[2 * h + c][:, t * P:(t + 1) * P], ek[:, T, c * P:(c + 1) * P], ident)
                        if t == HT - 1:
                            m.then_inc(sems["a0_aT_ps"], 1)

            def a0_project(h):
                pe.wait_ge(sems["a0_aT_lo"], KC * (h + 1))
                for t in range(HT):
                    if t % 2 == 0:
                        pe.wait_ge(sems["a0_attn"], HT + 2 * h + t // 2 + 1)
                    o = bank[4 + 2 * h + t // 2][:, (t % 2) * D:(t % 2 + 1) * D]
                    for kc in range(KC):
                        a = kc * 512 + t * P
                        ah, al = h_hi[:, h, a:a + P], h_lo[:, h, a:a + P]
                        wh, wl = wa(kc, 3 * D, 4 * D)
                        pe.matmul(o, ah, wh, start=kc == 0, stop=False)
                        pe.matmul(o, ah, wl, start=False, stop=False)
                        m = pe.matmul(o, al, wh, start=False, stop=kc == KC - 1)
                    if t % 2:
                        m.then_inc(sems["a0_o_ps"], 1)

            a0_state(0)
            a0_attend(0)
            a0_state(1)
            a0_transpose(0)
            a0_attend(1)
            a0_project(0)
            a0_transpose(1)
            a0_project(1)

            def ffn_up(kind, pbase, ubase, sbase, i, k, U):
                h = k % 2
                slot = (k // 2) % 2
                if h == 0:
                    pe.wait_ge(sems["pack_lo"], i * 2 + (pbase + k // 2 + 1))
                wh, wl = pk_hi[:, slot, :], pk_lo[:, slot, :]

                def product(o, col, width, x_c, name):
                    for kc in range(KC):
                        a = col + kc * width + x_c
                        m = split_mm(o, (wh[:, a:a + P], wl[:, a:a + P]),
                                     (x_half(xT_hi, kc, h), x_half(xT_lo, kc, h)), kc == 0, kc == KC - 1)
                    m.then_inc(sems[name], 1)

                if kind == "f1":
                    s = i * 4 + (sbase + k)
                    pe.wait_ge(sems["hid_mul"], s - 1)
                    product(bank[(3 * k) % 4][:, :], 0, P, 0, "gate_ready")
                    pe.wait_ge(sems["silu_done"], s)
                    pe.matmul(bank[(3 * k + 1) % 4][:, :], wh[0:32, 3 * D:3 * D + P],
                              cwT[:, h * 512:(h + 1) * 512], start=True, stop=True).then_inc(sems["cw_ready"], 1)
                    pe.wait_ge(sems["m1_done"], i * 4 + (M1_0 + k))
                    product(bank[(3 * k + 2) % 4][:, :], D, P, 0, "up_ready")
                    return
                for c in range(KC):
                    s = i * 8 + (sbase + 2 * k + c)
                    if not isinstance(s, int) or s >= 2:
                        pe.wait_ge(sems["hid_mul"], s - 1)
                    product(bank[2 * c][:, :], 0, D, c * P, "gate_ready")
                    if kind == "f0":
                        product(bank[2 * c + 1][:, :], KC * D, D, c * P, "up_ready")

            def ffn_down(kind, pbase, ubase, sbase, i, k):
                h = k % 2
                slot = (k // 2) % 2
                chunks = 1 if kind == "f1" else KC
                dcol = {"x0": 0, "f0": 2 * KC * D, "f1": 2 * D}[kind]
                s_last = i * (4 * chunks) + (sbase + chunks * (k + 1))
                pe.wait_ge(sems["hid_lo"], s_last)
                if kind != "f1":
                    u = i * 4 + (ubase + k)
                    if not isinstance(u, int) or u >= 2:
                        pe.wait_ge(sems["acc_done"], (u - 1) * 4)
                for t in range(HT):
                    o = bank[4 + 2 * h + t // 2][:, (t % 2) * D:(t % 2 + 1) * D]
                    for kc in range(chunks):
                        hh = h_hi[:, h, kc * 512 + t * P:kc * 512 + (t + 1) * P]
                        hl = h_lo[:, h, kc * 512 + t * P:kc * 512 + (t + 1) * P]
                        wh = pk_hi[:, slot, dcol + kc * D:dcol + (kc + 1) * D]
                        wl = pk_lo[:, slot, dcol + kc * D:dcol + (kc + 1) * D]
                        keep_open = kind == "f1"
                        pe.matmul(o, hh, wh, start=kc == 0 and not keep_open, stop=False, skip_group_check=keep_open)
                        pe.matmul(o, hh, wl, start=False, stop=False, skip_group_check=keep_open)
                        m = pe.matmul(o, hl, wh, start=False, stop=kc == chunks - 1 and not keep_open,
                                      skip_group_check=keep_open)
                    if kind != "f1" and t % 2:
                        m.then_inc(sems["out_ready"], 1)
                return m

            def ffn(kind, pbase, ubase, sbase, steps, before_second):
                args = (kind, pbase, ubase, sbase)
                ffn_up(*args, 0, 0, 0)
                before_second()

                def body(i, last):
                    for k in range(4):
                        if k < 3:
                            ffn_up(*args, i, k + 1, 0)
                        elif not last:
                            ffn_up(*args, i + 1, 0, 0)
                        m = ffn_down(*args, i, k)
                        if kind == "f1":
                            m.then_inc(sems["down_done"], 1)

                if steps > 2:
                    with pe.Fori(0, steps - 1) as i:
                        body(i, False)
                else:
                    for i in range(steps - 1):
                        body(i, False)
                body(steps - 1, True)

            def router(n, col):
                h = n % 2
                wait_xT(n)
                first = True
                for t in range(HT):
                    o = bank[4 + 2 * h][:, t * E0:(t + 1) * E0]
                    prods = [(x, w, kc) for kc in range(KC) for x in (xT_hi, xT_lo) for w in (rw_hi, rw_lo)]
                    for j, (x, w, kc) in enumerate(prods):
                        m = pe.matmul(o, x_tile(x, kc, HT * h + t), w[:, kc, col:col + E0],
                                      start=j == 0, stop=j == len(prods) - 1)
                m.then_inc(sems["rt_ps"], 1)

            pe.sem_inc(sems["down_done"], DOWN_0)
            transposes(0)
            pe.wait_ge(sems["xt_hi"], 2 + KC)
            pe.wait_ge(sems["xt_lo"], 2 + KC)

            def second_x0():
                transposes(1)
                pe.wait_ge(sems["xt_hi"], 2 + 2 * KC)
                pe.wait_ge(sems["xt_lo"], 2 + 2 * KC)

            ffn("x0", BASE_X0, 0, 0, PACKS_X0 // 2, second_x0)

            def wait_x(n):
                pe.wait_ge(sems["xt_hi"], 2 + KC * (n + 1))
                pe.wait_ge(sems["xt_lo"], 2 + KC * (n + 1))

            def route(n, col):
                h = n % 2
                for t in range(HT):
                    o = bank[4 + 2 * h][:, t * E0:(t + 1) * E0]
                    prods = [(x, w, kc) for kc in range(KC) for x in (xT_hi, xT_lo) for w in (rw_hi, rw_lo)]
                    for j, (x, w, kc) in enumerate(prods):
                        m = pe.matmul(o, x_tile(x, kc, HT * h + t), w[:, kc, col:col + E0],
                                      start=j == 0, stop=j == len(prods) - 1)
                m.then_inc(sems["rt_ps"], 1)

            transposes(2)
            wait_x(2)
            route(2, 0)

            def second_f0():
                transposes(3)
                wait_x(3)
                route(3, 0)
                pe.wait_ge(sems["rt_lg"], 2)

            ffn("f0", BASE_F0, 2 * PACKS_X0, 4 * PACKS_X0, PACKS_F0 // 2, second_f0)

            def a1_project(h):
                n = 4 + h
                transposes(n)
                wait_x(n)
                for j, name in enumerate(("a1_q_ps", "a1_k_ps")):
                    if h:
                        pe.wait_ge(sems["a1_q" if j == 0 else "a1_k"], KC)
                    for c in range(KC):
                        roll = ROLL * c
                        for kc in range(KC):
                            m = split_mm(bank[2 * j + c][:, :], wa(kc, j * D + c * P, j * D + (c + 1) * P),
                                         (x_half(xT_hi, kc, h, roll), x_half(xT_lo, kc, h, roll)),
                                         kc == 0, kc == KC - 1)
                        m.then_inc(sems[name], 1)
                for t in range(HT):
                    T = HT * h + t
                    if t >= 2:
                        pe.wait_ge(sems["a1_v"], T - 1)
                    for c in range(KC):
                        o = bank[4 + 2 * h + t % 2][:, c * D:(c + 1) * D]
                        for kc in range(KC):
                            xh, xl = x_tile(xT_hi, kc, T, ROLL * c), x_tile(xT_lo, kc, T, ROLL * c)
                            wh, wl = wa(kc, 2 * D, 3 * D)
                            pe.matmul(o, xh, wh, start=kc == 0, stop=False)
                            pe.matmul(o, xh, wl, start=False, stop=False)
                            m = pe.matmul(o, xl, wh, start=False, stop=kc == KC - 1)
                    m.then_inc(sems["a1_v_ps"], 1)

            pe.wait_ge(sems["wa_lo_done"], 2)
            for h in range(2):
                a1_project(h)

            def a1_scores(T):
                if T == 0:
                    pe.wait_ge(sems["a1_q"], 2 * KC)
                    pe.wait_ge(sems["a1_k"], 2 * KC)
                if T >= 4:
                    pe.wait_ge(sems["a1_s"], T - 3)
                pe.wait_ge(sems["a1_kx"], KC * (T + 1))
                for c in range(KC):
                    for j in range(NG):
                        g = T * P + j * GS
                        m = pe.matmul(bank[T % 4][j * GS:(j + 1) * GS, c * 256:(c + 1) * 256],
                                      q_buf[:, c, g:g + GS],
                                      kx[:, KC * (T % 2) + c, j * HC * GS:(j + 1) * HC * GS],
                                      start=True, stop=True, tile_position=(0, j * GS))
                m.then_inc(sems["a1_s_ps"], 1)

            def a1_values(T):
                pe.wait_ge(sems["a1_bd"], NG * (T + 1))
                h, t = T // HT, T % HT
                if t < 2:
                    pe.wait_ge(sems["a1_v"], HT * (h + 1))
                else:
                    pe.wait_ge(sems["a1_o"], T - 1)
                for hd in range(HEADS):
                    m = pe.matmul(bank[4 + 2 * h + t % 2][:, hd * HD:(hd + 1) * HD], p_bd[:, T % 2, hd, :],
                                  v1[:, T, hd * HD:(hd + 1) * HD], start=True, stop=True)
                m.then_inc(sems["a1_o_ps"], 1)

            for T in range(TILES + 2):
                if T < TILES:
                    a1_scores(T)
                if T >= 2:
                    a1_values(T - 2)

            def x1_scores(T):
                b = T // 2
                if T % 2 == 0:
                    pe.wait_ge(sems["pack_lo"], BASE_X1 + b + 1)
                if T >= 2:
                    pe.wait_ge(sems["x1_s"], T - 1)
                for kc in range(KC):
                    xh, xl = x_tile(xT_hi, kc, T), x_tile(xT_lo, kc, T)
                    wh, wl = pk_hi[:, b % 2, kc * D:(kc + 1) * D], pk_lo[:, b % 2, kc * D:(kc + 1) * D]
                    pe.matmul(bank[T % 2][:, 0:D], xh, wh, start=kc == 0, stop=False)
                    pe.matmul(bank[T % 2][:, 0:D], xh, wl, start=False, stop=False)
                    m = pe.matmul(bank[T % 2][:, 0:D], xl, wh, start=False, stop=kc == KC - 1)
                m.then_inc(sems["x1_s_ps"], 1)

            def x1_transpose(T):
                pe.wait_ge(sems["x1_exp"], T + 1)
                if T >= 2:
                    pe.wait_ge(sems["x1_pT_lo"], T - 1)
                for c in range(KC):
                    m = pe.transpose(bank[2 + T % 2][:, c * P:(c + 1) * P], sm[:, T % 4, c * P:(c + 1) * P], ident)
                m.then_inc(sems["x1_pT_ps"], 1)

            def x1_read(T):
                b, h, t = T // 2, T // HT, T % HT
                pe.wait_ge(sems["x1_pT_lo"], T + 1)
                if t >= 2:
                    pe.wait_ge(sems["x1_out"], T - 1)
                o = bank[4 + 2 * h + t % 2][:, 0:D]
                for kc in range(KC):
                    ph, pl = h_hi[:, T % 2, kc * P:(kc + 1) * P], h_lo[:, T % 2, kc * P:(kc + 1) * P]
                    a = KC * D + kc * D
                    wh, wl = pk_hi[:, b % 2, a:a + D], pk_lo[:, b % 2, a:a + D]
                    pe.matmul(o, ph, wh, start=kc == 0, stop=False)
                    pe.matmul(o, ph, wl, start=False, stop=False)
                    m = pe.matmul(o, pl, wh, start=False, stop=kc == KC - 1)
                m.then_inc(sems["x1_o_ps"], 1)

            for T in range(TILES + 2):
                if T % HT == 0 and T < TILES:
                    transposes(6 + T // HT)
                    wait_x(6 + T // HT)
                if T < TILES:
                    x1_scores(T)
                if 1 <= T <= TILES:
                    x1_transpose(T - 1)
                if T >= 2:
                    x1_read(T - 2)

            for h in range(2):
                transposes(8 + h)
                wait_x(8 + h)
                route(8 + h, E0)
            for h in range(2):
                pe.wait_ge(sems["rt_stack"], h + 1)
                for t in range(HT):
                    m = pe.transpose(bank[5 + 2 * h][0:32, t * P:(t + 1) * P], stack[:, HT * h + t, :], ident)
                m.then_inc(sems["cwT_ps"], 1)
            pe.wait_ge(sems["cwT_done"], 2)
            pe.wait_ge(sems["rt_lg"], 4)
            for b in range(4):
                pe.matmul(bank[4 + b][:, :], zero_r[:, 0:P], zero_r[:, :], start=True, stop=False,
                          skip_group_check=True)
            ffn("f1", BASE_F1, 2 * (PACKS_X0 + PACKS_F0), 4 * (PACKS_X0 + PACKS_F0), PACKS_F1 // 2, lambda: None)

        @block.scalar
        def _(act):
            A = nc.scalar.activation

            def pack_hi(slot, width, nth, free=None):
                act.wait_ge(raw_loaded[slot], nth * 16)
                if free:
                    act.wait_ge(sems[free[0]], free[1])
                A(pk_hi[:, slot, 0:width], pk_raw[:, slot, 0:width], ACT.Copy).then_inc(sems["pack_hi"], 1)

            def xT_high(n, wrap=False):
                h = n % 2
                for c in range(KC):
                    act.wait_ge(sems["xt_ps"], KC * n + c + 1)
                    src = bank[4 + 2 * h + c][:, :].rearrange("p (b s) -> p b s", b=2)
                    if wrap:
                        A(xT_hi[:, c, 2 * h:2 * h + 2, S:SX], src[:, :, 0:ROLL], ACT.Copy)
                    A(xT_hi[:, c, 2 * h:2 * h + 2, 0:S], src, ACT.Copy).then_inc(sems["xt_hi"], 1)

            act.wait_ge(sems["in_xT"], 16)
            for h in range(2):
                A(xT_hi[:, :, 2 * h:2 * h + 2, 0:S],
                  q_buf[:, :, h * 512:(h + 1) * 512].rearrange("p c (b s) -> p c b s", b=2), ACT.Copy
                  ).then_inc(sems["xt_hi"], 1)
            act.wait_ge(sems["in_w0"], 16)
            A(wa_hi[:, :, :], wa_raw[:, :, :], ACT.Copy).then_inc(sems["wa_hi_done"], 1)
            act.wait_ge(sems["in_small"], 16 * 7)
            A(rw_hi[:, :, :], rw_raw[:, :, :], ACT.Copy).then_inc(sems["small_ready"], 1)
            for h in range(2):
                for c in range(KC):
                    act.wait_ge(sems["a0_q_ps"], KC * h + c + 1)
                    A(eq[:, c, h * 512:(h + 1) * 512], bank[2 * h + c][:, :], ACT.Exp,
                      bias=bcol[:, c:c + 1]).then_inc(sems["a0_eq"], 1)
                act.wait_ge(sems["a0_kv"], HT * (h + 1))
                A(ek[:, HT * h:HT * (h + 1), :], k_tok[:, HT * h:HT * (h + 1), :], ACT.Exp).then_inc(sems["a0_ek"], 1)
            pack_hi(0, W_X0, 1)
            for h in range(2):
                for c in range(KC):
                    act.wait_ge(sems["a0_aT_ps"], KC * h + c + 1)
                    A(h_hi[:, h, c * 512:(c + 1) * 512], bank[2 * h + c][:, :], ACT.Copy).then_inc(sems["a0_aT_hi"], 1)

            def ffn(kind, pbase, ubase, sbase, steps, width, next_width):
                chunks = 1 if kind == "f1" else KC

                def body(i, last):
                    for k in range(4):
                        h, p = k % 2, i * 2 + (pbase + k // 2)
                        u = i * 4 + (ubase + k)
                        for c in range(chunks):
                            s = i * (4 * chunks) + (sbase + chunks * k + c)
                            r = (chunks * k + c) % 2
                            gate = bank[(3 * k) % 4] if kind == "f1" else bank[2 * c]
                            act.wait_ge(sems["gate_ready"], s + 1)
                            if not isinstance(s, int) or s >= 2:
                                act.wait_ge(sems["hid_mul"], s - 1)
                            A(sil[:, r, :], gate[:, :], ACT.Silu).then_inc(sems["silu_done"], 1)
                            act.wait_ge(sems["hid_mul"], s + 1)
                            if c == 0 and (not isinstance(u, int) or u >= 2):
                                if kind == "f1":
                                    act.wait_ge(sems["down_done"], i * 4 + (DOWN_0 + k - 1))
                                else:
                                    act.wait_ge(sems["out_ready"], (u - 1) * 2)
                            A(h_hi[:, h, c * 512:(c + 1) * 512], hraw[:, r, :], ACT.Copy).then_inc(sems["hid_hi"], 1)
                        if h == 0:
                            w = next_width if last and k == 2 else width
                            if w:
                                slot = (k // 2 + 1) % 2
                                nth = i + ((pbase + k // 2 + 1) // 2 + 1)
                                if kind == "f1":
                                    free = ("down_done", i * 4 + (DOWN_0 + k))
                                elif isinstance(p, int) and p == 0:
                                    free = None
                                else:
                                    free = ("out_ready", p * 4)
                                pack_hi(slot, w, nth, free)

                if steps > 2:
                    with act.Fori(0, steps - 1) as i:
                        body(i, False)
                else:
                    for i in range(steps - 1):
                        body(i, False)
                body(steps - 1, True)

            xT_high2 = xT_high
            xT_high(0)
            xT_high(1)
            ffn("x0", BASE_X0, 0, 0, PACKS_X0 // 2, W_X0, W_F0)
            for h in range(2):
                xT_high(2 + h)
            for h in range(2):
                t0, t1 = HT * h, HT * (h + 1)
                act.wait_ge(sems["rt_lg"], h + 1)
                A(inh[:, t0:t1, :], lg[:, t0:t1, :], ACT.Sigmoid).then_inc(sems["rt_sig"], 1)
            for h in range(2):
                t0, t1 = HT * h, HT * (h + 1)
                act.wait_ge(sems["rt_dist"], h + 1)
                A(wz[:, t0:t1, :], dist[:, t0:t1, :], ACT.Exp, scale=-10.0)
                A(fb[:, t0:t1, :], dist[:, t0:t1, :], ACT.Exp, scale=-1.0 / 0.3).then_inc(sems["rt_exp"], 1)
            ffn("f0", BASE_F0, 2 * PACKS_X0, 4 * PACKS_X0, PACKS_F0 // 2, W_F0, W_X1)

            act.wait_ge(sems["in_w1"], 16)
            act.wait_ge(sems["a0_o_ps"], 4)
            A(wa_hi[:, :, 0:3 * D], wa_raw[:, :, 0:3 * D], ACT.Copy).then_inc(sems["wa_hi_done"], 1)
            pack_hi(1, W_X1, (BASE_X1 + 1) // 2 + 1, ("out_ready", 4 * BASE_X1))
            for h in range(2):
                xT_high(4 + h, wrap=True)
                for c in range(KC):
                    act.wait_ge(sems["a1_k_ps"], KC * h + c + 1)
                    A(k_T[:, c, h * 512:(h + 1) * 512], bank[2 + c][:, :], ACT.Identity,
                      bias=bcol[:, 4 + c:5 + c]).then_inc(sems["a1_k"], 1)

            def a1_diag(T):
                act.wait_ge(sems["a1_pT"], T + 1)
                act.wait_ge(sems["bd_zero"], 1)
                if T >= 2:
                    act.wait_ge(sems["a1_o_ps"], T - 1)
                for j in range(NG):
                    q = slice(j * GS, (j + 1) * GS)
                    A(p_bd[q, T % 2, :, q], pT[q, T % 2, :].rearrange("p (h k) -> p h k", h=HEADS),
                      ACT.Copy).then_inc(sems["a1_bd"], 1)

            for T in range(TILES + 1):
                if T < TILES:
                    act.wait_ge(sems["a1_sub"], T + 1)
                    A(sm[:, T % 4, :], sm[:, T % 4, :], ACT.Exp).then_inc(sems["a1_exp"], 1)
                if T:
                    a1_diag(T - 1)

            def x1_high(T):
                act.wait_ge(sems["x1_pT_ps"], T + 1)
                if T >= 2:
                    act.wait_ge(sems["x1_o_ps"], T - 1)
                A(h_hi[:, T % 2, 0:D], bank[2 + T % 2][:, 0:D], ACT.Copy).then_inc(sems["x1_pT_hi"], 1)
                if T in (2, 4, 6):
                    p = BASE_X1 + T // 2 + 1
                    pack_hi(p % 2, W_X1 if T < 6 else W_F1, p // 2 + 1, ("x1_o_ps", T))

            for T in range(TILES + 1):
                if T % HT == 0 and T < TILES:
                    xT_high(6 + T // HT)
                if T < TILES:
                    act.wait_ge(sems["x1_max"], T + 1)
                    if T >= 4:
                        act.wait_ge(sems["x1_w"], T - 3)
                    A(sm[:, T % 4, 0:D], sm[:, T % 4, 0:D], ACT.Exp, bias=mx[:, T, 0:1],
                      accum_out=rs[:, T, 0:1]).then_inc(sems["x1_exp"], 1)
                if T:
                    x1_high(T - 1)

            for h in range(2):
                xT_high(8 + h)
            for h in range(2):
                t0 = HT * h
                act.wait_ge(sems["rt_dist"], 3 + h)
                A(fb[:, t0:t0 + HT, :], inh[:, t0:t0 + HT, :], ACT.Exp).then_inc(sems["rt_exp1"], 1)
            for h in range(2):
                act.wait_ge(sems["cwT_ps"], h + 1)
                A(cwT[:, h * 512:(h + 1) * 512], bank[5 + 2 * h][0:32, :], ACT.Copy).then_inc(sems["cwT_done"], 1)
            act.wait_ge(sems["x1_o_ps"], TILES)
            ffn("f1", BASE_F1, 2 * (PACKS_X0 + PACKS_F0), 4 * (PACKS_X0 + PACKS_F0), PACKS_F1 // 2, W_F1, 0)

        @block.gpsimd
        def _(pool):
            links = [0]

            def link(ins):
                links[0] += 1
                ins.then_inc(sems["pool_link"], 1)
                pool.wait_ge(sems["pool_link"], links[0])

            def pack_low(p, slot, width):
                pool.wait_ge(sems["pack_hi"], p + 1)
                pool.tensor_tensor(pk_lo[:, slot, 0:width], pk_raw[:, slot, 0:width],
                                   pk_hi[:, slot, 0:width].bitcast(F32), ALU.subtract).then_inc(sems["pack_lo"], 1)

            def rstd_of(n):
                h = n % 2
                pool.wait_ge(sems["ln_var"], n + 1)
                pool.tensor_tensor(rstd[:, HT * h:HT * (h + 1)], var_e[:, HT * h:HT * (h + 1)], mhalf[:, :],
                                   ALU.pow).then_inc(sems["ln_rstd"], 1)

            link(pool.memset(mhalf[:, :], -0.5))
            pool.memset(v_buf[:, :, :, P:P + 1], 1.0).then_inc(sems["ones_ready"], 1)
            pool.memset(p_bd[:, :, :, :], 0.0).then_inc(sems["bd_zero"], 1)
            pool.wait_ge(sems["wa_hi_done"], 1)
            pool.tensor_tensor(wa_lo[:, :, :], wa_raw[:, :, :], wa_hi[:, :, :].bitcast(F32),
                               ALU.subtract).then_inc(sems["wa_lo_done"], 1)
            pool.wait_ge(sems["small_ready"], 1)
            link(pool.tensor_tensor(rw_lo[:, :, :], rw_raw[:, :, :], rw_hi[:, :, :].bitcast(F32), ALU.subtract))
            pool.wait_ge(sems["in_x"], 16)
            pool.tensor_tensor(x_tok[:, :, :], x_tok[:, :, :],
                               brow[:, 2 * D:3 * D].unsqueeze(1).to_broadcast([P, TILES, D]), ALU.add
                               ).then_inc(sems["a0_xb"], 1)
            for h in range(2):
                pool.wait_ge(sems["a0_ek"], h + 1)
                pool.tensor_scalar(ek[:, HT * h:HT * (h + 1), :], ek[:, HT * h:HT * (h + 1), :], 1.0, None,
                                   ALU.min).then_inc(sems["a0_ek1"], 1)
            pack_low(0, 0, W_X0)
            for h in range(2):
                rstd_of(h)

            def ffn(kind, pbase, ubase, sbase, steps, width, next_width):
                chunks = 1 if kind == "f1" else KC

                def body(i, last):
                    for k in range(4):
                        h, p = k % 2, i * 2 + (pbase + k // 2)
                        for c in range(chunks):
                            s = i * (4 * chunks) + (sbase + chunks * k + c)
                            r = (chunks * k + c) % 2
                            pool.wait_ge(sems["hid_hi"], s + 1)
                            pool.tensor_tensor(h_lo[:, h, c * 512:(c + 1) * 512], hraw[:, r, :],
                                               h_hi[:, h, c * 512:(c + 1) * 512].bitcast(F32),
                                               ALU.subtract).then_inc(sems["hid_lo"], 1)
                        if h == 0:
                            w = next_width if last and k == 2 else width
                            if w:
                                pack_low(p + 1, (k // 2 + 1) % 2, w)

                if steps > 2:
                    with pool.Fori(0, steps - 1) as i:
                        body(i, False)
                else:
                    for i in range(steps - 1):
                        body(i, False)
                body(steps - 1, True)

            ffn("x0", BASE_X0, 0, 0, PACKS_X0 // 2, W_X0, W_F0)
            for h in range(2):
                rstd_of(2 + h)
            ffn("f0", BASE_F0, 2 * PACKS_X0, 4 * PACKS_X0, PACKS_F0 // 2, W_F0, W_X1)

            pool.wait_ge(sems["wa_hi_done"], 2)
            pool.tensor_tensor(wa_lo[:, :, 0:3 * D], wa_raw[:, :, 0:3 * D], wa_hi[:, :, 0:3 * D].bitcast(F32),
                               ALU.subtract).then_inc(sems["wa_lo_done"], 1)
            pack_low(BASE_X1 + 1, 1, W_X1)
            for h in range(2):
                rstd_of(4 + h)

            def a1_expand(T):
                h = T // HT
                pool.wait_ge(sems["a1_k"], KC * (h + 1))
                if T >= 2:
                    pool.wait_ge(sems["a1_s_ps"], T - 1)
                for c in range(KC):
                    pool.tensor_tensor(
                        kx[:, KC * (T % 2) + c, :].rearrange("p (g h k) -> p g h k", g=NG, h=HC),
                        k_T[:, c, T * P:(T + 1) * P].rearrange("p (g k) -> p g k", g=NG).unsqueeze(2)
                        .to_broadcast([P, NG, HC, GS]),
                        head8.unsqueeze(1).unsqueeze(3).to_broadcast([P, NG, HC, GS]),
                        ALU.mult).then_inc(sems["a1_kx"], 1)

            def a1_shift(T):
                pool.wait_ge(sems["a1_max"], T + 1)
                v = sm[:, T % 4, :].rearrange("p (h k) -> p h k", h=HEADS)
                pool.tensor_tensor(v, v, mx[:, T, :].unsqueeze(2).to_broadcast([P, HEADS, GS]),
                                   ALU.subtract).then_inc(sems["a1_sub"], 1)

            def a1_residual(h):
                t0, t1 = HT * h, HT * (h + 1)
                pool.wait_ge(sems["a1_o"], HT * (h + 1))
                pool.tensor_tensor(x_tok[:, t0:t1, 0:P], x_tok[:, t0:t1, 0:P], o_tok[:, t0:t1, 0:P],
                                   ALU.add).then_inc(sems["a1_res"], 1)
                pool.wait_ge(sems[f"a1_oroll{h}"], 48)
                pool.tensor_tensor(x_tok[:, t0:t1, P:D], x_tok[:, t0:t1, P:D], o_roll[:, t0:t1, :],
                                   ALU.add).then_inc(sems["a1_res"], 1)

            a1_expand(0)
            a1_expand(1)
            for T in range(TILES):
                a1_shift(T)
                if T + 2 < TILES:
                    a1_expand(T + 2)
            for h in range(2):
                a1_residual(h)
                rstd_of(6 + h)

            for T in range(TILES):
                b = T // 2
                pool.wait_ge(sems["x1_s"], T + 1)
                pool.tensor_tensor(sm[:, T % 4, 0:D], sm[:, T % 4, 0:D], fill[:, b, :], ALU.add
                                   ).then_inc(sems["x1_add"], 1)
                if T in (3, 5, 7):
                    p = BASE_X1 + T // 2 + 1
                    pack_low(p, p % 2, W_X1 if T < 7 else W_F1)
                if T == HT + 1:
                    rstd_of(8)
            rstd_of(9)
            ffn("f1", BASE_F1, 2 * (PACKS_X0 + PACKS_F0), 4 * (PACKS_X0 + PACKS_F0), PACKS_F1 // 2, W_F1, 0)
            for h in range(2):
                rstd_of(10 + h)

        @block.vector
        def _(dve):
            links = [0]

            def link(ins):
                links[0] += 1
                ins.then_inc(sems["dve_link"], 1)
                dve.wait_ge(sems["dve_link"], links[0])

            TT, TS, STT = dve.tensor_tensor, dve.tensor_scalar, dve.scalar_tensor_tensor

            def norm(n):
                h = n % 2
                t0 = HT * h
                for t in range(HT):
                    link(dve.bn_stats(stats[:, t, :], x_tok[:, t0 + t, :]))
                for t in range(HT):
                    m = dve.bn_aggr(mv[:, t0 + t, :], stats[:, t, :])
                link(m)
                TS(var_e[:, t0:t0 + HT], mv[:, t0:t0 + HT, 1], LN_EPS, None, ALU.add).then_inc(sems["ln_var"], 1)
                dve.wait_ge(sems["ln_rstd"], n + 1)
                for t in range(HT):
                    T = t0 + t
                    TS(x_tok[:, T, :], x_tok[:, T, :], mv[:, T, 0:1], rstd[:, T:T + 1],
                       ALU.subtract, ALU.mult).then_inc(sems["ln_done"], 1)

            def xT_low(n, wrap=False):
                h = n % 2
                for c in range(KC):
                    dve.wait_ge(sems["xt_hi"], 2 + KC * n + c + 1)
                    src = bank[4 + 2 * h + c][:, :].rearrange("p (b s) -> p b s", b=2)
                    hb = slice(2 * h, 2 * h + 2)
                    if wrap:
                        TT(xT_lo[:, c, hb, S:SX], src[:, :, 0:ROLL], xT_hi[:, c, hb, 0:ROLL].bitcast(F32), ALU.subtract)
                    TT(xT_lo[:, c, hb, 0:S], src, xT_hi[:, c, hb, 0:S].bitcast(F32), ALU.subtract
                       ).then_inc(sems["xt_lo"], 1)

            def top2(score, t0):
                for t in range(t0, t0 + HT):
                    m = dve.max(top[:, t, :], score[:, t, :])
                link(m)
                for t in range(t0, t0 + HT):
                    m = dve.max_index(top_i[:, t, :], top[:, t, :], score[:, t, :])
                link(m)
                link(dve.tensor_copy(top_f[:, t0:t0 + HT, :], top_i[:, t0:t0 + HT, :]))
                for t in range(t0, t0 + HT):
                    m = TS(zone[:, t, :], iota8, top_f[:, t, 0:1], None, ALU.is_equal)
                link(m)
                for t in range(t0, t0 + HT):
                    m = STT(pick[:, t, :], iota8, top_f[:, t, 1:2], zone[:, t, :], ALU.is_equal, ALU.add)
                link(m)

            def total(o, src):
                link(dve.tensor_reduce(o, src, axis=AXX, op=ALU.add))

            def per_token(v):
                return v.unsqueeze(2).to_broadcast([P, HT, E0])

            dve.sem_inc(sems["m1_done"], M1_0)
            dve.wait_ge(sems["in_xT"], 16)
            for h in range(2):
                dve.wait_ge(sems["xt_hi"], h + 1)
                TT(xT_lo[:, :, 2 * h:2 * h + 2, 0:S],
                   q_buf[:, :, h * 512:(h + 1) * 512].rearrange("p c (b s) -> p c b s", b=2),
                   xT_hi[:, :, 2 * h:2 * h + 2, 0:S].bitcast(F32), ALU.subtract).then_inc(sems["xt_lo"], 1)
            dve.wait_ge(sems["in_small"], 16 * 7)
            dve.memset(zero_r[:, :].bitcast(F32), 0.0)
            link(dve.memset(stack[:, :, :], 0.0))
            link(dve.memset(stack[:, :, 16:17], 1.0))
            link(dve.reciprocal(temp[:, 1:2], temp[:, 0:1]))
            link(dve.tensor_copy(ids_f[:, :], ids_i[:, :]))
            link(dve.tensor_copy(keep[:, :, :], mask_w[:, :].bitcast(U8).rearrange("p (b s) -> p b s", b=B)))
            link(dve.tensor_reduce(valid[:, :], keep[:, :, :], axis=AXX, op=ALU.max))
            link(TS(fill[:, :, :], keep[:, :, :], 1.0, -NEG_X, ALU.subtract, ALU.mult))
            cut = [float(VOCAB_CUT * e) for e in range(EX)]
            for e in range(EX):
                lo_ok = EX - 1 == e
                if e == 0:
                    link(TS(route0[:, :, 0], ids_f[:, :], cut[1], None, ALU.is_lt))
                elif lo_ok:
                    link(TS(route0[:, :, e], ids_f[:, :], cut[e], None, ALU.is_ge))
                else:
                    link(TS(s1[:, :], ids_f[:, :], cut[e], None, ALU.is_ge))
                    link(STT(route0[:, :, e], ids_f[:, :], cut[e + 1], s1[:, :], ALU.is_lt, ALU.mult))

            dve.wait_ge(sems["ones_ready"], 1)
            for h in range(2):
                for t in range(HT):
                    T = HT * h + t
                    dve.wait_ge(sems["a0_kv_ps"], T + 1)
                    TT(k_tok[:, T, :], bank[4 + t][:, 0:D], brow[:, 0:D], ALU.add)
                    TT(v_buf[:, T, :, 0:P], bank[4 + t][:, D:2 * D].rearrange("p (c d) -> p c d", c=KC),
                       brow[:, D:2 * D].rearrange("p (c d) -> p c d", c=KC), ALU.add).then_inc(sems["a0_kv"], 1)
                for c in range(KC):
                    q = slice(h * 512, (h + 1) * 512)
                    dve.wait_ge(sems["a0_eq"], KC * h + c + 1)
                    link(TS(q_buf[:, c, q], bank[2 * h + c][:, :], bcol[:, c:c + 1], 0.0, ALU.add, ALU.max))
                    STT(q_buf[:, c, q], eq[:, c, q], 1.0, q_buf[:, c, q], ALU.min, ALU.add).then_inc(sems["a0_q"], 1)
            for h in range(2):
                ht = slice(HT * h, HT * (h + 1))
                dve.wait_ge(sems["a0_ek1"], h + 1)
                STT(k_tok[:, ht, :].rearrange("p t d -> p (t d)"), k_tok[:, ht, :].rearrange("p t d -> p (t d)"),
                    0.0, ek[:, ht, :].rearrange("p t d -> p (t d)"), ALU.max, ALU.add).then_inc(sems["a0_kp"], 1)

            def a0_state(h):
                for b in range(2):
                    dve.wait_ge(sems["a0_st_ps"], 2 * h + b + 1)
                    for c in range(KC):
                        n = KC * (2 * h + b) + c
                        src = bank[2 * h + b]
                        TT(state[:, n, 0:P], src[:, c * 256:c * 256 + P], headmask, ALU.mult)
                        m = TS(state[:, n, P:BLK], head8, src[:, c * 256 + P:c * 256 + P + 1], None, ALU.mult)
                    m.then_inc(sems["a0_state"], 1)

            def a0_divide(h):
                for t in range(HT):
                    T = HT * h + t
                    dve.wait_ge(sems["a0_at_ps"], T + 1)
                    src = bank[4 + t][:, :].rearrange("p (c n) -> p c n", c=KC)
                    link(TS(mx[:, T, :].rearrange("p (c h) -> p c h", c=KC), src[:, :, P:BLK], 1e-6, None, ALU.add))
                    link(dve.reciprocal(rs[:, T, :], mx[:, T, :]))
                    TT(ek[:, T, :].rearrange("p (c h d) -> p c h d", c=KC, d=HD),
                       src[:, :, 0:P].rearrange("p c (h d) -> p c h d", d=HD),
                       rs[:, T, :].rearrange("p (c h) -> p c h", c=KC).unsqueeze(3).to_broadcast([P, KC, HC, HD]),
                       ALU.mult).then_inc(sems["a0_attn"], 1)

            def a0_low(h):
                for c in range(KC):
                    dve.wait_ge(sems["a0_aT_hi"], KC * h + c + 1)
                    q = slice(c * 512, (c + 1) * 512)
                    TT(h_lo[:, h, q], bank[2 * h + c][:, :], h_hi[:, h, q].bitcast(F32), ALU.subtract
                       ).then_inc(sems["a0_aT_lo"], 1)

            def a0_residual(h):
                for j in range(2):
                    dve.wait_ge(sems["a0_o_ps"], 2 * h + j + 1)
                    T = HT * h + 2 * j
                    v = x_tok[:, T:T + 2, :].rearrange("p t d -> p (t d)")
                    TT(v, bank[4 + 2 * h + j][:, :], v, ALU.add).then_inc(sems["a0_res"], 1)
                dve.wait_ge(sems["a0_res"], 2 * (h + 1))

            a0_state(0)
            a0_divide(0)
            a0_state(1)
            a0_low(0)
            a0_divide(1)
            dve.wait_ge(sems["a0_xb"], 1)
            a0_low(1)
            a0_residual(0)
            norm(0)
            a0_residual(1)
            xT_low(0)
            norm(1)
            xT_low(1)

            def ffn_mul(kind, sbase, i, k):
                chunks = 1 if kind == "f1" else KC
                for c in range(chunks):
                    s = i * (4 * chunks) + (sbase + chunks * k + c)
                    r = (chunks * k + c) % 2
                    if not isinstance(s, int) or s >= 2:
                        dve.wait_ge(sems["hid_lo"], s - 1)
                    if kind == "f1":
                        dve.wait_ge(sems["silu_done"], s + 1)
                        dve.wait_ge(sems["cw_ready"], i * 4 + (k + 1))
                        TT(sil[:, r, :], bank[(3 * k + 1) % 4][:, :], sil[:, r, :], ALU.mult).then_inc(sems["m1_done"], 1)
                        dve.wait_ge(sems["m1_done"], i * 4 + (M1_0 + k + 1))
                        dve.wait_ge(sems["up_ready"], 2 * 2 * PACKS_F0 + i * 4 + (k + 1))
                        other = bank[(3 * k + 2) % 4]
                    elif kind == "f0":
                        dve.wait_ge(sems["silu_done"], s + 1)
                        dve.wait_ge(sems["up_ready"], i * 8 + (2 * k + c + 1))
                        other = bank[2 * c + 1]
                    else:
                        dve.wait_ge(sems["silu_done"], s + 1)
                        other = bank[2 * c]
                    TT(hraw[:, r, :], other[:, :], sil[:, r, :], ALU.mult).then_inc(sems["hid_mul"], 1)

            def ffn_add(weights, ubase, i, k, expert):
                u = i * 4 + (ubase + k)
                h = k % 2
                if k >= 2 or not isinstance(i, int) or i > 0:
                    dve.wait_ge(sems["acc_done"], (u - 1) * 4)
                for t in range(HT):
                    T = HT * h + t
                    if t % 2 == 0:
                        dve.wait_ge(sems["out_ready"], u * 2 + (t // 2 + 1))
                    STT(x_tok[:, T, :], bank[4 + 2 * h + t // 2][:, (t % 2) * D:(t % 2 + 1) * D],
                        weights[:, T, expert], x_tok[:, T, :], ALU.mult, ALU.add).then_inc(sems["acc_done"], 1)

            def ffn(kind, weights, ubase, sbase, steps, norms):
                ffn_mul(kind, sbase, 0, 0)

                def body(i, last):
                    for k in range(4):
                        if k < 3:
                            ffn_mul(kind, sbase, i, k + 1)
                        elif not last:
                            ffn_mul(kind, sbase, i + 1, 0)
                        e = i * 2 + k // 2
                        ffn_add(weights, ubase, i, k, bass.ds(e, 1))
                        if last and k == 2:
                            dve.wait_ge(sems["acc_done"], 4 * (4 * i + ubase + k + 1))
                            norm(norms)
                    return None

                if steps > 2:
                    with dve.Fori(0, steps - 1) as i:
                        body(i, False)
                else:
                    for i in range(steps - 1):
                        body(i, False)
                body(steps - 1, True)
                dve.wait_ge(sems["acc_done"], 4 * (4 * steps + ubase))

            dve.wait_ge(sems["ln_done"], 8)
            ffn("x0", route0, 0, 0, PACKS_X0 // 2, 2)
            xT_low(2)
            norm(3)
            xT_low(3)

            def logits(m, scale_ap):
                h = m % 2
                dve.wait_ge(sems["rt_ps"], m + 1)
                t0 = HT * h
                src = bank[4 + 2 * h][:, 0:HT * E0].rearrange("p (t e) -> p t e", t=HT)
                if scale_ap is None:
                    dve.tensor_copy(lg[:, t0:t0 + HT, :], src).then_inc(sems["rt_lg"], 1)
                else:
                    TS(lg[:, t0:t0 + HT, :], src, scale_ap, None, ALU.mult).then_inc(sems["rt_lg"], 1)

            logits(0, temp[:, 1:2])
            logits(1, temp[:, 1:2])
            for h in range(2):
                ht = slice(HT * h, HT * (h + 1))
                dve.wait_ge(sems["rt_sig"], h + 1)
                link(TS(dist[:, ht, :], inh[:, ht, :], -1.0, float(GOLD_C), ALU.mult, ALU.add))
                link(STT(zone[:, ht, :], inh[:, ht, :], float(GOLD_C), dist[:, ht, :], ALU.subtract, ALU.max))
                dve.tensor_copy(dist[:, ht, :], zone[:, ht, :]).then_inc(sems["rt_dist"], 1)
            dve.wait_ge(sems["rt_dist"], 2)
            for h in range(2):
                t0 = HT * h
                ht = slice(t0, t0 + HT)
                link(TS(zone[:, ht, :], inh[:, ht, :], float(GOLD_LO), None, ALU.is_ge))
                link(STT(pick[:, ht, :], inh[:, ht, :], float(GOLD_HI), zone[:, ht, :], ALU.is_le, ALU.mult))
                dve.wait_ge(sems["rt_exp"], h + 1)
                link(TT(wz[:, ht, :], wz[:, ht, :], pick[:, ht, :], ALU.mult))
                total(s1[:, ht], wz[:, ht, :])
                link(TS(none_in[:, ht], s1[:, ht], 1e-8, None, ALU.is_lt))
                top2(fb, t0)
                link(TT(fb[:, ht, :], fb[:, ht, :], pick[:, ht, :], ALU.mult))
                total(s2[:, ht], fb[:, ht, :])
                link(TS(s2[:, ht], s2[:, ht], 1e-8, None, ALU.max))
                link(dve.reciprocal(s1[:, ht], s2[:, ht]))
                link(TT(fb[:, ht, :], fb[:, ht, :], per_token(s1[:, ht]), ALU.mult))
                link(TT(fb[:, ht, :], fb[:, ht, :], per_token(none_in[:, ht]), ALU.mult))
                link(TS(s2[:, ht], none_in[:, ht], -1.0, 1.0, ALU.mult, ALU.add))
                link(TT(wz[:, ht, :], wz[:, ht, :], per_token(s2[:, ht]), ALU.mult))
                link(TT(wz[:, ht, :], wz[:, ht, :], fb[:, ht, :], ALU.add))
                total(s1[:, ht], wz[:, ht, :])
                link(TS(s1[:, ht], s1[:, ht], 1e-8, None, ALU.max))
                link(dve.reciprocal(s2[:, ht], s1[:, ht]))
                link(TT(gold[:, ht, :], wz[:, ht, :], per_token(s2[:, ht]), ALU.mult))
            dve.wait_ge(sems["ln_done"], 16)
            ffn("f0", gold, 2 * PACKS_X0, 4 * PACKS_X0, PACKS_F0 // 2, 4)

            def a1_evacuate(h):
                for c in range(KC):
                    dve.wait_ge(sems["a1_q_ps"], KC * h + c + 1)
                    TS(q_buf[:, c, h * 512:(h + 1) * 512], bank[c][:, :], bcol[:, 2 + c:3 + c], None, ALU.add
                       ).then_inc(sems["a1_q"], 1)
                for t in range(HT):
                    T = HT * h + t
                    dve.wait_ge(sems["a1_v_ps"], T + 1)
                    src = bank[4 + 2 * h + t % 2]
                    TT(v1[:, T, 0:P], src[:, 0:P], brow[:, 3 * D:3 * D + P], ALU.add)
                    TT(v1[:, T, P:D], src[:, D + P:2 * D], brow[:, 3 * D + P:4 * D], ALU.add).then_inc(sems["a1_v"], 1)

            xT_low(4, wrap=True)
            norm(5)
            a1_evacuate(0)
            xT_low(5, wrap=True)
            a1_evacuate(1)

            def a1_soft(T):
                dve.wait_ge(sems["a1_s_ps"], T + 1)
                v = sm[:, T % 4, :].rearrange("p (h k) -> p h k", h=HEADS)
                STT(v, bank[T % 4][:, :].rearrange("p (h k) -> p h k", h=HEADS), HD ** -0.5,
                    causal.unsqueeze(1).to_broadcast([P, HEADS, GS]), ALU.mult, ALU.add).then_inc(sems["a1_s"], 1)
                dve.wait_ge(sems["a1_s"], T + 1)
                dve.tensor_reduce(mx[:, T, :], v, axis=AXX, op=ALU.max).then_inc(sems["a1_max"], 1)

            def a1_sum(T):
                dve.wait_ge(sems["a1_exp"], T + 1)
                v = sm[:, T % 4, :].rearrange("p (h k) -> p h k", h=HEADS)
                if T >= 2:
                    dve.wait_ge(sems["a1_bd"], NG * (T - 1))
                dve.transpose(pT[:, T % 2, :], sm[:, T % 4, :]).then_inc(sems["a1_pT"], 1)
                link(dve.tensor_reduce(mx[:, T, :], v, axis=AXX, op=ALU.add))
                link(dve.reciprocal(rs[:, T, :], mx[:, T, :]))

            def a1_out(T):
                dve.wait_ge(sems["a1_o_ps"], T + 1)
                h, t = T // HT, T % HT
                TT(o_tok[:, T, :].rearrange("p (h d) -> p h d", h=HEADS),
                   bank[4 + 2 * h + t % 2][:, 0:D].rearrange("p (h d) -> p h d", h=HEADS),
                   rs[:, T, :].unsqueeze(2).to_broadcast([P, HEADS, HD]), ALU.mult).then_inc(sems["a1_o"], 1)

            for T in range(TILES + 2):
                if T < TILES:
                    a1_soft(T)
                if 1 <= T <= TILES:
                    a1_sum(T - 1)
                if T >= 2:
                    a1_out(T - 2)
            dve.wait_ge(sems["a1_res"], 2)
            norm(6)
            xT_low(6)
            dve.wait_ge(sems["a1_res"], 4)
            norm(7)

            def x1_mask(T):
                dve.wait_ge(sems["x1_s_ps"], T + 1)
                if T >= 4:
                    dve.wait_ge(sems["x1_pT_ps"], T - 3)
                STT(sm[:, T % 4, 0:D], bank[T % 2][:, 0:D], D ** -0.5, keep[:, T // 2, :], ALU.mult, ALU.mult
                    ).then_inc(sems["x1_s"], 1)

            def x1_peak(T):
                dve.wait_ge(sems["x1_add"], T + 1)
                dve.tensor_reduce(mx[:, T, 0:1], sm[:, T % 4, 0:D], axis=AXX, op=ALU.max, negate=True
                                  ).then_inc(sems["x1_max"], 1)

            def x1_low(T):
                dve.wait_ge(sems["x1_pT_hi"], T + 1)
                TT(h_lo[:, T % 2, 0:D], bank[2 + T % 2][:, 0:D], h_hi[:, T % 2, 0:D].bitcast(F32), ALU.subtract
                   ).then_inc(sems["x1_pT_lo"], 1)
                link(dve.reciprocal(rs[:, T, 1:2], rs[:, T, 0:1]))
                TT(rs[:, T, 2:3], rs[:, T, 1:2], valid[:, T // 2:T // 2 + 1], ALU.mult).then_inc(sems["x1_w"], 1)

            def x1_add(T):
                h, t = T // HT, T % HT
                dve.wait_ge(sems["x1_o_ps"], T + 1)
                dve.wait_ge(sems["x1_w"], T + 1)
                STT(x_tok[:, T, :], bank[4 + 2 * h + t % 2][:, 0:D], rs[:, T, 2:3], x_tok[:, T, :],
                    ALU.mult, ALU.add).then_inc(sems["x1_out"], 1)

            dve.wait_ge(sems["ln_done"], 32)
            for T in range(TILES + 2):
                if T == HT:
                    xT_low(7)
                if T < TILES:
                    x1_mask(T)
                    x1_peak(T)
                if 1 <= T <= TILES:
                    x1_low(T - 1)
                if T >= 2:
                    x1_add(T - 2)
                if T == HT + 1:
                    dve.wait_ge(sems["x1_out"], HT)
                    norm(8)
            dve.wait_ge(sems["x1_out"], TILES)
            xT_low(8)
            norm(9)

            logits(2, None)
            xT_low(9)
            logits(3, None)
            for h in range(2):
                t0 = HT * h
                ht = slice(t0, t0 + HT)
                dve.wait_ge(sems["rt_lg"], 3 + h)
                link(dve.tensor_reduce(s1[:, ht], lg[:, ht, :], axis=AXX, op=ALU.max))
                TT(inh[:, ht, :], lg[:, ht, :], per_token(s1[:, ht]), ALU.subtract).then_inc(sems["rt_dist"], 1)
            for h in range(2):
                t0 = HT * h
                ht = slice(t0, t0 + HT)
                dve.wait_ge(sems["rt_exp1"], h + 1)
                total(s2[:, ht], fb[:, ht, :])
                link(dve.reciprocal(s1[:, ht], s2[:, ht]))
                link(TT(fb[:, ht, :], fb[:, ht, :], per_token(s1[:, ht]), ALU.mult))
                top2(fb, t0)
                link(TT(fb[:, ht, :], fb[:, ht, :], pick[:, ht, :], ALU.mult))
                link(dve.tensor_copy(cw_r[:, :, :], fb[:, ht, :]))
                link(dve.tensor_copy(stack[:, ht, 0:E1], cw_r[:, :, :].bitcast(F32)))
                TT(stack[:, ht, E1:2 * E1], fb[:, ht, :], cw_r[:, :, :].bitcast(F32), ALU.subtract
                   ).then_inc(sems["rt_stack"], 1)
                dve.wait_ge(sems["rt_stack"], h + 1)
            f1_base = 4 * (PACKS_X0 + PACKS_F0)
            with dve.Fori(0, PACKS_F1 // 2) as i:
                for k in range(4):
                    ffn_mul("f1", f1_base, i, k)
            for h in range(2):
                dve.wait_ge(sems["down_done"], DOWN_0 + 2 * PACKS_F1 - 1 + h)
                for j in range(2):
                    T = HT * h + 2 * j
                    v = x_tok[:, T:T + 2, :].rearrange("p t d -> p (t d)")
                    m = TT(v, bank[4 + 2 * h + j][:, :], v, ALU.add)
                    link(m)
                norm(10 + h)


def kernel(**inputs):
    import concourse.bacc as bacc
    from concourse.bass_utils import run_bass_kernel_spmd

    a = {k: np.asarray(v) for k, v in inputs.items()}
    f = np.float32

    def chunked(w):
        return np.ascontiguousarray(w.reshape(KC, P, -1).transpose(1, 0, 2))

    x = a["x"].reshape(B * S, D)
    ids = np.ascontiguousarray(a["itok_BxS_13_99985"].reshape(TILES, P).T)
    pad = a["mask_BxS2_bk0"].reshape(1, B * S).view(np.uint32)
    w0 = chunked(np.concatenate([a[f"L0_attn_{n}_w"].T for n in "qkvo"], 1))
    w1 = chunked(np.concatenate([a[f"L1_attn_W{n}"].T for n in "qkv"], 1))
    bcol = np.concatenate([a[n].reshape(KC, P).T for n in ("L0_attn_q_b", "L1_attn_bq", "L1_attn_bk")], 1)
    brow = np.concatenate([a[n] for n in ("L0_attn_k_b", "L0_attn_v_b", "L0_attn_o_b", "L1_attn_bv")]).reshape(1, -1)
    wr = chunked(np.concatenate([a["L0_ffn_Wr"], a["L1_ffn_gate_weight"].T], 1))

    p = np.arange(P)
    con = np.zeros((P, CONST_W), f)
    con[:, 0:P] = np.eye(P)
    con[:, P:2 * P] = (p[:, None] // HD == p[None, :] // HD)
    con[:, 2 * P:2 * P + HC] = (p[:, None] // HD == np.arange(HC)[None, :])
    con[:, P + BLK:P + BLK + GS] = np.where(np.arange(GS)[None, :] > p[:, None] % GS, NEG, 0.0)
    con[:, P + BLK + GS:] = np.arange(8)[None, :]

    ctx_ = a["ctx_2048"]
    pk_x0 = np.stack([chunked(ctx_[e].T).reshape(P, -1) for e in range(EX)])
    pk_x1 = np.stack([np.concatenate([chunked(ctx_[b].T).reshape(P, -1), chunked(ctx_[b]).reshape(P, -1)], 1)
                      for b in range(B)])
    pk_f0 = np.stack([np.concatenate([chunked(a[f"L0_ffn_W{n}"][e]).reshape(P, -1) for n in "gud"], 1)
                      for e in range(E0)])
    rows = (CH_R + CH_S) * P
    gate, up, down = (np.zeros((rows, D), f) for _ in range(3))
    nr = E1 * F1
    gu, dn = a["L1_ffn_gate_up_weights"], a["L1_ffn_down_weights"]
    sgu, sdn = a["L1_ffn_shared_gate_up"], a["L1_ffn_shared_down"]
    gate[0:nr] = gu[:, 0:F1].reshape(nr, D)
    up[0:nr] = gu[:, F1:].reshape(nr, D)
    down[0:nr] = dn.transpose(0, 2, 1).reshape(nr, D)
    gate[nr:nr + FS] = sgu[0:FS]
    up[nr:nr + FS] = sgu[FS:]
    down[nr:nr + FS] = sdn.T
    sel = np.zeros((rows // P, P, P), f)
    for j in range(rows // P):
        for q in range(P):
            n = j * P + q
            for r in ((n // F1, E1 + n // F1) if n < nr else (2 * E1,)):
                sel[j, r, q] = 1.0
    pk_f1 = np.stack([np.concatenate([chunked(gate[j * P:(j + 1) * P].T).reshape(P, -1),
                                      chunked(up[j * P:(j + 1) * P].T).reshape(P, -1),
                                      down[j * P:(j + 1) * P], sel[j]], 1) for j in range(rows // P)])

    arrays = {"x_rows": x, "x_cols": x.T, "ids": ids, "pad_mask": pad, "w_attn0": w0, "w_attn1": w1,
              "bias_cols": bcol, "bias_rows": brow, "w_route": wr,
              "temperature": a["L0_ffn_temperature"].reshape(1, 1), "consts": con,
              "pk_x0": pk_x0, "pk_f0": pk_f0, "pk_x1": pk_x1, "pk_f1": pk_f1}
    arrays = {k: np.ascontiguousarray(v) for k, v in arrays.items()}
    nc = bacc.Bacc("TRN2", target_bir_lowering=False, num_devices=1)
    args = [nc.dram_tensor(f"{k}_dram", v.shape, mybir.dt.from_np(v.dtype), kind="ExternalInput").ap()
            for k, v in arrays.items()]
    out = nc.dram_tensor("out_dram", (B * S, D), F32, kind="ExternalOutput").ap()
    decoder_program(nc, *args, out)
    r = run_bass_kernel_spmd(nc, [{f"{k}_dram": v for k, v in arrays.items()}], core_ids=[0])
    return r.results[0]["out_dram"].reshape(B, S, D)
```

```python
from contextlib import ExitStack

import numpy as np

import concourse.bass as bass
from concourse import mybir

F32 = mybir.dt.float32
F32R = mybir.dt.float32r
I32 = mybir.dt.int32
U32 = mybir.dt.uint32
U8 = mybir.dt.uint8
ALU = mybir.AluOpType
ACT = mybir.ActivationFunctionType
AXX = mybir.AxisListType.X

P = 128
B, S, D = 4, 256, 256
TILES = B * S // P
HT = TILES // 2
KC = D // P
HEADS, HD = 16, 16
HC = HEADS // KC
GS = 32
ROLL = GS // 2
SX = S + ROLL
NG = P // GS
E0, EX, E1, F1 = 8, 4, 8, 176
FS = 2 * F1
CH_S = -(-FS // P)
CH_R = E1 * F1 // P
U_S = 2 * CH_S
PACKS_X0, PACKS_F0, PACKS_X1, PACKS_F1 = EX, E0, B, CH_R + CH_S
W_X0, W_F0, W_X1, W_F1 = KC * D, 3 * KC * D, 2 * KC * D, 3 * D + P
BASE_X0, BASE_F0 = 0, PACKS_X0
BASE_X1 = BASE_F0 + PACKS_F0
BASE_F1 = BASE_X1 + PACKS_X1
WMAX = W_F0
VOCAB_CUT = 12500 // EX
LN_EPS = 1e-5
GOLD_C = 1.0 / np.e
GOLD_LO = 0.5 - np.log(4.0 / 3.0)
GOLD_HI = 0.5
NEG = -1e9
NEG_X = -1e30
BIG = 3e38
CW_BANKS = ((3 * (U_S - 1) + 1) % 4, (3 * (U_S - 1)) % 4)
DOWN_0, M1_0 = 2, 1
LAG_A1, LAG_PT, LAG_X1 = 2, 2, 3
BLK = P + HC
CONST_W = P + BLK + GS + 8


def decoder_program(nc, x_rows, x_cols, ids, pad_mask, w_attn0, w_attn1, bias_cols, bias_rows,
                    w_route, temperature, consts, pk_x0, pk_f0, pk_x1, pk_f1, out):
    with ExitStack() as ctx:
        def sb(name, shape, dt=F32):
            return ctx.enter_context(nc.sbuf_tensor(name, shape, dt))

        def sem(name):
            return ctx.enter_context(nc.semaphore(name))

        bank = [ctx.enter_context(nc.psum_tensor(f"bank{i}", [P, 512], F32)) for i in range(8)]

        x_tok = sb("x_tok", [P, TILES, D])
        xT_hi = sb("xT_hi", [P, KC, B, SX], F32R)
        xT_lo = sb("xT_lo", [P, KC, B, SX], F32R)
        wa_raw = sb("wa_raw", [P, KC, 4 * D])
        wa_hi = sb("wa_hi", [P, KC, 4 * D], F32R)
        wa_lo = sb("wa_lo", [P, KC, 4 * D], F32R)
        pk_raw = sb("pk_raw", [P, 2, WMAX])
        pk_hi = sb("pk_hi", [P, 2, WMAX], F32R)
        pk_lo = sb("pk_lo", [P, 2, WMAX], F32R)
        q_buf = sb("q_buf", [P, KC, TILES * P])
        kv_buf = sb("kv_buf", [P, TILES * D + TILES * KC * (P + 1)])
        k_tok = kv_buf[:, 0:TILES * D].rearrange("p (t d) -> p t d", d=D)
        v_buf = kv_buf[:, TILES * D:].rearrange("p (t c d) -> p t c d", t=TILES, c=KC)
        v1 = kv_buf[:, 0:TILES * HEADS * (HD + 1)].rearrange("p (t h d) -> p t h d", t=TILES, h=HEADS)
        k_T = sb("k_T", [P, KC, TILES * P])
        kx = sb("kx", [P, 4, 4 * D])
        ek = kx[:, 0:2, :].rearrange("p a (t d) -> p (a t) d", d=D)
        eq = kx[:, 2:4, :]
        state = sb("state", [P, B * KC, BLK])
        o_roll = state[:, :, 0:P]
        sm = sb("sm", [P, 4, 512])
        pT = sb("pT", [P, 2, 512])
        h_hi = sb("h_hi", [P, 2, 1024], F32R)
        h_lo = sb("h_lo", [P, 2, 1024], F32R)
        scratch = sb("scratch", [P, 2048])
        sil = scratch[:, 0:1024].rearrange("p (r n) -> p r n", r=2)
        hraw = scratch[:, 1024:2048].rearrange("p (r n) -> p r n", r=2)
        o_tok = scratch[:, :].rearrange("p (t d) -> p t d", t=TILES)
        cap = sb("cap", [P, B, S])
        mask_w = sb("mask_w", [P, B * S // 4], U32)
        valid = sb("valid", [P, B])
        brow = sb("brow", [P, 4 * D])
        bcol = sb("bcol", [P, 6])
        con = sb("con", [P, CONST_W])
        ident = con[:, 0:P]
        headmask = con[:, P:2 * P]
        head8 = con[:, 2 * P:2 * P + HC]
        causal = con[:, P + BLK:P + BLK + GS]
        iota8 = con[:, P + BLK + GS:P + BLK + GS + 8]
        zero_r = sb("zero_r", [P, 512], F32R)
        rw_raw = sb("rw_raw", [P, KC, 2 * E0])
        rw_hi = sb("rw_hi", [P, KC, 2 * E0], F32R)
        rw_lo = sb("rw_lo", [P, KC, 2 * E0], F32R)
        temp = sb("temp", [P, 2])
        ids_i = sb("ids_i", [P, TILES], I32)
        ids_f = sb("ids_f", [P, TILES])
        route0 = sb("route0", [P, TILES, EX])
        gold = sb("gold", [P, TILES, E0])
        stats = sb("stats", [P, HT, 6])
        mv = sb("mv", [P, TILES, 2])
        var_e = sb("var_e", [P, TILES])
        rstd = sb("rstd", [P, TILES])
        mhalf = sb("mhalf", [P, HT])
        mx = sb("mx", [P, TILES, HEADS])
        rs = sb("rs", [P, TILES, HEADS])
        lg = sb("lg", [P, TILES, E0])
        inh = sb("inh", [P, TILES, E0])
        dist = sb("dist", [P, TILES, E0])
        wz = sb("wz", [P, TILES, E0])
        fb = sb("fb", [P, TILES, E0])
        zone = sb("zone", [P, TILES, E0])
        pick = sb("pick", [P, TILES, E0])
        top = sb("top", [P, TILES, 8])
        top_i = sb("top_i", [P, TILES, 8], U32)
        top_f = sb("top_f", [P, TILES, 8])
        s1 = sb("s1", [P, TILES])
        s2 = sb("s2", [P, TILES])
        none_in = sb("none_in", [P, TILES])
        stack = sb("stack", [P, TILES, 2 * E1])
        cw_r = sb("cw_r", [P, TILES, E1], F32R)
        cwT = sb("cwT", [2 * E1, TILES * P], F32R)

        sems = {}

        names = """in_x in_xT0 in_xT1 in_w0_kv in_w0_q in_w0_o in_w1 in_small out_done
            xraw_hi wa_hi_done wa_lo_done small_ready ones_ready wa1_hi wa1_lo
            a0_q_ps a0_eq a0_q a0_kv_ps a0_kv a0_ek a0_ek1 a0_kp a0_st_ps a0_state a0_at_ps
            a0_attn a0_aT_ps a0_aT_hi a0_aT_lo a0_o_ps a0_res a0_xb
            ln_var ln_rstd ln_done xt_ps xt_hi xt_lo
            gate_ready up_ready cw_ready silu_done m1_done hid_mul hid_hi hid_lo
            out_ready acc_done down_done pack_hi pack_lo
            rt_ps rt_lg rt_sig rt_dist rt_exp rt_exp1 rt_stack cwT_ps cwT_done
            a1_q_ps a1_k_ps a1_q a1_k a1_v_ps a1_v a1_kx0 a1_kx1 a1_s_ps a1_s a1_sub a1_exp a1_pT
            a1_o_ps a1_o a1_oroll0 a1_oroll1 a1_res a1_max v_ones
            x1_s_ps x1_s x1_max x1_exp x1_pT_ps x1_pT_hi x1_pT_lo x1_o_ps x1_w x1_out
            dve_link pool_link mask_ready acc_open raw0 raw1 fin""".split()
        for n in names:
            sems[n] = sem(n)
        raw_loaded = [sems["raw0"], sems["raw1"]]

        def routed(i, k):
            return not isinstance(i, int) or 4 * i + k >= U_S

        def steps_of(eng, kind, steps, body):
            lead = {"x0": steps - 1, "f0": 1, "f1": 2}[kind]
            for i in range(lead):
                body(i, False)
            if lead < steps - 1:
                with eng.Fori(lead, steps - 1) as i:
                    body(i, False)
            body(steps - 1, True)

        def x1_pack(part, b):
            ring, late = (pk_hi, wa_hi) if part == "hi" else (pk_lo, wa_lo)
            return ring[:, b, 0:W_X1] if b < 2 else late[:, b - 2, 0:W_X1]

        def tile_cols(T):
            return T // 2, (T % 2) * P

        def x_half(buf, c, h, roll=0):
            return buf[:, c, 2 * h:2 * h + 2, roll:roll + S]

        def x_tile(buf, c, T, roll=0):
            b, o = tile_cols(T)
            return buf[:, c, b, roll + o:roll + o + P]

        block = ctx.enter_context(nc.Block())

        @block.sync
        def _(sp):
            xc = x_cols.rearrange("(c p) t -> p c t", p=P)
            sp.dma_start(q_buf[:, :, 0:512], xc[:, :, 0:512]).then_inc(sems["in_xT0"], 16)
            for name, cols in (("kv", slice(D, 3 * D)), ("q", slice(0, D))):
                sp.dma_start(wa_raw[:, :, cols], w_attn0[:, :, cols]).then_inc(sems[f"in_w0_{name}"], 16)
            sp.dma_start(q_buf[:, :, 512:1024], xc[:, :, 512:1024]).then_inc(sems["in_xT1"], 16)
            sp.dma_start(con[:, :], consts).then_inc(sems["in_small"], 16)
            sp.dma_start(bcol[:, :], bias_cols).then_inc(sems["in_small"], 16)
            sp.dma_start(brow[:, :], bias_rows.partition_broadcast(P)).then_inc(sems["in_small"], 16)
            sp.dma_start(wa_raw[:, :, 3 * D:4 * D], w_attn0[:, :, 3 * D:4 * D]).then_inc(sems["in_w0_o"], 16)
            sp.dma_start(x_tok[:, :, :], x_rows.rearrange("(t p) d -> p t d", p=P)).then_inc(sems["in_x"], 16)
            sp.dma_start(rw_raw[:, :, :], w_route).then_inc(sems["in_small"], 16)
            sp.dma_start(temp[:, 0:1], temperature.partition_broadcast(P)).then_inc(sems["in_small"], 16)
            sp.dma_start(ids_i[:, :], ids).then_inc(sems["in_small"], 16)
            sp.dma_start(mask_w[:, :], pad_mask.partition_broadcast(P)).then_inc(sems["in_small"], 16)

            def load(p, slot, src, width):
                if not (isinstance(p, int) and p < 2):
                    sp.wait_ge(sems["pack_lo"], p - 1)
                sp.dma_start(pk_raw[:, slot, 0:width], src).then_inc(raw_loaded[slot], 16)

            for p in range(PACKS_X0):
                load(p, p % 2, pk_x0[p, :, :], W_X0)
            sp.wait_ge(sems["wa_lo_done"], 3)
            sp.dma_start(wa_raw[:, :, 0:3 * D], w_attn1).then_inc(sems["in_w1"], 16)
            with sp.Fori(0, PACKS_F0 // 2) as i:
                for k in range(2):
                    load(i * 2 + (BASE_F0 + k), k, pk_f0[bass.ds(i * 2 + k, 1), :, :].rearrange("a p n -> (a p) n"), W_F0)
            for b in range(PACKS_X1):
                load(BASE_X1 + b, b % 2, pk_x1[b, :, :], W_X1)
            for h in range(2):
                sp.wait_ge(sems["a1_o"], HT * (h + 1))
                a, z = HT * h, HT * (h + 1)
                sp.dma_start(o_roll[ROLL:P, a:z, :], o_tok[0:P - ROLL, a:z, P:D]).then_inc(sems[f"a1_oroll{h}"], 16)
                sp.dma_start(o_roll[0:ROLL, a:z:2, :], o_tok[P - ROLL:P, a + 1:z:2, P:D]).then_inc(sems[f"a1_oroll{h}"], 16)
                sp.dma_start(o_roll[0:ROLL, a + 1:z:2, :], o_tok[P - ROLL:P, a:z:2, P:D]).then_inc(sems[f"a1_oroll{h}"], 16)
            with sp.Fori(0, PACKS_F1 // 2) as i:
                for k in range(2):
                    load(i * 2 + (BASE_F1 + k), k, pk_f1[bass.ds(i * 2 + k, 1), :, :].rearrange("a p n -> (a p) n"), W_F1)
            out_v = out.rearrange("(t p) d -> p t d", p=P)
            for h in range(2):
                for t in range(0, HT, 2):
                    T = HT * h + t
                    sp.wait_ge(sems["ln_done"], 4 * (10 + h) + t + 2)
                    sp.dma_start(out_v[:, T:T + 2, :], x_tok[:, T:T + 2, :]).then_inc(sems["out_done"], 16)
            sp.wait_ge(sems["out_done"], 16 * 4)

        @block.tensor
        def _(pe):
            def split_mm(o, w, x, first, last, skip=False):
                (wh, wl), (xh, xl) = w, x
                pe.matmul(o, wh, xh, start=first, stop=False, skip_group_check=skip)
                pe.matmul(o, wh, xl, start=False, stop=False, skip_group_check=skip)
                return pe.matmul(o, wl, xh, start=False, stop=last, skip_group_check=skip)

            def transposes(n):
                h = n % 2
                for t in range(HT):
                    pe.wait_ge(sems["ln_done"], 4 * n + t + 1)
                    for c in range(KC):
                        m = pe.transpose(bank[4 + 2 * h + c][:, t * P:(t + 1) * P],
                                         x_tok[:, HT * h + t, c * P:(c + 1) * P], ident)
                        if t == HT - 1:
                            m.then_inc(sems["xt_ps"], 1)

            wa = lambda c, a, z: (wa_hi[:, c, a:z], wa_lo[:, c, a:z])

            def a0_query(h):
                for c in range(KC):
                    for kc in range(KC):
                        m = split_mm(bank[2 * h + c][:, :], wa(kc, c * P, (c + 1) * P),
                                     (x_half(xT_hi, kc, h), x_half(xT_lo, kc, h)), kc == 0, kc == KC - 1)
                    m.then_inc(sems["a0_q_ps"], 1)

            def a0_keys_values(h):
                for t in range(HT):
                    T = HT * h + t
                    if h:
                        pe.wait_ge(sems["a0_kv"], t + 1)
                    for kc in range(KC):
                        xh, xl = x_tile(xT_hi, kc, T), x_tile(xT_lo, kc, T)
                        wh, wl = wa(kc, D, 3 * D)
                        pe.matmul(bank[4 + t][:, :], xh, wh, start=kc == 0, stop=False)
                        pe.matmul(bank[4 + t][:, :], xl, wh, start=False, stop=False)
                        m = pe.matmul(bank[4 + t][:, :], xh, wl, start=False, stop=kc == KC - 1)
                    m.then_inc(sems["a0_kv_ps"], 1)

            def a0_state(h):
                pe.wait_ge(sems["a0_kp"], h + 1)
                pe.wait_ge(sems["a0_q"], KC * (h + 1))
                for b in range(2):
                    for c in range(KC):
                        for t in range(2):
                            T = HT * h + 2 * b + t
                            m = pe.matmul(bank[2 * h + b][:, c * 256:c * 256 + P + 1],
                                          k_tok[:, T, c * P:(c + 1) * P], v_buf[:, T, c, :],
                                          start=t == 0, stop=t == 1)
                    m.then_inc(sems["a0_st_ps"], 1)

            def a0_attend(h):
                pe.wait_ge(sems["a0_state"], 2 * (h + 1))
                for t in range(HT):
                    T = HT * h + t
                    if h:
                        pe.wait_ge(sems["a0_attn"], t + 1)
                    else:
                        pe.wait_ge(sems["a0_kv"], HT + t + 1)
                    for c in range(KC):
                        m = pe.matmul(bank[4 + t][:, c * 256:c * 256 + BLK], q_buf[:, c, T * P:(T + 1) * P],
                                      state[:, KC * (T // 2) + c, :], start=True, stop=True)
                    m.then_inc(sems["a0_at_ps"], 1)

            def a0_transpose(h):
                for t in range(HT):
                    T = HT * h + t
                    pe.wait_ge(sems["a0_attn"], T + 1)
                    for c in range(KC):
                        m = pe.transpose(bank[2 * h + c][:, t * P:(t + 1) * P], ek[:, T, c * P:(c + 1) * P], ident)
                        if t == HT - 1:
                            m.then_inc(sems["a0_aT_ps"], 1)

            def a0_project(h):
                pe.wait_ge(sems["a0_aT_lo"], KC * (h + 1))
                for t in range(HT):
                    if t % 2 == 0:
                        pe.wait_ge(sems["a0_attn"], HT + 2 * h + t // 2 + 1)
                    o = bank[4 + 2 * h + t // 2][:, (t % 2) * D:(t % 2 + 1) * D]
                    for kc in range(KC):
                        a = kc * 512 + t * P
                        ah, al = h_hi[:, h, a:a + P], h_lo[:, h, a:a + P]
                        wh, wl = wa(kc, 3 * D, 4 * D)
                        pe.matmul(o, ah, wh, start=kc == 0, stop=False)
                        pe.matmul(o, ah, wl, start=False, stop=False)
                        m = pe.matmul(o, al, wh, start=False, stop=kc == KC - 1)
                    if t % 2:
                        m.then_inc(sems["a0_o_ps"], 1)

            pe.wait_ge(sems["xt_lo"], 1)
            pe.wait_ge(sems["wa_lo_done"], 1)
            a0_keys_values(0)
            pe.wait_ge(sems["wa_lo_done"], 2)
            a0_query(0)
            pe.wait_ge(sems["xt_lo"], 2)
            a0_keys_values(1)
            a0_state(0)
            a0_query(1)
            a0_attend(0)
            a0_state(1)
            pe.wait_ge(sems["in_small"], 16 * 7)
            a0_transpose(0)
            a0_attend(1)
            pe.wait_ge(sems["wa_lo_done"], 3)
            a0_project(0)
            a0_transpose(1)
            a0_project(1)

            def ffn_up(kind, pbase, ubase, sbase, i, k):
                h = k % 2
                slot = (k // 2) % 2
                if h == 0:
                    pe.wait_ge(sems["pack_lo"], i * 2 + (pbase + k // 2 + 1))
                wh, wl = pk_hi[:, slot, :], pk_lo[:, slot, :]

                def product(o, col, width, x_c, name):
                    for kc in range(KC):
                        a = col + kc * width + x_c
                        m = split_mm(o, (wh[:, a:a + P], wl[:, a:a + P]),
                                     (x_half(xT_hi, kc, h), x_half(xT_lo, kc, h)), kc == 0, kc == KC - 1)
                    m.then_inc(sems[name], 1)

                if kind == "f1":
                    s = i * 4 + (sbase + k)
                    pe.wait_ge(sems["hid_mul"], s - 1)
                    product(bank[(3 * k) % 4][:, :], 0, P, 0, "gate_ready")
                    if routed(i, k):
                        pe.wait_ge(sems["silu_done"], s)
                        pe.matmul(bank[(3 * k + 1) % 4][:, :], wh[0:2 * E1, 3 * D:3 * D + P],
                                  cwT[:, h * 512:(h + 1) * 512], start=True, stop=True).then_inc(sems["cw_ready"], 1)
                        pe.wait_ge(sems["m1_done"], i * 4 + (k - U_S + M1_0))
                    product(bank[(3 * k + 2) % 4][:, :], D, P, 0, "up_ready")
                    return
                for c in range(KC):
                    s = i * 8 + (sbase + 2 * k + c)
                    if not isinstance(s, int) or s >= 2:
                        pe.wait_ge(sems["hid_mul"], s - 1)
                    product(bank[2 * c][:, :], 0, D, c * P, "gate_ready")
                    if kind == "f0":
                        product(bank[2 * c + 1][:, :], KC * D, D, c * P, "up_ready")

            def ffn_down(kind, pbase, ubase, sbase, i, k):
                h = k % 2
                slot = (k // 2) % 2
                chunks = 1 if kind == "f1" else KC
                dcol = {"x0": 0, "f0": 2 * KC * D, "f1": 2 * D}[kind]
                s_last = i * (4 * chunks) + (sbase + chunks * (k + 1))
                pe.wait_ge(sems["hid_lo"], s_last)
                if kind != "f1":
                    u = i * 4 + (ubase + k)
                    if not isinstance(u, int) or u >= 2:
                        pe.wait_ge(sems["acc_done"], (u - 1) * 4)
                for t in range(HT):
                    o = bank[4 + 2 * h + t // 2][:, (t % 2) * D:(t % 2 + 1) * D]
                    for kc in range(chunks):
                        hh = h_hi[:, h, kc * 512 + t * P:kc * 512 + (t + 1) * P]
                        hl = h_lo[:, h, kc * 512 + t * P:kc * 512 + (t + 1) * P]
                        wh = pk_hi[:, slot, dcol + kc * D:dcol + (kc + 1) * D]
                        wl = pk_lo[:, slot, dcol + kc * D:dcol + (kc + 1) * D]
                        keep_open = kind == "f1"
                        pe.matmul(o, hh, wh, start=kc == 0 and not keep_open, stop=False, skip_group_check=keep_open)
                        pe.matmul(o, hh, wl, start=False, stop=False, skip_group_check=keep_open)
                        m = pe.matmul(o, hl, wh, start=False, stop=kc == chunks - 1 and not keep_open,
                                      skip_group_check=keep_open)
                    if kind != "f1" and t % 2:
                        m.then_inc(sems["out_ready"], 1)
                return m

            def ffn(kind, pbase, ubase, sbase, steps, before_second, before_unit=None):
                args = (kind, pbase, ubase, sbase)
                ffn_up(*args, 0, 0)
                before_second()

                def body(i, last):
                    for k in range(4):
                        if before_unit and isinstance(i, int) and 4 * i + k + 1 == before_unit[0]:
                            before_unit[1]()
                        if k < 3:
                            ffn_up(*args, i, k + 1)
                        elif not last:
                            ffn_up(*args, i + 1, 0)
                        m = ffn_down(*args, i, k)
                        if kind == "f1":
                            m.then_inc(sems["down_done"], 1)

                steps_of(pe, kind, steps, body)

            pe.sem_inc(sems["down_done"], DOWN_0)
            transposes(0)
            pe.wait_ge(sems["xt_hi"], 2 + KC)
            pe.wait_ge(sems["xt_lo"], 2 + KC)

            def second_x0():
                transposes(1)
                pe.wait_ge(sems["xt_hi"], 2 + 2 * KC)
                pe.wait_ge(sems["xt_lo"], 2 + 2 * KC)

            ffn("x0", BASE_X0, 0, 0, PACKS_X0 // 2, second_x0)

            def wait_x(n):
                pe.wait_ge(sems["xt_hi"], 2 + KC * (n + 1))
                pe.wait_ge(sems["xt_lo"], 2 + KC * (n + 1))

            def route(n, col):
                h = n % 2
                for t in range(HT):
                    o = bank[4 + 2 * h][:, t * E0:(t + 1) * E0]
                    prods = [(x, w, kc) for kc in range(KC) for x in (xT_hi, xT_lo) for w in (rw_hi, rw_lo)]
                    for j, (x, w, kc) in enumerate(prods):
                        m = pe.matmul(o, x_tile(x, kc, HT * h + t), w[:, kc, col:col + E0],
                                      start=j == 0, stop=j == len(prods) - 1)
                m.then_inc(sems["rt_ps"], 1)

            transposes(2)
            wait_x(2)
            route(2, 0)

            def second_f0():
                transposes(3)
                wait_x(3)
                route(3, 0)
                pe.wait_ge(sems["rt_lg"], 2)

            ffn("f0", BASE_F0, 2 * PACKS_X0, 4 * PACKS_X0, PACKS_F0 // 2, second_f0)

            def a1_query_key(h, j):
                if h or j:
                    pe.wait_ge(sems["a1_q" if j else "a1_k"], KC * (h + 1) if j else KC * h)
                for c in range(KC):
                    roll = ROLL * c
                    for kc in range(KC):
                        m = split_mm(bank[2 + c][:, :], wa(kc, j * D + c * P, j * D + (c + 1) * P),
                                     (x_half(xT_hi, kc, h, roll), x_half(xT_lo, kc, h, roll)),
                                     kc == 0, kc == KC - 1)
                    m.then_inc(sems["a1_k_ps" if j else "a1_q_ps"], 1)

            def a1_value(h):
                for t in range(HT):
                    T = HT * h + t
                    if t >= 2:
                        pe.wait_ge(sems["a1_v"], T - 1)
                    for c in range(KC):
                        o = bank[4 + 2 * h + t % 2][:, c * D:(c + 1) * D]
                        for kc in range(KC):
                            xh, xl = x_tile(xT_hi, kc, T, ROLL * c), x_tile(xT_lo, kc, T, ROLL * c)
                            wh, wl = wa(kc, 2 * D, 3 * D)
                            pe.matmul(o, xh, wh, start=kc == 0, stop=False)
                            pe.matmul(o, xh, wl, start=False, stop=False)
                            m = pe.matmul(o, xl, wh, start=False, stop=kc == KC - 1)
                    m.then_inc(sems["a1_v_ps"], 1)

            def a1_scores(T):
                if T % HT == 0:
                    pe.wait_ge(sems["a1_q"], KC * (T // HT + 1))
                if T >= 2:
                    pe.wait_ge(sems["a1_s"], T - 1)
                pe.wait_ge(sems["a1_kx0"], T + 1)
                pe.wait_ge(sems["a1_kx1"], T + 1)
                for c in range(KC):
                    for j in range(NG):
                        g = T * P + j * GS
                        m = pe.matmul(bank[T % 2][j * GS:(j + 1) * GS, c * 256:(c + 1) * 256],
                                      q_buf[:, c, g:g + GS],
                                      kx[:, KC * (T % 2) + c, j * HC * GS:(j + 1) * HC * GS],
                                      start=True, stop=True, tile_position=(0, j * GS))
                m.then_inc(sems["a1_s_ps"], 1)

            def a1_values(T):
                h, t = T // HT, T % HT
                pe.wait_ge(sems["a1_pT"], T + 1)
                if T == 0:
                    pe.wait_ge(sems["v_ones"], 1)
                if t < 2:
                    pe.wait_ge(sems["a1_v"], HT * (h + 1))
                else:
                    pe.wait_ge(sems["a1_o"], T - 1)
                for hd in range(HEADS):
                    for j in range(NG):
                        rows = slice(j * GS, (j + 1) * GS)
                        m = pe.matmul(bank[4 + 2 * h + t % 2][rows, hd * (HD + 1):(hd + 1) * (HD + 1)],
                                      pT[rows, T % 2, hd * GS:(hd + 1) * GS], v1[rows, T, hd, :],
                                      start=True, stop=True, tile_position=(j * GS, j * GS))
                m.then_inc(sems["a1_o_ps"], 1)

            pe.wait_ge(sems["wa1_lo"], 1)
            transposes(4)
            wait_x(4)
            a1_query_key(0, 0)
            a1_query_key(0, 1)
            transposes(5)
            a1_value(0)
            for T in range(TILES + LAG_A1):
                if T < TILES:
                    a1_scores(T)
                if T >= LAG_A1:
                    a1_values(T - LAG_A1)
                if T == 0:
                    wait_x(5)
                    a1_query_key(1, 0)
                if T == 1:
                    a1_query_key(1, 1)
                if T == 2:
                    a1_value(1)

            def x1_scores(T):
                b = T // 2
                if T % 2 == 0:
                    pe.wait_ge(sems["pack_lo"], BASE_X1 + b + 1)
                if T >= 2:
                    pe.wait_ge(sems["x1_s"], T - 1)
                for kc in range(KC):
                    xh, xl = x_tile(xT_hi, kc, T), x_tile(xT_lo, kc, T)
                    wh, wl = (x1_pack(buf, b)[:, kc * D:(kc + 1) * D] for buf in ("hi", "lo"))
                    pe.matmul(bank[T % 2][:, 0:D], xh, wh, start=kc == 0, stop=False)
                    pe.matmul(bank[T % 2][:, 0:D], xh, wl, start=False, stop=False)
                    m = pe.matmul(bank[T % 2][:, 0:D], xl, wh, start=False, stop=kc == KC - 1)
                m.then_inc(sems["x1_s_ps"], 1)

            def x1_transpose(T):
                pe.wait_ge(sems["x1_exp"], T + 1)
                if T >= 2:
                    pe.wait_ge(sems["x1_pT_lo"], T - 1)
                for c in range(KC):
                    m = pe.transpose(bank[2 + T % 2][:, c * P:(c + 1) * P], sm[:, T % 4, c * P:(c + 1) * P], ident)
                m.then_inc(sems["x1_pT_ps"], 1)

            def x1_read(T):
                b, h, t = T // 2, T // HT, T % HT
                pe.wait_ge(sems["x1_pT_lo"], T + 1)
                if t >= 2:
                    pe.wait_ge(sems["x1_out"], T - 1)
                o = bank[4 + 2 * h + t % 2][:, 0:D]
                for kc in range(KC):
                    ph, pl = h_hi[:, T % 2, kc * P:(kc + 1) * P], h_lo[:, T % 2, kc * P:(kc + 1) * P]
                    a = KC * D + kc * D
                    wh, wl = (x1_pack(buf, b)[:, a:a + D] for buf in ("hi", "lo"))
                    pe.matmul(o, ph, wh, start=kc == 0, stop=False)
                    pe.matmul(o, ph, wl, start=False, stop=False)
                    m = pe.matmul(o, pl, wh, start=False, stop=kc == KC - 1)
                m.then_inc(sems["x1_o_ps"], 1)

            transposes(6)
            wait_x(6)
            for T in range(TILES + LAG_X1):
                if T < TILES:
                    x1_scores(T)
                if T == 1:
                    transposes(7)
                    wait_x(7)
                if LAG_PT <= T < TILES + LAG_PT:
                    x1_transpose(T - LAG_PT)
                if T >= LAG_X1:
                    x1_read(T - LAG_X1)

            def open_sums(h):
                pe.wait_ge(sems["rt_lg"], 3 + h)
                for j in range(2):
                    pe.matmul(bank[4 + 2 * h + j][:, :], zero_r[:, 0:P], zero_r[:, :], start=True, stop=False,
                              skip_group_check=True)

            def second_f1():
                transposes(9)
                wait_x(9)
                route(9, E0)
                open_sums(0)
                open_sums(1)

            def combine_rows():
                pe.wait_ge(sems["rt_stack"], 1)
                pe.wait_ge(sems["silu_done"], 4 * (PACKS_X0 + PACKS_F0) + U_S)
                for h, b in enumerate(CW_BANKS):
                    for t in range(HT):
                        m = pe.transpose(bank[b][0:2 * E1, t * P:(t + 1) * P], stack[:, HT * h + t, :], ident)
                    m.then_inc(sems["cwT_ps"], 1)
                pe.wait_ge(sems["cwT_done"], 2)

            transposes(8)
            wait_x(8)
            route(8, E0)
            ffn("f1", BASE_F1, 2 * (PACKS_X0 + PACKS_F0), 4 * (PACKS_X0 + PACKS_F0), PACKS_F1 // 2, second_f1,
                (U_S, combine_rows))

        @block.scalar
        def _(act):
            A = nc.scalar.activation

            def pack_hi(slot, width, nth, free=None, to=None):
                act.wait_ge(raw_loaded[slot], nth * 16)
                if free:
                    act.wait_ge(sems[free[0]], free[1])
                A(pk_hi[:, slot, 0:width] if to is None else to, pk_raw[:, slot, 0:width], ACT.Copy
                  ).then_inc(sems["pack_hi"], 1)

            def xT_high(n, wrap=False):
                h = n % 2
                for c in range(KC):
                    act.wait_ge(sems["xt_ps"], KC * n + c + 1)
                    src = bank[4 + 2 * h + c][:, :].rearrange("p (b s) -> p b s", b=2)
                    if wrap:
                        A(xT_hi[:, c, 2 * h:2 * h + 2, S:SX], src[:, :, 0:ROLL], ACT.Copy)
                    A(xT_hi[:, c, 2 * h:2 * h + 2, 0:S], src, ACT.Copy).then_inc(sems["xt_hi"], 1)

            def x_high(h):
                act.wait_ge(sems[f"in_xT{h}"], 16)
                A(xT_hi[:, :, 2 * h:2 * h + 2, 0:S],
                  q_buf[:, :, h * 512:(h + 1) * 512].rearrange("p c (b s) -> p c b s", b=2), ACT.Copy
                  ).then_inc(sems["xt_hi"], 1)

            def w_high(name, cols):
                act.wait_ge(sems[f"in_w0_{name}"], 16)
                A(wa_hi[:, :, cols], wa_raw[:, :, cols], ACT.Copy).then_inc(sems["wa_hi_done"], 1)

            x_high(0)
            w_high("kv", slice(D, 3 * D))
            w_high("q", slice(0, D))
            x_high(1)
            act.wait_ge(sems["in_small"], 16 * 7)
            for h in range(2):
                act.wait_ge(sems["a0_kv"], HT * (h + 1))
                A(ek[:, HT * h:HT * (h + 1), :], k_tok[:, HT * h:HT * (h + 1), :], ACT.Exp).then_inc(sems["a0_ek"], 1)
                for c in range(KC):
                    act.wait_ge(sems["a0_q_ps"], KC * h + c + 1)
                    A(eq[:, c, h * 512:(h + 1) * 512], bank[2 * h + c][:, :], ACT.Exp,
                      bias=bcol[:, c:c + 1]).then_inc(sems["a0_eq"], 1)
            w_high("o", slice(3 * D, 4 * D))
            A(rw_hi[:, :, :], rw_raw[:, :, :], ACT.Copy).then_inc(sems["small_ready"], 1)
            pack_hi(0, W_X0, 1)
            for h in range(2):
                for c in range(KC):
                    act.wait_ge(sems["a0_aT_ps"], KC * h + c + 1)
                    A(h_hi[:, h, c * 512:(c + 1) * 512], bank[2 * h + c][:, :], ACT.Copy).then_inc(sems["a0_aT_hi"], 1)

            def ffn(kind, pbase, ubase, sbase, steps, width, next_width, after_first, before_unit=None):
                chunks = 1 if kind == "f1" else KC

                def body(i, last):
                    for k in range(4):
                        if isinstance(i, int) and 4 * i + k == 1:
                            after_first()
                        if before_unit and isinstance(i, int) and 4 * i + k == before_unit[0]:
                            before_unit[1]()
                        h, p = k % 2, i * 2 + (pbase + k // 2)
                        u = i * 4 + (ubase + k)
                        for c in range(chunks):
                            s = i * (4 * chunks) + (sbase + chunks * k + c)
                            r = (chunks * k + c) % 2
                            gate = bank[(3 * k) % 4] if kind == "f1" else bank[2 * c]
                            act.wait_ge(sems["gate_ready"], s + 1)
                            if not isinstance(s, int) or s >= 2:
                                act.wait_ge(sems["hid_mul"], s - 1)
                            A(sil[:, r, :], gate[:, :], ACT.Silu).then_inc(sems["silu_done"], 1)
                            act.wait_ge(sems["hid_mul"], s + 1)
                            if c == 0 and (not isinstance(u, int) or u >= 2):
                                if kind == "f1":
                                    act.wait_ge(sems["down_done"], i * 4 + (DOWN_0 + k - 1))
                                else:
                                    act.wait_ge(sems["out_ready"], (u - 1) * 2)
                            A(h_hi[:, h, c * 512:(c + 1) * 512], hraw[:, r, :], ACT.Copy).then_inc(sems["hid_hi"], 1)
                        if h == 0:
                            w = next_width if last and k == 2 else width
                            if w:
                                slot = (k // 2 + 1) % 2
                                nth = i + ((pbase + k // 2 + 1) // 2 + 1)
                                if kind == "f1":
                                    free = ("down_done", i * 4 + (DOWN_0 + k))
                                elif isinstance(p, int) and p == 0:
                                    free = None
                                else:
                                    free = ("out_ready", p * 4)
                                pack_hi(slot, w, nth, free)

                steps_of(act, kind, steps, body)

            xT_high(0)
            ffn("x0", BASE_X0, 0, 0, PACKS_X0 // 2, W_X0, W_F0, lambda: xT_high(1))
            xT_high(2)

            def second_f0():
                xT_high(3)
                act.wait_ge(sems["rt_lg"], 2)
                A(inh[:, :, :], lg[:, :, :], ACT.Sigmoid).then_inc(sems["rt_sig"], 1)
                act.wait_ge(sems["rt_dist"], 1)
                A(wz[:, :, :], dist[:, :, :], ACT.Exp, scale=-10.0)
                A(fb[:, :, :], dist[:, :, :], ACT.Exp, scale=-1.0 / 0.3).then_inc(sems["rt_exp"], 1)
                act.wait_ge(sems["in_w1"], 16)
                act.wait_ge(sems["a0_o_ps"], 4)
                A(wa_hi[:, :, 0:3 * D], wa_raw[:, :, 0:3 * D], ACT.Copy).then_inc(sems["wa1_hi"], 1)

            ffn("f0", BASE_F0, 2 * PACKS_X0, 4 * PACKS_X0, PACKS_F0 // 2, W_F0, W_X1, second_f0)

            def a1_keys(h):
                for c in range(KC):
                    act.wait_ge(sems["a1_k_ps"], KC * h + c + 1)
                    A(k_T[:, c, h * 512:(h + 1) * 512], bank[2 + c][:, :], ACT.Identity,
                      bias=bcol[:, 4 + c:5 + c]).then_inc(sems["a1_k"], 1)
                act.wait_ge(sems["a1_k"], KC * (h + 1))

            def a1_expand(T):
                if T >= 2:
                    act.wait_ge(sems["a1_s_ps"], T - 1)
                to = kx[:, KC * (T % 2) + 1, :].rearrange("p (g h k) -> p g h k", g=NG, h=HC)
                of = k_T[:, 1, T * P:(T + 1) * P].rearrange("p (g k) -> p g k", g=NG)
                for hd in range(HC):
                    m = A(to[:, :, hd, :], of, ACT.Copy, scale=head8[:, hd:hd + 1])
                m.then_inc(sems["a1_kx1"], 1)

            xT_high(4, wrap=True)
            a1_keys(0)
            xT_high(5, wrap=True)
            a1_expand(0)
            a1_expand(1)

            for T in range(TILES):
                act.wait_ge(sems["a1_sub"], T + 1)
                A(sm[:, T % 4, :], sm[:, T % 4, :], ACT.Exp).then_inc(sems["a1_exp"], 1)
                if T == 1:
                    a1_keys(1)
                if T + 2 < TILES:
                    a1_expand(T + 2)
                if T == 0:
                    pack_hi(1, W_X1, (BASE_X1 + 1) // 2 + 1, ("out_ready", 4 * BASE_X1))
                if T >= 6:
                    b = T - 4
                    pack_hi(b % 2, W_X1, (BASE_X1 + b) // 2 + 1, ("a1_v_ps", TILES), x1_pack("hi", b))

            def x1_high(T):
                act.wait_ge(sems["x1_pT_ps"], T + 1)
                if T >= 2:
                    act.wait_ge(sems["x1_o_ps"], T - 1)
                A(h_hi[:, T % 2, 0:D], bank[2 + T % 2][:, 0:D], ACT.Copy).then_inc(sems["x1_pT_hi"], 1)
                if T == 3:
                    pack_hi(0, W_F1, BASE_F1 // 2 + 1, ("x1_o_ps", 2))

            xT_high(6)
            for T in range(TILES + LAG_PT):
                if T >= LAG_PT:
                    x1_high(T - LAG_PT)
                if T < TILES:
                    act.wait_ge(sems["x1_max"], T + 1)
                    A(sm[:, T % 4, 0:D], sm[:, T % 4, 0:D], ACT.Exp, bias=mx[:, T, 0:1],
                      accum_out=rs[:, T, 0:1]).then_inc(sems["x1_exp"], 1)
                if T == 1:
                    xT_high(7)

            xT_high(8)

            def second_f1():
                xT_high(9)
                act.wait_ge(sems["rt_dist"], 2)
                A(fb[:, :, :], inh[:, :, :], ACT.Exp).then_inc(sems["rt_exp1"], 1)

            def combine_rows():
                for h, b in enumerate(CW_BANKS):
                    act.wait_ge(sems["cwT_ps"], h + 1)
                    A(cwT[:, h * 512:(h + 1) * 512], bank[b][0:2 * E1, :], ACT.Copy).then_inc(sems["cwT_done"], 1)

            act.wait_ge(sems["x1_o_ps"], TILES)
            ffn("f1", BASE_F1, 2 * (PACKS_X0 + PACKS_F0), 4 * (PACKS_X0 + PACKS_F0), PACKS_F1 // 2, W_F1, 0,
                second_f1, (U_S, combine_rows))

        @block.gpsimd
        def _(pool):
            links = [0]

            def link(ins):
                links[0] += 1
                ins.then_inc(sems["pool_link"], 1)
                pool.wait_ge(sems["pool_link"], links[0])

            def pack_low(p, slot, width, to=None, hi=None):
                pool.wait_ge(sems["pack_hi"], p + 1)
                if to is None:
                    to, hi = pk_lo[:, slot, 0:width], pk_hi[:, slot, 0:width]
                pool.tensor_tensor(to, pk_raw[:, slot, 0:width], hi.bitcast(F32), ALU.subtract
                                   ).then_inc(sems["pack_lo"], 1)

            def rstd_of(n):
                h = n % 2
                pool.wait_ge(sems["ln_var"], n + 1)
                pool.tensor_tensor(rstd[:, HT * h:HT * (h + 1)], var_e[:, HT * h:HT * (h + 1)], mhalf[:, :],
                                   ALU.pow).then_inc(sems["ln_rstd"], 1)

            pool.memset(mhalf[:, :], -0.5)
            pool.memset(v_buf[:, :, :, P:P + 1], 1.0).then_inc(sems["ones_ready"], 1)
            pool.wait_ge(sems["ones_ready"], 1)

            def w_low(n, cols):
                pool.wait_ge(sems["wa_hi_done"], n)
                pool.tensor_tensor(wa_lo[:, :, cols], wa_raw[:, :, cols], wa_hi[:, :, cols].bitcast(F32),
                                   ALU.subtract).then_inc(sems["wa_lo_done"], 1)

            w_low(1, slice(D, 3 * D))
            w_low(2, slice(0, D))
            pool.wait_ge(sems["in_small"], 16 * 7)
            pool.wait_ge(sems["in_x"], 16)
            pool.tensor_tensor(x_tok[:, :, :], x_tok[:, :, :],
                               brow[:, 2 * D:3 * D].unsqueeze(1).to_broadcast([P, TILES, D]), ALU.add
                               ).then_inc(sems["a0_xb"], 1)
            for h in range(2):
                pool.wait_ge(sems["a0_ek"], h + 1)
                pool.tensor_scalar(ek[:, HT * h:HT * (h + 1), :], ek[:, HT * h:HT * (h + 1), :], 1.0, None,
                                   ALU.min).then_inc(sems["a0_ek1"], 1)
            w_low(3, slice(3 * D, 4 * D))
            pool.wait_ge(sems["small_ready"], 1)
            link(pool.tensor_tensor(rw_lo[:, :, :], rw_raw[:, :, :], rw_hi[:, :, :].bitcast(F32), ALU.subtract))
            pack_low(0, 0, W_X0)
            for h in range(2):
                rstd_of(h)

            def ffn(kind, pbase, ubase, sbase, steps, width, next_width):
                chunks = 1 if kind == "f1" else KC

                def body(i, last):
                    for k in range(4):
                        h, p = k % 2, i * 2 + (pbase + k // 2)
                        for c in range(chunks):
                            s = i * (4 * chunks) + (sbase + chunks * k + c)
                            r = (chunks * k + c) % 2
                            pool.wait_ge(sems["hid_hi"], s + 1)
                            pool.tensor_tensor(h_lo[:, h, c * 512:(c + 1) * 512], hraw[:, r, :],
                                               h_hi[:, h, c * 512:(c + 1) * 512].bitcast(F32),
                                               ALU.subtract).then_inc(sems["hid_lo"], 1)
                        if h == 0:
                            w = next_width if last and k == 2 else width
                            if w:
                                pack_low(p + 1, (k // 2 + 1) % 2, w)

                steps_of(pool, kind, steps, body)

            ffn("x0", BASE_X0, 0, 0, PACKS_X0 // 2, W_X0, W_F0)
            for h in range(2):
                rstd_of(2 + h)
            pool.wait_ge(sems["a0_st_ps"], B)
            pool.memset(v1[:, :, :, HD:HD + 1], 1.0).then_inc(sems["v_ones"], 1)
            pool.wait_ge(sems["wa1_hi"], 1)
            pool.tensor_tensor(wa_lo[:, :, 0:3 * D], wa_raw[:, :, 0:3 * D], wa_hi[:, :, 0:3 * D].bitcast(F32),
                               ALU.subtract).then_inc(sems["wa1_lo"], 1)
            ffn("f0", BASE_F0, 2 * PACKS_X0, 4 * PACKS_X0, PACKS_F0 // 2, W_F0, W_X1)

            for h in range(2):
                rstd_of(4 + h)

            def a1_expand(T):
                pool.wait_ge(sems["a1_k"], KC * (T // HT + 1))
                if T >= 2:
                    pool.wait_ge(sems["a1_s_ps"], T - 1)
                pool.tensor_tensor(
                    kx[:, KC * (T % 2), :].rearrange("p (g h k) -> p g h k", g=NG, h=HC),
                    k_T[:, 0, T * P:(T + 1) * P].rearrange("p (g k) -> p g k", g=NG).unsqueeze(2)
                    .to_broadcast([P, NG, HC, GS]),
                    head8.unsqueeze(1).unsqueeze(3).to_broadcast([P, NG, HC, GS]),
                    ALU.mult).then_inc(sems["a1_kx0"], 1)

            def a1_shift(T):
                pool.wait_ge(sems["a1_max"], T + 1)
                v = sm[:, T % 4, :].rearrange("p (h k) -> p h k", h=HEADS)
                pool.tensor_tensor(v, v, mx[:, T, :].unsqueeze(2).to_broadcast([P, HEADS, GS]),
                                   ALU.subtract).then_inc(sems["a1_sub"], 1)

            def a1_residual(h):
                t0, t1 = HT * h, HT * (h + 1)
                pool.wait_ge(sems["a1_o"], HT * (h + 1))
                pool.tensor_tensor(x_tok[:, t0:t1, 0:P], x_tok[:, t0:t1, 0:P], o_tok[:, t0:t1, 0:P],
                                   ALU.add).then_inc(sems["a1_res"], 1)
                pool.wait_ge(sems[f"a1_oroll{h}"], 48)
                pool.tensor_tensor(x_tok[:, t0:t1, P:D], x_tok[:, t0:t1, P:D], o_roll[:, t0:t1, :],
                                   ALU.add).then_inc(sems["a1_res"], 1)

            a1_expand(0)
            a1_expand(1)
            for T in range(TILES):
                a1_shift(T)
                if T + 2 < TILES:
                    a1_expand(T + 2)
                if T == 0:
                    pack_low(BASE_X1 + 1, 1, W_X1)
                if T >= 6:
                    b = T - 4
                    pack_low(BASE_X1 + b, b % 2, W_X1, x1_pack("lo", b), x1_pack("hi", b))
            for h in range(2):
                a1_residual(h)
                rstd_of(6 + h)

            pack_low(BASE_F1, 0, W_F1)
            rstd_of(8)
            rstd_of(9)
            ffn("f1", BASE_F1, 2 * (PACKS_X0 + PACKS_F0), 4 * (PACKS_X0 + PACKS_F0), PACKS_F1 // 2, W_F1, 0)
            for h in range(2):
                rstd_of(10 + h)

        @block.vector
        def _(dve):
            links = [0]

            def link(ins):
                links[0] += 1
                ins.then_inc(sems["dve_link"], 1)
                dve.wait_ge(sems["dve_link"], links[0])

            TT, TS, STT = dve.tensor_tensor, dve.tensor_scalar, dve.scalar_tensor_tensor

            def norm(n):
                h = n % 2
                t0 = HT * h
                for t in range(HT):
                    m = dve.bn_stats(stats[:, t, :], x_tok[:, t0 + t, :])
                link(m)
                for t in range(HT):
                    m = dve.bn_aggr(mv[:, t0 + t, :], stats[:, t, :])
                link(m)
                TS(var_e[:, t0:t0 + HT], mv[:, t0:t0 + HT, 1], LN_EPS, None, ALU.add).then_inc(sems["ln_var"], 1)
                dve.wait_ge(sems["ln_rstd"], n + 1)
                for t in range(HT):
                    T = t0 + t
                    TS(x_tok[:, T, :], x_tok[:, T, :], mv[:, T, 0:1], rstd[:, T:T + 1],
                       ALU.subtract, ALU.mult).then_inc(sems["ln_done"], 1)

            def xT_low(n, wrap=False):
                h = n % 2
                for c in range(KC):
                    dve.wait_ge(sems["xt_hi"], 2 + KC * n + c + 1)
                    src = bank[4 + 2 * h + c][:, :].rearrange("p (b s) -> p b s", b=2)
                    hb = slice(2 * h, 2 * h + 2)
                    if wrap:
                        TT(xT_lo[:, c, hb, S:SX], src[:, :, 0:ROLL], xT_hi[:, c, hb, 0:ROLL].bitcast(F32), ALU.subtract)
                    TT(xT_lo[:, c, hb, 0:S], src, xT_hi[:, c, hb, 0:S].bitcast(F32), ALU.subtract
                       ).then_inc(sems["xt_lo"], 1)

            def top2(score):
                for T in range(TILES):
                    m = dve.max(top[:, T, :], score[:, T, :])
                link(m)
                for T in range(TILES):
                    m = dve.max_index(top_i[:, T, :], top[:, T, :], score[:, T, :])
                link(m)
                link(dve.tensor_copy(top_f[:, :, :], top_i[:, :, :]))
                idx = iota8.unsqueeze(1).to_broadcast([P, TILES, 8])
                TT(zone[:, :, :], idx, top_f[:, :, 0:1].to_broadcast([P, TILES, 8]), ALU.is_equal)
                link(TT(pick[:, :, :], idx, top_f[:, :, 1:2].to_broadcast([P, TILES, 8]), ALU.is_equal))
                link(TT(pick[:, :, :], pick[:, :, :], zone[:, :, :], ALU.add))

            def total(o, src):
                link(dve.tensor_reduce(o, src, axis=AXX, op=ALU.add))

            def per_token(v):
                return v.unsqueeze(2).to_broadcast([P, TILES, E0])

            dve.sem_inc(sems["m1_done"], M1_0)
            def x_low(h):
                dve.wait_ge(sems[f"in_xT{h}"], 16)
                dve.wait_ge(sems["xt_hi"], h + 1)
                TT(xT_lo[:, :, 2 * h:2 * h + 2, 0:S],
                   q_buf[:, :, h * 512:(h + 1) * 512].rearrange("p c (b s) -> p c b s", b=2),
                   xT_hi[:, :, 2 * h:2 * h + 2, 0:S].bitcast(F32), ALU.subtract).then_inc(sems["xt_lo"], 1)

            x_low(0)
            x_low(1)
            dve.wait_ge(sems["xt_lo"], 2)
            dve.wait_ge(sems["in_small"], 16 * 7)
            dve.wait_ge(sems["ones_ready"], 1)

            for h in range(2):
                for t in range(HT):
                    T = HT * h + t
                    dve.wait_ge(sems["a0_kv_ps"], T + 1)
                    TT(k_tok[:, T, :], bank[4 + t][:, 0:D], brow[:, 0:D], ALU.add)
                    TT(v_buf[:, T, :, 0:P], bank[4 + t][:, D:2 * D].rearrange("p (c d) -> p c d", c=KC),
                       brow[:, D:2 * D].rearrange("p (c d) -> p c d", c=KC), ALU.add).then_inc(sems["a0_kv"], 1)
                if h == 0:
                    dve.memset(zero_r[:, :].bitcast(F32), 0.0)
                    dve.reciprocal(temp[:, 1:2], temp[:, 0:1])
                    dve.tensor_copy(ids_f[:, :], ids_i[:, :])
                    link(dve.tensor_copy(cap[:, :, :], mask_w[:, :].bitcast(U8).rearrange("p (b s) -> p b s", b=B)))
                    link(dve.tensor_reduce(valid[:, :], cap[:, :, :], axis=AXX, op=ALU.max))
                    link(TS(cap[:, :, :], cap[:, :, :], BIG, NEG_X, ALU.mult, ALU.add))
                    cut = [float(VOCAB_CUT * e) for e in range(EX)]
                    TS(route0[:, :, 0], ids_f[:, :], cut[1], None, ALU.is_lt)
                    for e in range(1, EX - 1):
                        link(TS(s1[:, :], ids_f[:, :], cut[e], None, ALU.is_ge))
                        link(STT(route0[:, :, e], ids_f[:, :], cut[e + 1], s1[:, :], ALU.is_lt, ALU.mult))
                    link(TS(route0[:, :, EX - 1], ids_f[:, :], cut[EX - 1], None, ALU.is_ge))
                for c in range(KC):
                    q = slice(h * 512, (h + 1) * 512)
                    dve.wait_ge(sems["a0_eq"], KC * h + c + 1)
                    link(TS(q_buf[:, c, q], bank[2 * h + c][:, :], bcol[:, c:c + 1], 0.0, ALU.add, ALU.max))
                    STT(q_buf[:, c, q], eq[:, c, q], 1.0, q_buf[:, c, q], ALU.min, ALU.add).then_inc(sems["a0_q"], 1)
                ht = slice(HT * h, HT * (h + 1))
                dve.wait_ge(sems["a0_ek1"], h + 1)
                STT(k_tok[:, ht, :].rearrange("p t d -> p (t d)"), k_tok[:, ht, :].rearrange("p t d -> p (t d)"),
                    0.0, ek[:, ht, :].rearrange("p t d -> p (t d)"), ALU.max, ALU.add).then_inc(sems["a0_kp"], 1)

            def a0_state(h):
                for b in range(2):
                    dve.wait_ge(sems["a0_st_ps"], 2 * h + b + 1)
                    for c in range(KC):
                        n = KC * (2 * h + b) + c
                        src = bank[2 * h + b]
                        TT(state[:, n, 0:P], src[:, c * 256:c * 256 + P], headmask, ALU.mult)
                        m = TS(state[:, n, P:BLK], head8, src[:, c * 256 + P:c * 256 + P + 1], None, ALU.mult)
                    m.then_inc(sems["a0_state"], 1)

            def a0_divide(h):
                for t in range(HT):
                    T = HT * h + t
                    dve.wait_ge(sems["a0_at_ps"], T + 1)
                    src = bank[4 + t][:, :].rearrange("p (c n) -> p c n", c=KC)
                    link(TS(mx[:, T, :].rearrange("p (c h) -> p c h", c=KC), src[:, :, P:BLK], 1e-6, None, ALU.add))
                    link(dve.reciprocal(rs[:, T, :], mx[:, T, :]))
                    TT(ek[:, T, :].rearrange("p (c h d) -> p c h d", c=KC, d=HD),
                       src[:, :, 0:P].rearrange("p c (h d) -> p c h d", d=HD),
                       rs[:, T, :].rearrange("p (c h) -> p c h", c=KC).unsqueeze(3).to_broadcast([P, KC, HC, HD]),
                       ALU.mult).then_inc(sems["a0_attn"], 1)

            def a0_low(h):
                for c in range(KC):
                    dve.wait_ge(sems["a0_aT_hi"], KC * h + c + 1)
                    q = slice(c * 512, (c + 1) * 512)
                    TT(h_lo[:, h, q], bank[2 * h + c][:, :], h_hi[:, h, q].bitcast(F32), ALU.subtract
                       ).then_inc(sems["a0_aT_lo"], 1)

            def a0_residual(h):
                for j in range(2):
                    dve.wait_ge(sems["a0_o_ps"], 2 * h + j + 1)
                    T = HT * h + 2 * j
                    v = x_tok[:, T:T + 2, :].rearrange("p t d -> p (t d)")
                    TT(v, bank[4 + 2 * h + j][:, :], v, ALU.add).then_inc(sems["a0_res"], 1)
                dve.wait_ge(sems["a0_res"], 2 * (h + 1))

            a0_state(0)
            a0_divide(0)
            a0_state(1)
            a0_low(0)
            a0_divide(1)
            dve.wait_ge(sems["a0_xb"], 1)
            a0_low(1)
            a0_residual(0)
            norm(0)
            a0_residual(1)
            xT_low(0)
            norm(1)

            def ffn_mul(kind, sbase, i, k):
                chunks = 1 if kind == "f1" else KC
                for c in range(chunks):
                    s = i * (4 * chunks) + (sbase + chunks * k + c)
                    r = (chunks * k + c) % 2
                    if not isinstance(s, int) or s >= 2:
                        dve.wait_ge(sems["hid_lo"], s - 1)
                    if kind == "f1":
                        dve.wait_ge(sems["silu_done"], s + 1)
                        if routed(i, k):
                            dve.wait_ge(sems["cw_ready"], i * 4 + (k + 1 - U_S))
                            TT(sil[:, r, :], bank[(3 * k + 1) % 4][:, :], sil[:, r, :], ALU.mult
                               ).then_inc(sems["m1_done"], 1)
                            dve.wait_ge(sems["m1_done"], i * 4 + (k + 1 - U_S + M1_0))
                        dve.wait_ge(sems["up_ready"], 2 * 2 * PACKS_F0 + i * 4 + (k + 1))
                        other = bank[(3 * k + 2) % 4]
                    elif kind == "f0":
                        dve.wait_ge(sems["silu_done"], s + 1)
                        dve.wait_ge(sems["up_ready"], i * 8 + (2 * k + c + 1))
                        other = bank[2 * c + 1]
                    else:
                        dve.wait_ge(sems["silu_done"], s + 1)
                        other = bank[2 * c]
                    TT(hraw[:, r, :], other[:, :], sil[:, r, :], ALU.mult).then_inc(sems["hid_mul"], 1)

            def ffn_add(weights, ubase, i, k, expert):
                u = i * 4 + (ubase + k)
                h = k % 2
                if k >= 2 or not isinstance(i, int) or i > 0:
                    dve.wait_ge(sems["acc_done"], (u - 1) * 4)
                for t in range(HT):
                    T = HT * h + t
                    if t % 2 == 0:
                        dve.wait_ge(sems["out_ready"], u * 2 + (t // 2 + 1))
                    STT(x_tok[:, T, :], bank[4 + 2 * h + t // 2][:, (t % 2) * D:(t % 2 + 1) * D],
                        weights[:, T, expert], x_tok[:, T, :], ALU.mult, ALU.add).then_inc(sems["acc_done"], 1)

            def ffn(kind, weights, ubase, sbase, steps, norms, before_second, before_add=None):
                ffn_mul(kind, sbase, 0, 0)
                before_second()

                def body(i, last):
                    for k in range(4):
                        if k < 3:
                            ffn_mul(kind, sbase, i, k + 1)
                        elif not last:
                            ffn_mul(kind, sbase, i + 1, 0)
                        if before_add and isinstance(i, int) and 4 * i + k == 0:
                            before_add()
                        e = i * 2 + k // 2
                        ffn_add(weights, ubase, i, k, bass.ds(e, 1))
                        if last and k == 2:
                            dve.wait_ge(sems["acc_done"], 4 * (4 * i + ubase + k + 1))
                            norm(norms)
                steps_of(dve, kind, steps, body)
                dve.wait_ge(sems["acc_done"], 4 * (4 * steps + ubase))

            dve.wait_ge(sems["ln_done"], 8)
            ffn("x0", route0, 0, 0, PACKS_X0 // 2, 2, lambda: xT_low(1))
            xT_low(2)
            norm(3)

            def logits(m, scale_ap):
                h = m % 2
                dve.wait_ge(sems["rt_ps"], m + 1)
                t0 = HT * h
                src = bank[4 + 2 * h][:, 0:HT * E0].rearrange("p (t e) -> p t e", t=HT)
                if scale_ap is None:
                    dve.tensor_copy(lg[:, t0:t0 + HT, :], src).then_inc(sems["rt_lg"], 1)
                else:
                    TS(lg[:, t0:t0 + HT, :], src, scale_ap, None, ALU.mult).then_inc(sems["rt_lg"], 1)

            logits(0, temp[:, 1:2])

            def second_f0():
                xT_low(3)
                logits(1, temp[:, 1:2])
                dve.wait_ge(sems["rt_sig"], 1)
                link(TS(zone[:, :, :], inh[:, :, :], -1.0, float(GOLD_C), ALU.mult, ALU.add))
                STT(dist[:, :, :], inh[:, :, :], float(GOLD_C), zone[:, :, :], ALU.subtract, ALU.max
                    ).then_inc(sems["rt_dist"], 1)

            def gold_weights():
                dve.wait_ge(sems["rt_dist"], 1)
                link(TS(zone[:, :, :], inh[:, :, :], float(GOLD_LO), None, ALU.is_ge))
                link(STT(pick[:, :, :], inh[:, :, :], float(GOLD_HI), zone[:, :, :], ALU.is_le, ALU.mult))
                dve.wait_ge(sems["rt_exp"], 1)
                link(TT(wz[:, :, :], wz[:, :, :], pick[:, :, :], ALU.mult))
                total(s1[:, :], wz[:, :, :])
                link(TS(none_in[:, :], s1[:, :], 1e-8, None, ALU.is_lt))
                top2(fb)
                link(TT(fb[:, :, :], fb[:, :, :], pick[:, :, :], ALU.mult))
                total(s2[:, :], fb[:, :, :])
                link(TS(s2[:, :], s2[:, :], 1e-8, None, ALU.max))
                link(dve.reciprocal(s1[:, :], s2[:, :]))
                link(TT(fb[:, :, :], fb[:, :, :], per_token(s1[:, :]), ALU.mult))
                link(TT(fb[:, :, :], fb[:, :, :], per_token(none_in[:, :]), ALU.mult))
                link(TS(s2[:, :], none_in[:, :], -1.0, 1.0, ALU.mult, ALU.add))
                link(TT(wz[:, :, :], wz[:, :, :], per_token(s2[:, :]), ALU.mult))
                link(TT(wz[:, :, :], wz[:, :, :], fb[:, :, :], ALU.add))
                total(s1[:, :], wz[:, :, :])
                link(TS(s1[:, :], s1[:, :], 1e-8, None, ALU.max))
                link(dve.reciprocal(s2[:, :], s1[:, :]))
                link(TT(gold[:, :, :], wz[:, :, :], per_token(s2[:, :]), ALU.mult))
                dve.wait_ge(sems["ln_done"], 16)

            ffn("f0", gold, 2 * PACKS_X0, 4 * PACKS_X0, PACKS_F0 // 2, 4, second_f0, gold_weights)

            def a1_queries(h):
                for c in range(KC):
                    dve.wait_ge(sems["a1_q_ps"], KC * h + c + 1)
                    TS(q_buf[:, c, h * 512:(h + 1) * 512], bank[2 + c][:, :], bcol[:, 2 + c:3 + c], None, ALU.add
                       ).then_inc(sems["a1_q"], 1)

            def a1_values(h):
                for t in range(HT):
                    T = HT * h + t
                    dve.wait_ge(sems["a1_v_ps"], T + 1)
                    src = bank[4 + 2 * h + t % 2]
                    for c in range(KC):
                        m = TT(v1[:, T, c * HC:(c + 1) * HC, 0:HD],
                               src[:, c * (D + P):c * (D + P) + P].rearrange("p (h d) -> p h d", d=HD),
                               brow[:, 3 * D + c * P:3 * D + (c + 1) * P].rearrange("p (h d) -> p h d", d=HD),
                               ALU.add)
                    m.then_inc(sems["a1_v"], 1)

            xT_low(4, wrap=True)
            norm(5)
            a1_queries(0)
            xT_low(5, wrap=True)
            a1_values(0)

            def a1_soft(T):
                dve.wait_ge(sems["a1_s_ps"], T + 1)
                v = sm[:, T % 4, :].rearrange("p (h k) -> p h k", h=HEADS)
                STT(v, bank[T % 2][:, :].rearrange("p (h k) -> p h k", h=HEADS), HD ** -0.5,
                    causal.unsqueeze(1).to_broadcast([P, HEADS, GS]), ALU.mult, ALU.add).then_inc(sems["a1_s"], 1)
                dve.wait_ge(sems["a1_s"], T + 1)
                dve.tensor_reduce(mx[:, T, :], v, axis=AXX, op=ALU.max).then_inc(sems["a1_max"], 1)

            def a1_turn(T):
                dve.wait_ge(sems["a1_exp"], T + 1)
                if T >= 2:
                    dve.wait_ge(sems["a1_o_ps"], T - 1)
                dve.transpose(pT[:, T % 2, :], sm[:, T % 4, :]).then_inc(sems["a1_pT"], 1)

            def a1_out(T):
                dve.wait_ge(sems["a1_o_ps"], T + 1)
                h, t = T // HT, T % HT
                o = bank[4 + 2 * h + t % 2][:, 0:HEADS * (HD + 1)].rearrange("p (h d) -> p h d", d=HD + 1)
                link(dve.reciprocal(rs[:, T, :], o[:, :, HD]))
                TT(o_tok[:, T, :].rearrange("p (h d) -> p h d", h=HEADS), o[:, :, 0:HD],
                   rs[:, T, :].unsqueeze(2).to_broadcast([P, HEADS, HD]), ALU.mult).then_inc(sems["a1_o"], 1)

            for T in range(TILES + LAG_A1 + 1):
                if T < TILES:
                    a1_soft(T)
                if 1 <= T <= TILES:
                    a1_turn(T - 1)
                if T == 0:
                    a1_queries(1)
                if T > LAG_A1:
                    a1_out(T - LAG_A1 - 1)
                if T == 2:
                    a1_values(1)
                if T == TILES:
                    dve.wait_ge(sems["a1_res"], 2)
                    norm(6)
            xT_low(6)
            dve.wait_ge(sems["a1_res"], 4)
            norm(7)

            def x1_mask(T):
                dve.wait_ge(sems["x1_s_ps"], T + 1)
                if T >= 4:
                    dve.wait_ge(sems["x1_pT_ps"], T - 3)
                STT(sm[:, T % 4, 0:D], bank[T % 2][:, 0:D], D ** -0.5, cap[:, T // 2, :], ALU.mult, ALU.min
                    ).then_inc(sems["x1_s"], 1)
                dve.wait_ge(sems["x1_s"], T + 1)
                dve.tensor_reduce(mx[:, T, 0:1], sm[:, T % 4, 0:D], axis=AXX, op=ALU.max, negate=True
                                  ).then_inc(sems["x1_max"], 1)

            def x1_low(T):
                dve.wait_ge(sems["x1_pT_hi"], T + 1)
                TT(h_lo[:, T % 2, 0:D], bank[2 + T % 2][:, 0:D], h_hi[:, T % 2, 0:D].bitcast(F32), ALU.subtract
                   ).then_inc(sems["x1_pT_lo"], 1)
                link(dve.reciprocal(rs[:, T, 1:2], rs[:, T, 0:1]))
                TT(rs[:, T, 2:3], rs[:, T, 1:2], valid[:, T // 2:T // 2 + 1], ALU.mult).then_inc(sems["x1_w"], 1)

            def x1_add(T):
                h, t = T // HT, T % HT
                dve.wait_ge(sems["x1_o_ps"], T + 1)
                dve.wait_ge(sems["x1_w"], T + 1)
                STT(x_tok[:, T, :], bank[4 + 2 * h + t % 2][:, 0:D], rs[:, T, 2:3], x_tok[:, T, :],
                    ALU.mult, ALU.add).then_inc(sems["x1_out"], 1)

            dve.wait_ge(sems["ln_done"], 32)
            for T in range(TILES + LAG_X1):
                if T < TILES:
                    x1_mask(T)
                if T == 1:
                    xT_low(7)
                if LAG_PT <= T < TILES + LAG_PT:
                    x1_low(T - LAG_PT)
                if T >= LAG_X1:
                    x1_add(T - LAG_X1)
                if T == TILES:
                    dve.wait_ge(sems["x1_out"], HT)
                    norm(8)
            dve.wait_ge(sems["x1_out"], TILES)
            xT_low(8)
            norm(9)

            logits(2, None)
            f1_base = 4 * (PACKS_X0 + PACKS_F0)
            ffn_mul("f1", f1_base, 0, 0)
            xT_low(9)
            logits(3, None)
            dve.wait_ge(sems["rt_lg"], 4)
            link(dve.tensor_reduce(s1[:, :], lg[:, :, :], axis=AXX, op=ALU.max))
            TT(inh[:, :, :], lg[:, :, :], per_token(s1[:, :]), ALU.subtract).then_inc(sems["rt_dist"], 1)
            ffn_mul("f1", f1_base, 0, 1)
            dve.wait_ge(sems["rt_exp1"], 1)
            total(s2[:, :], fb[:, :, :])
            link(dve.reciprocal(s1[:, :], s2[:, :]))
            link(TT(fb[:, :, :], fb[:, :, :], per_token(s1[:, :]), ALU.mult))
            ffn_mul("f1", f1_base, 0, 2)
            top2(fb)
            link(TT(fb[:, :, :], fb[:, :, :], pick[:, :, :], ALU.mult))
            link(dve.tensor_copy(cw_r[:, :, :], fb[:, :, :]))
            dve.tensor_copy(stack[:, :, 0:E1], cw_r[:, :, :].bitcast(F32))
            TT(stack[:, :, E1:2 * E1], fb[:, :, :], cw_r[:, :, :].bitcast(F32), ALU.subtract
               ).then_inc(sems["rt_stack"], 1)
            ffn_mul("f1", f1_base, 0, 3)
            for k in range(4):
                ffn_mul("f1", f1_base, 1, k)
            with dve.Fori(2, PACKS_F1 // 2) as i:
                for k in range(4):
                    ffn_mul("f1", f1_base, i, k)
            for h in range(2):
                dve.wait_ge(sems["down_done"], DOWN_0 + 2 * PACKS_F1 - 1 + h)
                for j in range(2):
                    T = HT * h + 2 * j
                    v = x_tok[:, T:T + 2, :].rearrange("p t d -> p (t d)")
                    m = TT(v, bank[4 + 2 * h + j][:, :], v, ALU.add)
                link(m)
                norm(10 + h)


def kernel(**inputs):
    import concourse.bacc as bacc
    from concourse.bass_utils import run_bass_kernel_spmd

    a = {k: np.asarray(v) for k, v in inputs.items()}
    f = np.float32

    def chunked(w):
        return np.ascontiguousarray(w.reshape(KC, P, -1).transpose(1, 0, 2))

    x = a["x"].reshape(B * S, D)
    ids = np.ascontiguousarray(a["itok_BxS_13_99985"].reshape(TILES, P).T)
    pad = a["mask_BxS2_bk0"].reshape(1, B * S).view(np.uint32)
    w0 = chunked(np.concatenate([a[f"L0_attn_{n}_w"].T for n in "qkvo"], 1))
    w1 = chunked(np.concatenate([a[f"L1_attn_W{n}"].T for n in "qkv"], 1))
    bcol = np.concatenate([a[n].reshape(KC, P).T for n in ("L0_attn_q_b", "L1_attn_bq", "L1_attn_bk")], 1)
    brow = np.concatenate([a[n] for n in ("L0_attn_k_b", "L0_attn_v_b", "L0_attn_o_b", "L1_attn_bv")]).reshape(1, -1)
    wr = chunked(np.concatenate([a["L0_ffn_Wr"], a["L1_ffn_gate_weight"].T], 1))

    p = np.arange(P)
    con = np.zeros((P, CONST_W), f)
    con[:, 0:P] = np.eye(P)
    con[:, P:2 * P] = (p[:, None] // HD == p[None, :] // HD)
    con[:, 2 * P:2 * P + HC] = (p[:, None] // HD == np.arange(HC)[None, :])
    con[:, P + BLK:P + BLK + GS] = np.where(np.arange(GS)[None, :] > p[:, None] % GS, NEG, 0.0)
    con[:, P + BLK + GS:P + BLK + GS + 8] = np.arange(8)[None, :]

    ctx_ = a["ctx_2048"]
    pk_x0 = np.stack([chunked(ctx_[e].T).reshape(P, -1) for e in range(EX)])
    pk_x1 = np.stack([np.concatenate([chunked(ctx_[b].T).reshape(P, -1), chunked(ctx_[b]).reshape(P, -1)], 1)
                      for b in range(B)])
    pk_f0 = np.stack([np.concatenate([chunked(a[f"L0_ffn_W{n}"][e]).reshape(P, -1) for n in "gud"], 1)
                      for e in range(E0)])
    rows = (CH_R + CH_S) * P
    gate, up, down = (np.zeros((rows, D), f) for _ in range(3))
    ns, nr = CH_S * P, E1 * F1
    gu, dn = a["L1_ffn_gate_up_weights"], a["L1_ffn_down_weights"]
    sgu, sdn = a["L1_ffn_shared_gate_up"], a["L1_ffn_shared_down"]
    gate[0:FS] = sgu[0:FS]
    up[0:FS] = sgu[FS:]
    down[0:FS] = sdn.T
    gate[ns:] = gu[:, 0:F1].reshape(nr, D)
    up[ns:] = gu[:, F1:].reshape(nr, D)
    down[ns:] = dn.transpose(0, 2, 1).reshape(nr, D)
    sel = np.zeros((rows // P, P, P), f)
    for n in range(nr):
        j, q = divmod(ns + n, P)
        sel[j, n // F1, q] = sel[j, E1 + n // F1, q] = 1.0
    pk_f1 = np.stack([np.concatenate([chunked(gate[j * P:(j + 1) * P].T).reshape(P, -1),
                                      chunked(up[j * P:(j + 1) * P].T).reshape(P, -1),
                                      down[j * P:(j + 1) * P], sel[j]], 1) for j in range(rows // P)])

    arrays = {"x_rows": x, "x_cols": x.T, "ids": ids, "pad_mask": pad, "w_attn0": w0, "w_attn1": w1,
              "bias_cols": bcol, "bias_rows": brow, "w_route": wr,
              "temperature": a["L0_ffn_temperature"].reshape(1, 1), "consts": con,
              "pk_x0": pk_x0, "pk_f0": pk_f0, "pk_x1": pk_x1, "pk_f1": pk_f1}
    arrays = {k: np.ascontiguousarray(v) for k, v in arrays.items()}
    nc = bacc.Bacc("TRN2", target_bir_lowering=False, num_devices=1)
    args = [nc.dram_tensor(f"{k}_dram", v.shape, mybir.dt.from_np(v.dtype), kind="ExternalInput").ap()
            for k, v in arrays.items()]
    out = nc.dram_tensor("out_dram", (B * S, D), F32, kind="ExternalOutput").ap()
    decoder_program(nc, *args, out)
    r = run_bass_kernel_spmd(nc, [{f"{k}_dram": v for k, v in arrays.items()}], core_ids=[0])
    return r.results[0]["out_dram"].reshape(B, S, D)
```

```python
from contextlib import ExitStack

import numpy as np

import concourse.bass as bass
from concourse import mybir

F32 = mybir.dt.float32
F32R = mybir.dt.float32r
I32 = mybir.dt.int32
U32 = mybir.dt.uint32
U8 = mybir.dt.uint8
ALU = mybir.AluOpType
ACT = mybir.ActivationFunctionType
AXX = mybir.AxisListType.X

P = 128
B, S, D = 4, 256, 256
TILES = B * S // P
HT = TILES // 2
KC = D // P
HEADS, HD = 16, 16
HC = HEADS // KC
GS = 32
ROLL = GS // 2
SX = S + ROLL
NG = P // GS
E0, EX, E1, F1 = 8, 4, 8, 176
FS = 2 * F1
CH_S = -(-FS // P)
CH_R = E1 * F1 // P
U_S = 2 * CH_S
PACKS_X0, PACKS_F0, PACKS_X1, PACKS_F1 = EX, E0, B, CH_R + CH_S
W_X0, W_F0, W_X1, W_F1 = KC * D, 3 * KC * D, 2 * KC * D, 3 * D + P
BASE_X0, BASE_F0 = 0, PACKS_X0
BASE_X1 = BASE_F0 + PACKS_F0
BASE_F1 = BASE_X1 + PACKS_X1
WMAX = W_F0
VOCAB_CUT = 12500 // EX
LN_EPS = 1e-5
GOLD_C = 1.0 / np.e
GOLD_LO = 0.5 - np.log(4.0 / 3.0)
GOLD_HI = 0.5
NEG = -1e9
NEG_X = -1e30
BIG = 3e38
CW_BANKS = ((3 * (U_S - 1) + 1) % 4, (3 * (U_S - 1)) % 4)
DOWN_0, M1_0 = 2, 1
LAG_A1, LAG_PT, LAG_X1 = 2, 2, 3
BLK = P + HC
CONST_W = P + BLK + GS + 8


def decoder_program(nc, x_rows, x_cols, ids, pad_mask, w_attn0, w_attn1, bias_cols, bias_rows,
                    w_route, temperature, consts, pk_x0, pk_f0, pk_x1, pk_f1, out):
    with ExitStack() as ctx:
        def sb(name, shape, dt=F32):
            return ctx.enter_context(nc.sbuf_tensor(name, shape, dt))

        def sem(name):
            return ctx.enter_context(nc.semaphore(name))

        bank = [ctx.enter_context(nc.psum_tensor(f"bank{i}", [P, 512], F32)) for i in range(8)]

        x_tok = sb("x_tok", [P, TILES, D])
        xT_hi = sb("xT_hi", [P, KC, B, SX], F32R)
        xT_lo = sb("xT_lo", [P, KC, B, SX], F32R)
        wa_raw = sb("wa_raw", [P, KC, 4 * D])
        wa_hi = sb("wa_hi", [P, KC, 4 * D], F32R)
        wa_lo = sb("wa_lo", [P, KC, 4 * D], F32R)
        pk_raw = sb("pk_raw", [P, 2, WMAX])
        pk_hi = sb("pk_hi", [P, 2, WMAX], F32R)
        pk_lo = sb("pk_lo", [P, 2, WMAX], F32R)
        q_buf = sb("q_buf", [P, KC, TILES * P])
        kv_buf = sb("kv_buf", [P, TILES * D + TILES * KC * (P + 1)])
        k_tok = kv_buf[:, 0:TILES * D].rearrange("p (t d) -> p t d", d=D)
        v_buf = kv_buf[:, TILES * D:].rearrange("p (t c d) -> p t c d", t=TILES, c=KC)
        v1 = kv_buf[:, 0:TILES * HEADS * (HD + 1)].rearrange("p (t h d) -> p t h d", t=TILES, h=HEADS)
        k_T = sb("k_T", [P, KC, TILES * P])
        kx = sb("kx", [P, 4, 4 * D])
        ek = kx[:, 0:2, :].rearrange("p a (t d) -> p (a t) d", d=D)
        eq = kx[:, 2:4, :]
        state = sb("state", [P, B * KC, BLK])
        o_roll = state[:, :, 0:P]
        sm = sb("sm", [P, 4, 512])
        pT = sb("pT", [P, 2, 512])
        h_hi = sb("h_hi", [P, 2, 1024], F32R)
        h_lo = sb("h_lo", [P, 2, 1024], F32R)
        scratch = sb("scratch", [P, 2048])
        sil = scratch[:, 0:1024].rearrange("p (r n) -> p r n", r=2)
        hraw = scratch[:, 1024:2048].rearrange("p (r n) -> p r n", r=2)
        o_tok = scratch[:, :].rearrange("p (t d) -> p t d", t=TILES)
        cap = sb("cap", [P, B, S])
        mask_w = sb("mask_w", [P, B * S // 4], U32)
        valid = sb("valid", [P, B])
        brow = sb("brow", [P, 4 * D])
        bcol = sb("bcol", [P, 6])
        con = sb("con", [P, CONST_W])
        ident = con[:, 0:P]
        headmask = con[:, P:2 * P]
        head8 = con[:, 2 * P:2 * P + HC]
        causal = con[:, P + BLK:P + BLK + GS]
        iota8 = con[:, P + BLK + GS:P + BLK + GS + 8]
        zero_r = sb("zero_r", [P, 512], F32R)
        rw_raw = sb("rw_raw", [P, KC, 2 * E0])
        rw = sb("rw", [P, KC, 2, 2, E0], F32R)
        temp = sb("temp", [P, 2])
        ids_i = sb("ids_i", [P, TILES], I32)
        ids_f = sb("ids_f", [P, TILES])
        route0 = sb("route0", [P, TILES, EX])
        gold = sb("gold", [P, TILES, E0])
        stats = sb("stats", [P, HT, 6])
        mv = sb("mv", [P, TILES, 2])
        var_e = sb("var_e", [P, TILES])
        rstd = sb("rstd", [P, TILES])
        mhalf = sb("mhalf", [P, HT])
        mx = sb("mx", [P, TILES, HEADS])
        rs = sb("rs", [P, TILES, HEADS])
        lg = sb("lg", [P, TILES, E0])
        inh = sb("inh", [P, TILES, E0])
        dist = sb("dist", [P, TILES, E0])
        wz = sb("wz", [P, TILES, E0])
        fb = sb("fb", [P, TILES, E0])
        zone = sb("zone", [P, TILES, E0])
        pick = sb("pick", [P, TILES, E0])
        top = sb("top", [P, TILES, 8])
        top_i = sb("top_i", [P, TILES, 8], U32)
        top_f = sb("top_f", [P, TILES, 8])
        s1 = sb("s1", [P, TILES])
        s2 = sb("s2", [P, TILES])
        none_in = sb("none_in", [P, TILES])
        stack = sb("stack", [P, TILES, 2 * E1])
        cw_r = sb("cw_r", [P, TILES, E1], F32R)
        cwT = sb("cwT", [2 * E1, TILES * P], F32R)

        sems = {}

        names = """in_x in_xT0 in_xT1 in_w0_kv in_w0_q in_w0_o in_w1 in_small out_done wa_hi_done wa_lo_kv
            wa_lo_done small_ready ones_ready wa1_hi wa1_lo a0_q_ps a0_eq a0_q a0_kv_ps a0_kv a0_ek
            a0_kp a0_st_ps a0_state a0_at_ps a0_attn a0_aT_ps a0_aT_hi a0_aT_lo a0_o_ps a0_res a0_xb
            ln_var ln_rstd ln_done xt_ps xt_hi xt_lo gate_ready up_ready cw_ready silu_done m1_done
            hid_mul hid_hi hid_lo out_ready acc_done down_done pack_hi pack_lo rt_ps rt_lg rt_sig
            rt_dist rt_exp rt_exp1 rt_stack cwT_ps cwT_done a1_q_ps a1_k_ps a1_q a1_k a1_v_ps a1_v
            a1_kx0 a1_kx1 a1_s_ps a1_s a1_sub a1_exp a1_pT a1_o_ps a1_o a1_oroll0 a1_oroll1 a1_res
            a1_max v_ones x1_s_ps x1_s x1_max x1_exp x1_pT_ps x1_pT_hi x1_pT_lo x1_o_ps x1_w x1_out
            dve_link pool_link raw0 raw1""".split()
        for n in names:
            sems[n] = sem(n)
        raw_loaded = [sems["raw0"], sems["raw1"]]

        def routed(i, k):
            return not isinstance(i, int) or 4 * i + k >= U_S

        def steps_of(eng, kind, steps, body):
            lead = {"x0": steps - 1, "f0": 1, "f1": 2}[kind]
            for i in range(lead):
                body(i, False)
            if lead < steps - 1:
                with eng.Fori(lead, steps - 1) as i:
                    body(i, False)
            body(steps - 1, True)

        def a1_bank(h, j, c):
            return bank[c] if h == 0 and j else bank[2 + c]

        def x1_pack(part, b):
            ring, late = (pk_hi, wa_hi) if part == "hi" else (pk_lo, wa_lo)
            return ring[:, b, 0:W_X1] if b < 2 else late[:, b - 2, 0:W_X1]

        def tile_cols(T):
            return T // 2, (T % 2) * P

        def x_half(buf, c, h, roll=0):
            return buf[:, c, 2 * h:2 * h + 2, roll:roll + S]

        def x_tile(buf, c, T, roll=0):
            b, o = tile_cols(T)
            return buf[:, c, b, roll + o:roll + o + P]

        block = ctx.enter_context(nc.Block())

        @block.sync
        def _(sp):
            xc = x_cols.rearrange("(c p) t -> p c t", p=P)
            sp.dma_start(q_buf[:, :, 0:512], xc[:, :, 0:512]).then_inc(sems["in_xT0"], 16)
            for name, cols in (("kv", slice(D, 3 * D)), ("q", slice(0, D))):
                sp.dma_start(wa_raw[:, :, cols], w_attn0[:, :, cols]).then_inc(sems[f"in_w0_{name}"], 16)
            sp.dma_start(q_buf[:, :, 512:1024], xc[:, :, 512:1024]).then_inc(sems["in_xT1"], 16)
            sp.dma_start(con[:, :], consts).then_inc(sems["in_small"], 16)
            sp.dma_start(bcol[:, :], bias_cols).then_inc(sems["in_small"], 16)
            sp.dma_start(brow[:, :], bias_rows.partition_broadcast(P)).then_inc(sems["in_small"], 16)
            sp.dma_start(wa_raw[:, :, 3 * D:4 * D], w_attn0[:, :, 3 * D:4 * D]).then_inc(sems["in_w0_o"], 16)
            sp.dma_start(x_tok[:, :, :], x_rows.rearrange("(t p) d -> p t d", p=P)).then_inc(sems["in_x"], 16)
            sp.dma_start(rw_raw[:, :, :], w_route).then_inc(sems["in_small"], 16)
            sp.dma_start(temp[:, 0:1], temperature.partition_broadcast(P)).then_inc(sems["in_small"], 16)
            sp.dma_start(ids_i[:, :], ids).then_inc(sems["in_small"], 16)
            sp.dma_start(mask_w[:, :], pad_mask.partition_broadcast(P)).then_inc(sems["in_small"], 16)

            def load(p, slot, src, width):
                if not (isinstance(p, int) and p < 2):
                    sp.wait_ge(sems["pack_lo"], p - 1)
                sp.dma_start(pk_raw[:, slot, 0:width], src).then_inc(raw_loaded[slot], 16)

            for p in range(PACKS_X0):
                load(p, p % 2, pk_x0[p, :, :], W_X0)
            sp.wait_ge(sems["wa_lo_kv"], 1)
            sp.wait_ge(sems["wa_lo_done"], 2)
            sp.dma_start(wa_raw[:, :, 0:3 * D], w_attn1).then_inc(sems["in_w1"], 16)
            with sp.Fori(0, PACKS_F0 // 2) as i:
                for k in range(2):
                    load(i * 2 + (BASE_F0 + k), k, pk_f0[bass.ds(i * 2 + k, 1), :, :].rearrange("a p n -> (a p) n"), W_F0)
            for b in range(PACKS_X1):
                load(BASE_X1 + b, b % 2, pk_x1[b, :, :], W_X1)
            for h in range(2):
                sp.wait_ge(sems["a1_o"], HT * (h + 1))
                a, z = HT * h, HT * (h + 1)
                sp.dma_start(o_roll[ROLL:P, a:z, :], o_tok[0:P - ROLL, a:z, P:D]).then_inc(sems[f"a1_oroll{h}"], 16)
                sp.dma_start(o_roll[0:ROLL, a:z:2, :], o_tok[P - ROLL:P, a + 1:z:2, P:D]).then_inc(sems[f"a1_oroll{h}"], 16)
                sp.dma_start(o_roll[0:ROLL, a + 1:z:2, :], o_tok[P - ROLL:P, a:z:2, P:D]).then_inc(sems[f"a1_oroll{h}"], 16)
            with sp.Fori(0, PACKS_F1 // 2) as i:
                for k in range(2):
                    load(i * 2 + (BASE_F1 + k), k, pk_f1[bass.ds(i * 2 + k, 1), :, :].rearrange("a p n -> (a p) n"), W_F1)
            out_v = out.rearrange("(t p) d -> p t d", p=P)
            for h in range(2):
                for t in range(0, HT, 2):
                    T = HT * h + t
                    sp.wait_ge(sems["ln_done"], 4 * (10 + h) + t + 2)
                    sp.dma_start(out_v[:, T:T + 2, :], x_tok[:, T:T + 2, :]).then_inc(sems["out_done"], 16)
            sp.wait_ge(sems["out_done"], 16 * 4)

        @block.tensor
        def _(pe):
            def split_mm(o, w, x, first, last, skip=False):
                (wh, wl), (xh, xl) = w, x
                pe.matmul(o, wh, xh, start=first, stop=False, skip_group_check=skip)
                pe.matmul(o, wh, xl, start=False, stop=False, skip_group_check=skip)
                return pe.matmul(o, wl, xh, start=False, stop=last, skip_group_check=skip)

            def both_chunks(o, w, x, fresh=None):
                steps = [(0, kc) for kc in range(KC)] + [(1, kc) for kc in range(KC)]
                for part, kc in steps:
                    if fresh is not None:
                        pe.wait_ge(sems["xt_lo" if part else "xt_hi"], 2 + KC * fresh + kc + 1)
                    if part == 0:
                        pe.matmul(o, w(kc)[0], x(kc)[0], start=kc == 0, stop=False)
                        pe.matmul(o, w(kc)[1], x(kc)[0], start=False, stop=False)
                    else:
                        m = pe.matmul(o, w(kc)[0], x(kc)[1], start=False, stop=kc == KC - 1)
                return m

            def transposes(n):
                h = n % 2
                for t in range(HT):
                    pe.wait_ge(sems["ln_done"], 4 * n + t + 1)
                    for c in range(KC):
                        m = pe.transpose(bank[4 + 2 * h + c][:, t * P:(t + 1) * P],
                                         x_tok[:, HT * h + t, c * P:(c + 1) * P], ident)
                        if t == HT - 1:
                            m.then_inc(sems["xt_ps"], 1)

            wa = lambda c, a, z: (wa_hi[:, c, a:z], wa_lo[:, c, a:z])

            def a0_query(h):
                for c in range(KC):
                    for kc in range(KC):
                        m = split_mm(bank[2 * h + c][:, :], wa(kc, c * P, (c + 1) * P),
                                     (x_half(xT_hi, kc, h), x_half(xT_lo, kc, h)), kc == 0, kc == KC - 1)
                    m.then_inc(sems["a0_q_ps"], 1)

            def a0_keys_values(h):
                for t in range(HT):
                    T = HT * h + t
                    if h:
                        pe.wait_ge(sems["a0_kv"], t + 1)
                    for kc in range(KC):
                        xh, xl = x_tile(xT_hi, kc, T), x_tile(xT_lo, kc, T)
                        wh, wl = wa(kc, D, 3 * D)
                        pe.matmul(bank[4 + t][:, :], xh, wh, start=kc == 0, stop=False)
                        pe.matmul(bank[4 + t][:, :], xl, wh, start=False, stop=False)
                        m = pe.matmul(bank[4 + t][:, :], xh, wl, start=False, stop=kc == KC - 1)
                    m.then_inc(sems["a0_kv_ps"], 1)

            def a0_state(h):
                pe.wait_ge(sems["a0_kp"], h + 1)
                pe.wait_ge(sems["a0_q"], KC * (h + 1))
                for b in range(2):
                    for c in range(KC):
                        for t in range(2):
                            T = HT * h + 2 * b + t
                            m = pe.matmul(bank[2 * h + b][:, c * 256:c * 256 + P + 1],
                                          k_tok[:, T, c * P:(c + 1) * P], v_buf[:, T, c, :],
                                          start=t == 0, stop=t == 1)
                    m.then_inc(sems["a0_st_ps"], 1)

            def a0_attend(h):
                pe.wait_ge(sems["a0_state"], 2 * (h + 1))
                for t in range(HT):
                    T = HT * h + t
                    if h:
                        pe.wait_ge(sems["a0_attn"], t + 1)
                    else:
                        pe.wait_ge(sems["a0_kv"], HT + t + 1)
                    for c in range(KC):
                        m = pe.matmul(bank[4 + t][:, c * 256:c * 256 + BLK], q_buf[:, c, T * P:(T + 1) * P],
                                      state[:, KC * (T // 2) + c, :], start=True, stop=True)
                    m.then_inc(sems["a0_at_ps"], 1)

            def a0_transpose(h):
                for t in range(HT):
                    T = HT * h + t
                    pe.wait_ge(sems["a0_attn"], T + 1)
                    for c in range(KC):
                        m = pe.transpose(bank[2 * h + c][:, t * P:(t + 1) * P], ek[:, T, c * P:(c + 1) * P], ident)
                        if t == HT - 1:
                            m.then_inc(sems["a0_aT_ps"], 1)

            def a0_project(h):
                pe.wait_ge(sems["a0_aT_lo"], KC * (h + 1))
                for t in range(HT):
                    if t % 2 == 0:
                        pe.wait_ge(sems["a0_attn"], HT + 2 * h + t // 2 + 1)
                    o = bank[4 + 2 * h + t // 2][:, (t % 2) * D:(t % 2 + 1) * D]
                    for kc in range(KC):
                        a = kc * 512 + t * P
                        ah, al = h_hi[:, h, a:a + P], h_lo[:, h, a:a + P]
                        wh, wl = wa(kc, 3 * D, 4 * D)
                        pe.matmul(o, ah, wh, start=kc == 0, stop=False)
                        pe.matmul(o, ah, wl, start=False, stop=False)
                        m = pe.matmul(o, al, wh, start=False, stop=kc == KC - 1)
                    if t % 2:
                        m.then_inc(sems["a0_o_ps"], 1)

            pe.wait_ge(sems["xt_lo"], 1)
            pe.wait_ge(sems["wa_lo_kv"], 1)
            a0_keys_values(0)
            pe.wait_ge(sems["wa_lo_done"], 1)
            a0_query(0)
            pe.wait_ge(sems["xt_lo"], 2)
            a0_keys_values(1)
            a0_state(0)
            a0_query(1)
            a0_attend(0)
            a0_state(1)
            pe.wait_ge(sems["in_small"], 16 * 7)
            a0_transpose(0)
            a0_attend(1)
            pe.wait_ge(sems["wa_lo_done"], 2)
            a0_project(0)
            a0_transpose(1)
            a0_project(1)

            def ffn_up(kind, pbase, ubase, sbase, i, k, parts=None, fresh=None):
                h = k % 2
                slot = (k // 2) % 2
                if h == 0:
                    pe.wait_ge(sems["pack_lo"], i * 2 + (pbase + k // 2 + 1))
                wh, wl = pk_hi[:, slot, :], pk_lo[:, slot, :]

                def product(o, col, width, x_c, name, fresh=None):
                    def w(kc):
                        a = col + kc * width + x_c
                        return wh[:, a:a + P], wl[:, a:a + P]

                    both_chunks(o, w, lambda kc: (x_half(xT_hi, kc, h), x_half(xT_lo, kc, h)), fresh
                                ).then_inc(sems[name], 1)

                if kind == "f1":
                    s = i * 4 + (sbase + k)
                    if parts != (1,):
                        pe.wait_ge(sems["hid_mul"], s - 1)
                        product(bank[(3 * k) % 4][:, :], 0, P, 0, "gate_ready", fresh)
                    if parts == (0,):
                        return
                    if routed(i, k):
                        pe.wait_ge(sems["silu_done"], s)
                        pe.matmul(bank[(3 * k + 1) % 4][:, :], wh[0:2 * E1, 3 * D:3 * D + P],
                                  cwT[:, h * 512:(h + 1) * 512], start=True, stop=True).then_inc(sems["cw_ready"], 1)
                        pe.wait_ge(sems["m1_done"], i * 4 + (k - U_S + M1_0))
                    product(bank[(3 * k + 2) % 4][:, :], D, P, 0, "up_ready")
                    return
                for c in parts or range(KC):
                    s = i * 8 + (sbase + 2 * k + c)
                    if not isinstance(s, int) or s >= 2:
                        pe.wait_ge(sems["hid_mul"], s - 1)
                    product(bank[2 * c][:, :], 0, D, c * P, "gate_ready", fresh if c == 0 else None)
                    if kind == "f0":
                        product(bank[2 * c + 1][:, :], KC * D, D, c * P, "up_ready")

            def ffn_down(kind, pbase, ubase, sbase, i, k, tiles=range(HT)):
                h = k % 2
                slot = (k // 2) % 2
                chunks = 1 if kind == "f1" else KC
                dcol = {"x0": 0, "f0": 2 * KC * D, "f1": 2 * D}[kind]
                s_last = i * (4 * chunks) + (sbase + chunks * (k + 1))
                pe.wait_ge(sems["hid_lo"], s_last)
                if kind != "f1":
                    u = i * 4 + (ubase + k)
                    if not isinstance(u, int) or u >= 2:
                        pe.wait_ge(sems["acc_done"], (u - 1) * 4)
                for t in tiles:
                    o = bank[4 + 2 * h + t // 2][:, (t % 2) * D:(t % 2 + 1) * D]
                    for kc in range(chunks):
                        hh = h_hi[:, h, kc * 512 + t * P:kc * 512 + (t + 1) * P]
                        hl = h_lo[:, h, kc * 512 + t * P:kc * 512 + (t + 1) * P]
                        wh = pk_hi[:, slot, dcol + kc * D:dcol + (kc + 1) * D]
                        wl = pk_lo[:, slot, dcol + kc * D:dcol + (kc + 1) * D]
                        keep_open = kind == "f1"
                        pe.matmul(o, hh, wh, start=kc == 0 and not keep_open, stop=False, skip_group_check=keep_open)
                        pe.matmul(o, hh, wl, start=False, stop=False, skip_group_check=keep_open)
                        m = pe.matmul(o, hl, wh, start=False, stop=kc == chunks - 1 and not keep_open,
                                      skip_group_check=keep_open)
                    if kind != "f1" and t % 2:
                        m.then_inc(sems["out_ready"], 1)
                return m

            def ffn(kind, pbase, ubase, sbase, steps, halves, before_second, before_unit=None):
                args = (kind, pbase, ubase, sbase)
                ffn_up(*args, 0, 0, None, halves[0])
                before_second()

                def body(i, last):
                    for k in range(4):
                        if before_unit and isinstance(i, int) and 4 * i + k + 1 == before_unit[0]:
                            before_unit[1]()
                        if last and k == 2:
                            ffn_up(*args, i, 3, (0,))
                            ffn_down(*args, i, 2, (0, 1))
                            ffn_up(*args, i, 3, (1,))
                            m = ffn_down(*args, i, 2, (2, 3))
                        else:
                            if k < 3:
                                first = isinstance(i, int) and 4 * i + k == 0
                                ffn_up(*args, i, k + 1, None, halves[1] if first else None)
                            elif not last:
                                ffn_up(*args, i + 1, 0)
                            m = ffn_down(*args, i, k)
                        if kind == "f1":
                            m.then_inc(sems["down_done"], 1)

                steps_of(pe, kind, steps, body)

            pe.sem_inc(sems["down_done"], DOWN_0)
            transposes(0)
            ffn("x0", BASE_X0, 0, 0, PACKS_X0 // 2, (0, 1), lambda: transposes(1))

            def wait_x(n):
                pe.wait_ge(sems["xt_hi"], 2 + KC * (n + 1))
                pe.wait_ge(sems["xt_lo"], 2 + KC * (n + 1))

            def route(n, router):
                h = n % 2
                for t in range(HT):
                    o = bank[4 + 2 * h][:, t * 2 * E0:(t + 1) * 2 * E0]
                    prods = [(x, kc) for kc in range(KC) for x in (xT_hi, xT_lo)]
                    for j, (x, kc) in enumerate(prods):
                        m = pe.matmul(o, x_tile(x, kc, HT * h + t), rw[:, kc, router, :, :],
                                      start=j == 0, stop=j == len(prods) - 1)
                m.then_inc(sems["rt_ps"], 1)

            transposes(2)

            def second_f0():
                transposes(3)
                route(2, 0)
                wait_x(3)
                route(3, 0)
                pe.wait_ge(sems["rt_lg"], 2)

            ffn("f0", BASE_F0, 2 * PACKS_X0, 4 * PACKS_X0, PACKS_F0 // 2, (2, None), second_f0)

            def a1_query_key(h, j):
                if h and j:
                    pe.wait_ge(sems["a1_q"], KC * (h + 1))
                for c in range(KC):
                    roll = ROLL * c
                    both_chunks(a1_bank(h, j, c)[:, :], lambda kc: wa(kc, j * D + c * P, j * D + (c + 1) * P),
                                lambda kc: (x_half(xT_hi, kc, h, roll), x_half(xT_lo, kc, h, roll)),
                                4 + h if j == 0 and c == 0 else None
                                ).then_inc(sems["a1_k_ps" if j else "a1_q_ps"], 1)

            def a1_value(h):
                for t in range(HT):
                    T = HT * h + t
                    if t >= 2:
                        pe.wait_ge(sems["a1_v"], T - 1)
                    for c in range(KC):
                        o = bank[4 + 2 * h + t % 2][:, c * D:(c + 1) * D]
                        for kc in range(KC):
                            xh, xl = x_tile(xT_hi, kc, T, ROLL * c), x_tile(xT_lo, kc, T, ROLL * c)
                            wh, wl = wa(kc, 2 * D, 3 * D)
                            pe.matmul(o, xh, wh, start=kc == 0, stop=False)
                            pe.matmul(o, xh, wl, start=False, stop=False)
                            m = pe.matmul(o, xl, wh, start=False, stop=kc == KC - 1)
                    m.then_inc(sems["a1_v_ps"], 1)

            def a1_scores(T):
                if T % HT == 0:
                    pe.wait_ge(sems["a1_q"], KC * (T // HT + 1))
                if T >= 2:
                    pe.wait_ge(sems["a1_s"], T - 1)
                pe.wait_ge(sems["a1_kx0"], T + 1)
                pe.wait_ge(sems["a1_kx1"], T + 1)
                for c in range(KC):
                    for j in range(NG):
                        g = T * P + j * GS
                        m = pe.matmul(bank[T % 2][j * GS:(j + 1) * GS, c * 256:(c + 1) * 256],
                                      q_buf[:, c, g:g + GS],
                                      kx[:, KC * (T % 2) + c, j * HC * GS:(j + 1) * HC * GS],
                                      start=True, stop=True, tile_position=(0, j * GS))
                m.then_inc(sems["a1_s_ps"], 1)

            def a1_values(T):
                h, t = T // HT, T % HT
                pe.wait_ge(sems["a1_pT"], T + 1)
                if T == 0:
                    pe.wait_ge(sems["v_ones"], 1)
                if t < 2:
                    pe.wait_ge(sems["a1_v"], HT * (h + 1))
                else:
                    pe.wait_ge(sems["a1_o"], T - 1)
                for hd in range(HEADS):
                    for j in range(NG):
                        rows = slice(j * GS, (j + 1) * GS)
                        m = pe.matmul(bank[4 + 2 * h + t % 2][rows, hd * (HD + 1):(hd + 1) * (HD + 1)],
                                      pT[rows, T % 2, hd * GS:(hd + 1) * GS], v1[rows, T, hd, :],
                                      start=True, stop=True, tile_position=(j * GS, j * GS))
                m.then_inc(sems["a1_o_ps"], 1)

            pe.wait_ge(sems["wa1_lo"], 1)
            transposes(4)
            a1_query_key(0, 0)
            a1_query_key(0, 1)
            transposes(5)
            a1_value(0)
            for T in range(TILES + LAG_A1):
                if T < TILES:
                    a1_scores(T)
                if T >= LAG_A1:
                    a1_values(T - LAG_A1)
                if T == 0:
                    a1_query_key(1, 0)
                if T == 1:
                    a1_query_key(1, 1)
                if T == 2:
                    a1_value(1)

            def x1_scores(T):
                b = T // 2
                if T % 2 == 0:
                    pe.wait_ge(sems["pack_lo"], BASE_X1 + b + 1)
                if T >= 2:
                    pe.wait_ge(sems["x1_s"], T - 1)
                for kc in range(KC):
                    xh, xl = x_tile(xT_hi, kc, T), x_tile(xT_lo, kc, T)
                    wh, wl = (x1_pack(buf, b)[:, kc * D:(kc + 1) * D] for buf in ("hi", "lo"))
                    pe.matmul(bank[T % 2][:, 0:D], xh, wh, start=kc == 0, stop=False)
                    pe.matmul(bank[T % 2][:, 0:D], xh, wl, start=False, stop=False)
                    m = pe.matmul(bank[T % 2][:, 0:D], xl, wh, start=False, stop=kc == KC - 1)
                m.then_inc(sems["x1_s_ps"], 1)

            def x1_transpose(T):
                pe.wait_ge(sems["x1_exp"], T + 1)
                if T >= 2:
                    pe.wait_ge(sems["x1_pT_lo"], T - 1)
                for c in range(KC):
                    m = pe.transpose(bank[2 + T % 2][:, c * P:(c + 1) * P], sm[:, T % 4, c * P:(c + 1) * P], ident)
                m.then_inc(sems["x1_pT_ps"], 1)

            def x1_read(T):
                b, h, t = T // 2, T // HT, T % HT
                pe.wait_ge(sems["x1_pT_lo"], T + 1)
                if t >= 2:
                    pe.wait_ge(sems["x1_out"], T - 1)
                o = bank[4 + 2 * h + t % 2][:, 0:D]
                for kc in range(KC):
                    ph, pl = h_hi[:, T % 2, kc * P:(kc + 1) * P], h_lo[:, T % 2, kc * P:(kc + 1) * P]
                    a = KC * D + kc * D
                    wh, wl = (x1_pack(buf, b)[:, a:a + D] for buf in ("hi", "lo"))
                    pe.matmul(o, ph, wh, start=kc == 0, stop=False)
                    pe.matmul(o, ph, wl, start=False, stop=False)
                    m = pe.matmul(o, pl, wh, start=False, stop=kc == KC - 1)
                m.then_inc(sems["x1_o_ps"], 1)

            transposes(6)
            wait_x(6)
            for T in range(TILES + LAG_X1):
                if T < TILES:
                    x1_scores(T)
                if T == 2:
                    transposes(7)
                if T == 3:
                    wait_x(7)
                if LAG_PT <= T < TILES + LAG_PT:
                    x1_transpose(T - LAG_PT)
                if T >= LAG_X1:
                    x1_read(T - LAG_X1)

            def open_sums(h):
                pe.wait_ge(sems["rt_lg"], 3 + h)
                for j in range(2):
                    pe.matmul(bank[4 + 2 * h + j][:, :], zero_r[:, 0:P], zero_r[:, :], start=True, stop=False,
                              skip_group_check=True)

            def second_f1():
                transposes(9)
                route(8, 1)
                wait_x(9)
                route(9, 1)
                open_sums(0)
                open_sums(1)

            def combine_rows():
                pe.wait_ge(sems["rt_stack"], 1)
                pe.wait_ge(sems["silu_done"], 4 * (PACKS_X0 + PACKS_F0) + U_S)
                for h, b in enumerate(CW_BANKS):
                    for t in range(HT):
                        m = pe.transpose(bank[b][0:2 * E1, t * P:(t + 1) * P], stack[:, HT * h + t, :], ident)
                    m.then_inc(sems["cwT_ps"], 1)
                pe.wait_ge(sems["cwT_done"], 2)

            transposes(8)
            ffn("f1", BASE_F1, 2 * (PACKS_X0 + PACKS_F0), 4 * (PACKS_X0 + PACKS_F0), PACKS_F1 // 2, (8, None), second_f1,
                (U_S, combine_rows))

        @block.scalar
        def _(act):
            A = nc.scalar.activation

            def pack_hi(slot, width, nth, free=None, to=None):
                act.wait_ge(raw_loaded[slot], nth * 16)
                if free:
                    act.wait_ge(sems[free[0]], free[1])
                A(pk_hi[:, slot, 0:width] if to is None else to, pk_raw[:, slot, 0:width], ACT.Copy
                  ).then_inc(sems["pack_hi"], 1)

            def xT_high(n, wrap=False):
                h = n % 2
                for c in range(KC):
                    act.wait_ge(sems["xt_ps"], KC * n + c + 1)
                    src = bank[4 + 2 * h + c][:, :].rearrange("p (b s) -> p b s", b=2)
                    if wrap:
                        A(xT_hi[:, c, 2 * h:2 * h + 2, S:SX], src[:, :, 0:ROLL], ACT.Copy)
                    A(xT_hi[:, c, 2 * h:2 * h + 2, 0:S], src, ACT.Copy).then_inc(sems["xt_hi"], 1)

            def x_high(h):
                act.wait_ge(sems[f"in_xT{h}"], 16)
                A(xT_hi[:, :, 2 * h:2 * h + 2, 0:S],
                  q_buf[:, :, h * 512:(h + 1) * 512].rearrange("p c (b s) -> p c b s", b=2), ACT.Copy
                  ).then_inc(sems["xt_hi"], 1)

            def w_high(name, cols):
                act.wait_ge(sems[f"in_w0_{name}"], 16)
                A(wa_hi[:, :, cols], wa_raw[:, :, cols], ACT.Copy).then_inc(sems["wa_hi_done"], 1)

            x_high(0)
            w_high("kv", slice(D, 3 * D))
            w_high("q", slice(0, D))
            x_high(1)
            act.wait_ge(sems["in_small"], 16 * 7)
            for h in range(2):
                act.wait_ge(sems["a0_kv"], HT * (h + 1))
                A(ek[:, HT * h:HT * (h + 1), :], k_tok[:, HT * h:HT * (h + 1), :], ACT.Exp).then_inc(sems["a0_ek"], 1)
                for c in range(KC):
                    act.wait_ge(sems["a0_q_ps"], KC * h + c + 1)
                    A(eq[:, c, h * 512:(h + 1) * 512], bank[2 * h + c][:, :], ACT.Exp,
                      bias=bcol[:, c:c + 1]).then_inc(sems["a0_eq"], 1)
            w_high("o", slice(3 * D, 4 * D))
            A(rw[:, :, :, 0, :], rw_raw[:, :, :].rearrange("p c (r e) -> p c r e", e=E0), ACT.Copy
              ).then_inc(sems["small_ready"], 1)
            pack_hi(0, W_X0, 1)
            for h in range(2):
                for c in range(KC):
                    act.wait_ge(sems["a0_aT_ps"], KC * h + c + 1)
                    A(h_hi[:, h, c * 512:(c + 1) * 512], bank[2 * h + c][:, :], ACT.Copy).then_inc(sems["a0_aT_hi"], 1)

            def ffn(kind, pbase, ubase, sbase, steps, width, next_width, other_half, after_first=None,
                    before_unit=None):
                chunks = 1 if kind == "f1" else KC

                def body(i, last):
                    for k in range(4):
                        if after_first and isinstance(i, int) and 4 * i + k == 1:
                            after_first()
                        if before_unit and isinstance(i, int) and 4 * i + k == before_unit[0]:
                            before_unit[1]()
                        h, p = k % 2, i * 2 + (pbase + k // 2)
                        u = i * 4 + (ubase + k)
                        for c in range(chunks):
                            s = i * (4 * chunks) + (sbase + chunks * k + c)
                            r = (chunks * k + c) % 2
                            gate = bank[(3 * k) % 4] if kind == "f1" else bank[2 * c]
                            act.wait_ge(sems["gate_ready"], s + 1)
                            if not isinstance(s, int) or s >= 2:
                                act.wait_ge(sems["hid_mul"], s - 1)
                            A(sil[:, r, :], gate[:, :], ACT.Silu).then_inc(sems["silu_done"], 1)
                            if isinstance(i, int) and 4 * i + k == 0 and c == chunks - 1:
                                xT_high(other_half)
                            act.wait_ge(sems["hid_mul"], s + 1)
                            if c == 0 and (not isinstance(u, int) or u >= 2):
                                if kind == "f1":
                                    act.wait_ge(sems["down_done"], i * 4 + (DOWN_0 + k - 1))
                                else:
                                    act.wait_ge(sems["out_ready"], (u - 1) * 2)
                            A(h_hi[:, h, c * 512:(c + 1) * 512], hraw[:, r, :], ACT.Copy).then_inc(sems["hid_hi"], 1)
                        if h == 0:
                            w = next_width if last and k == 2 else width
                            if w:
                                slot = (k // 2 + 1) % 2
                                nth = i + ((pbase + k // 2 + 1) // 2 + 1)
                                if kind == "f1":
                                    free = ("down_done", i * 4 + (DOWN_0 + k))
                                elif isinstance(p, int) and p == 0:
                                    free = None
                                else:
                                    free = ("out_ready", p * 4)
                                pack_hi(slot, w, nth, free)

                steps_of(act, kind, steps, body)

            xT_high(0)
            ffn("x0", BASE_X0, 0, 0, PACKS_X0 // 2, W_X0, W_F0, 1)
            xT_high(2)

            def second_f0():
                act.wait_ge(sems["rt_lg"], 2)
                A(inh[:, :, :], lg[:, :, :], ACT.Sigmoid).then_inc(sems["rt_sig"], 1)
                act.wait_ge(sems["rt_dist"], 1)
                A(wz[:, :, :], dist[:, :, :], ACT.Exp, scale=-10.0)
                A(fb[:, :, :], dist[:, :, :], ACT.Exp, scale=-1.0 / 0.3).then_inc(sems["rt_exp"], 1)
                act.wait_ge(sems["in_w1"], 16)
                act.wait_ge(sems["a0_o_ps"], 4)
                A(wa_hi[:, :, 0:3 * D], wa_raw[:, :, 0:3 * D], ACT.Copy).then_inc(sems["wa1_hi"], 1)

            ffn("f0", BASE_F0, 2 * PACKS_X0, 4 * PACKS_X0, PACKS_F0 // 2, W_F0, W_X1, 3, second_f0)

            def a1_keys(h):
                for c in range(KC):
                    act.wait_ge(sems["a1_k_ps"], KC * h + c + 1)
                    A(k_T[:, c, h * 512:(h + 1) * 512], a1_bank(h, 1, c)[:, :], ACT.Identity,
                      bias=bcol[:, 4 + c:5 + c]).then_inc(sems["a1_k"], 1)
                act.wait_ge(sems["a1_k"], KC * (h + 1))

            def a1_expand(T):
                if T >= 2:
                    act.wait_ge(sems["a1_s_ps"], T - 1)
                to = kx[:, KC * (T % 2) + 1, :].rearrange("p (g h k) -> p g h k", g=NG, h=HC)
                of = k_T[:, 1, T * P:(T + 1) * P].rearrange("p (g k) -> p g k", g=NG)
                for hd in range(HC):
                    m = A(to[:, :, hd, :], of, ACT.Copy, scale=head8[:, hd:hd + 1])
                m.then_inc(sems["a1_kx1"], 1)

            xT_high(4, wrap=True)
            a1_keys(0)
            xT_high(5, wrap=True)
            a1_expand(0)
            a1_expand(1)

            for T in range(TILES):
                act.wait_ge(sems["a1_sub"], T + 1)
                A(sm[:, T % 4, :], sm[:, T % 4, :], ACT.Exp).then_inc(sems["a1_exp"], 1)
                if T == 1:
                    a1_keys(1)
                if T + 2 < TILES:
                    a1_expand(T + 2)
                if T == 0:
                    pack_hi(1, W_X1, (BASE_X1 + 1) // 2 + 1, ("out_ready", 4 * BASE_X1))
                if T >= 6:
                    b = T - 4
                    pack_hi(b % 2, W_X1, (BASE_X1 + b) // 2 + 1, ("a1_v_ps", TILES), x1_pack("hi", b))

            def x1_high(T):
                act.wait_ge(sems["x1_pT_ps"], T + 1)
                if T >= 2:
                    act.wait_ge(sems["x1_o_ps"], T - 1)
                A(h_hi[:, T % 2, 0:D], bank[2 + T % 2][:, 0:D], ACT.Copy).then_inc(sems["x1_pT_hi"], 1)
                if T == 3:
                    pack_hi(0, W_F1, BASE_F1 // 2 + 1, ("x1_o_ps", 2))

            xT_high(6)
            for T in range(TILES + LAG_PT):
                if T >= LAG_PT:
                    x1_high(T - LAG_PT)
                if T < TILES:
                    act.wait_ge(sems["x1_max"], T + 1)
                    A(sm[:, T % 4, 0:D], sm[:, T % 4, 0:D], ACT.Exp, bias=mx[:, T, 0:1],
                      accum_out=rs[:, T, 0:1]).then_inc(sems["x1_exp"], 1)
                if T == 2:
                    xT_high(7)

            xT_high(8)

            def second_f1():
                act.wait_ge(sems["rt_dist"], 2)
                A(fb[:, :, :], inh[:, :, :], ACT.Exp).then_inc(sems["rt_exp1"], 1)

            def combine_rows():
                for h, b in enumerate(CW_BANKS):
                    act.wait_ge(sems["cwT_ps"], h + 1)
                    A(cwT[:, h * 512:(h + 1) * 512], bank[b][0:2 * E1, :], ACT.Copy).then_inc(sems["cwT_done"], 1)

            act.wait_ge(sems["x1_o_ps"], TILES)
            ffn("f1", BASE_F1, 2 * (PACKS_X0 + PACKS_F0), 4 * (PACKS_X0 + PACKS_F0), PACKS_F1 // 2, W_F1, 0,
                9, second_f1, (U_S, combine_rows))

        @block.gpsimd
        def _(pool):
            links = [0]

            def link(ins):
                links[0] += 1
                ins.then_inc(sems["pool_link"], 1)
                pool.wait_ge(sems["pool_link"], links[0])

            def pack_low(p, slot, width, to=None, hi=None):
                pool.wait_ge(sems["pack_hi"], p + 1)
                if to is None:
                    to, hi = pk_lo[:, slot, 0:width], pk_hi[:, slot, 0:width]
                pool.tensor_tensor(to, pk_raw[:, slot, 0:width], hi.bitcast(F32), ALU.subtract
                                   ).then_inc(sems["pack_lo"], 1)

            def rstd_of(n):
                h = n % 2
                pool.wait_ge(sems["ln_var"], n + 1)
                pool.tensor_tensor(rstd[:, HT * h:HT * (h + 1)], var_e[:, HT * h:HT * (h + 1)], mhalf[:, :],
                                   ALU.pow).then_inc(sems["ln_rstd"], 1)

            pool.memset(mhalf[:, :], -0.5)
            pool.memset(v_buf[:, :, :, P:P + 1], 1.0).then_inc(sems["ones_ready"], 1)
            pool.wait_ge(sems["ones_ready"], 1)

            def w_low(n, cols):
                pool.wait_ge(sems["wa_hi_done"], n)
                pool.tensor_tensor(wa_lo[:, :, cols], wa_raw[:, :, cols], wa_hi[:, :, cols].bitcast(F32),
                                   ALU.subtract).then_inc(sems["wa_lo_done"], 1)

            w_low(2, slice(0, D))
            pool.wait_ge(sems["in_small"], 16 * 7)
            pool.wait_ge(sems["in_x"], 16)
            pool.tensor_tensor(x_tok[:, :, :], x_tok[:, :, :],
                               brow[:, 2 * D:3 * D].unsqueeze(1).to_broadcast([P, TILES, D]), ALU.add
                               ).then_inc(sems["a0_xb"], 1)
            w_low(3, slice(3 * D, 4 * D))
            pool.wait_ge(sems["small_ready"], 1)
            link(pool.tensor_tensor(rw[:, :, :, 1, :], rw_raw[:, :, :].rearrange("p c (r e) -> p c r e", e=E0),
                                    rw[:, :, :, 0, :].bitcast(F32), ALU.subtract))
            pack_low(0, 0, W_X0)
            for h in range(2):
                rstd_of(h)

            def ffn(kind, pbase, ubase, sbase, steps, width, next_width, norms, after_unit=None):
                chunks = 1 if kind == "f1" else KC

                def body(i, last):
                    for k in range(4):
                        h, p = k % 2, i * 2 + (pbase + k // 2)
                        for c in range(chunks):
                            s = i * (4 * chunks) + (sbase + chunks * k + c)
                            r = (chunks * k + c) % 2
                            pool.wait_ge(sems["hid_hi"], s + 1)
                            pool.tensor_tensor(h_lo[:, h, c * 512:(c + 1) * 512], hraw[:, r, :],
                                               h_hi[:, h, c * 512:(c + 1) * 512].bitcast(F32),
                                               ALU.subtract).then_inc(sems["hid_lo"], 1)
                        if h == 0:
                            w = next_width if last and k == 2 else width
                            if w:
                                pack_low(p + 1, (k // 2 + 1) % 2, w)
                        if after_unit and isinstance(i, int) and 4 * i + k == after_unit[0]:
                            after_unit[1]()

                steps_of(pool, kind, steps, body)
                rstd_of(norms)

            ffn("x0", BASE_X0, 0, 0, PACKS_X0 // 2, W_X0, W_F0, 2)
            rstd_of(3)
            pool.wait_ge(sems["a0_st_ps"], B)
            pool.memset(v1[:, :, :, HD:HD + 1], 1.0).then_inc(sems["v_ones"], 1)

            def attention_low():
                pool.wait_ge(sems["wa1_hi"], 1)
                pool.tensor_tensor(wa_lo[:, :, 0:3 * D], wa_raw[:, :, 0:3 * D], wa_hi[:, :, 0:3 * D].bitcast(F32),
                                   ALU.subtract).then_inc(sems["wa1_lo"], 1)

            ffn("f0", BASE_F0, 2 * PACKS_X0, 4 * PACKS_X0, PACKS_F0 // 2, W_F0, W_X1, 4, (2, attention_low))

            rstd_of(5)

            def a1_expand(T):
                pool.wait_ge(sems["a1_k"], KC * (T // HT + 1))
                if T >= 2:
                    pool.wait_ge(sems["a1_s_ps"], T - 1)
                pool.tensor_tensor(
                    kx[:, KC * (T % 2), :].rearrange("p (g h k) -> p g h k", g=NG, h=HC),
                    k_T[:, 0, T * P:(T + 1) * P].rearrange("p (g k) -> p g k", g=NG).unsqueeze(2)
                    .to_broadcast([P, NG, HC, GS]),
                    head8.unsqueeze(1).unsqueeze(3).to_broadcast([P, NG, HC, GS]),
                    ALU.mult).then_inc(sems["a1_kx0"], 1)

            def a1_shift(T):
                pool.wait_ge(sems["a1_max"], T + 1)
                v = sm[:, T % 4, :].rearrange("p (h k) -> p h k", h=HEADS)
                pool.tensor_tensor(v, v, mx[:, T, :].unsqueeze(2).to_broadcast([P, HEADS, GS]),
                                   ALU.subtract).then_inc(sems["a1_sub"], 1)

            def a1_residual(h):
                t0, t1 = HT * h, HT * (h + 1)
                pool.wait_ge(sems["a1_o"], HT * (h + 1))
                pool.tensor_tensor(x_tok[:, t0:t1, 0:P], x_tok[:, t0:t1, 0:P], o_tok[:, t0:t1, 0:P],
                                   ALU.add).then_inc(sems["a1_res"], 1)
                pool.wait_ge(sems[f"a1_oroll{h}"], 48)
                pool.tensor_tensor(x_tok[:, t0:t1, P:D], x_tok[:, t0:t1, P:D], o_roll[:, t0:t1, :],
                                   ALU.add).then_inc(sems["a1_res"], 1)

            a1_expand(0)
            a1_expand(1)
            for T in range(TILES):
                a1_shift(T)
                if T + 2 < TILES:
                    a1_expand(T + 2)
                if T == 0:
                    pack_low(BASE_X1 + 1, 1, W_X1)
                if T == 6:
                    pack_low(BASE_X1 + 2, 0, W_X1, x1_pack("lo", 2), x1_pack("hi", 2))
            a1_residual(0)
            rstd_of(6)
            pack_low(BASE_X1 + 3, 1, W_X1, x1_pack("lo", 3), x1_pack("hi", 3))
            a1_residual(1)
            rstd_of(7)

            pack_low(BASE_F1, 0, W_F1)
            rstd_of(8)
            rstd_of(9)
            ffn("f1", BASE_F1, 2 * (PACKS_X0 + PACKS_F0), 4 * (PACKS_X0 + PACKS_F0), PACKS_F1 // 2, W_F1, 0, 10)
            rstd_of(11)

        @block.vector
        def _(dve):
            links = [0]

            def link(ins):
                links[0] += 1
                ins.then_inc(sems["dve_link"], 1)
                dve.wait_ge(sems["dve_link"], links[0])

            TT, TS, STT = dve.tensor_tensor, dve.tensor_scalar, dve.scalar_tensor_tensor

            def norm_stats(n):
                h = n % 2
                t0 = HT * h
                for t in range(HT):
                    m = dve.bn_stats(stats[:, t, :], x_tok[:, t0 + t, :])
                link(m)
                for t in range(HT):
                    m = dve.bn_aggr(mv[:, t0 + t, :], stats[:, t, :])
                link(m)
                TS(var_e[:, t0:t0 + HT], mv[:, t0:t0 + HT, 1], LN_EPS, None, ALU.add).then_inc(sems["ln_var"], 1)

            def norm_apply(n):
                t0 = HT * (n % 2)
                dve.wait_ge(sems["ln_rstd"], n + 1)
                for t in range(HT):
                    T = t0 + t
                    TS(x_tok[:, T, :], x_tok[:, T, :], mv[:, T, 0:1], rstd[:, T:T + 1],
                       ALU.subtract, ALU.mult).then_inc(sems["ln_done"], 1)

            def norm(n):
                norm_stats(n)
                norm_apply(n)

            def xT_low(n, wrap=False):
                h = n % 2
                for c in range(KC):
                    dve.wait_ge(sems["xt_hi"], 2 + KC * n + c + 1)
                    src = bank[4 + 2 * h + c][:, :].rearrange("p (b s) -> p b s", b=2)
                    hb = slice(2 * h, 2 * h + 2)
                    if wrap:
                        TT(xT_lo[:, c, hb, S:SX], src[:, :, 0:ROLL], xT_hi[:, c, hb, 0:ROLL].bitcast(F32), ALU.subtract)
                    TT(xT_lo[:, c, hb, 0:S], src, xT_hi[:, c, hb, 0:S].bitcast(F32), ALU.subtract
                       ).then_inc(sems["xt_lo"], 1)

            def top2(score):
                for T in range(TILES):
                    m = dve.max(top[:, T, :], score[:, T, :])
                link(m)
                for T in range(TILES):
                    m = dve.max_index(top_i[:, T, :], top[:, T, :], score[:, T, :])
                link(m)
                link(dve.tensor_copy(top_f[:, :, :], top_i[:, :, :]))
                idx = iota8.unsqueeze(1).to_broadcast([P, TILES, 8])
                TT(zone[:, :, :], idx, top_f[:, :, 0:1].to_broadcast([P, TILES, 8]), ALU.is_equal)
                link(TT(pick[:, :, :], idx, top_f[:, :, 1:2].to_broadcast([P, TILES, 8]), ALU.is_equal))
                link(TT(pick[:, :, :], pick[:, :, :], zone[:, :, :], ALU.add))

            def total(o, src):
                link(dve.tensor_reduce(o, src, axis=AXX, op=ALU.add))

            def per_token(v):
                return v.unsqueeze(2).to_broadcast([P, TILES, E0])

            dve.sem_inc(sems["m1_done"], M1_0)

            def x_low(h):
                dve.wait_ge(sems[f"in_xT{h}"], 16)
                dve.wait_ge(sems["xt_hi"], h + 1)
                TT(xT_lo[:, :, 2 * h:2 * h + 2, 0:S],
                   q_buf[:, :, h * 512:(h + 1) * 512].rearrange("p c (b s) -> p c b s", b=2),
                   xT_hi[:, :, 2 * h:2 * h + 2, 0:S].bitcast(F32), ALU.subtract).then_inc(sems["xt_lo"], 1)

            def first_constants():
                dve.reciprocal(temp[:, 1:2], temp[:, 0:1])
                link(dve.tensor_copy(ids_f[:, :], ids_i[:, :]))
                cut = [float(VOCAB_CUT * e) for e in range(EX)]
                TS(route0[:, :, 0], ids_f[:, :], cut[1], None, ALU.is_lt)
                for e in range(1, EX - 1):
                    link(TS(s1[:, :], ids_f[:, :], cut[e], None, ALU.is_ge))
                    link(STT(route0[:, :, e], ids_f[:, :], cut[e + 1], s1[:, :], ALU.is_lt, ALU.mult))
                link(TS(route0[:, :, EX - 1], ids_f[:, :], cut[EX - 1], None, ALU.is_ge))

            def later_constants():
                dve.memset(zero_r[:, :].bitcast(F32), 0.0)
                link(dve.tensor_copy(cap[:, :, :], mask_w[:, :].bitcast(U8).rearrange("p (b s) -> p b s", b=B)))
                link(dve.tensor_reduce(valid[:, :], cap[:, :, :], axis=AXX, op=ALU.max))
                link(TS(cap[:, :, :], cap[:, :, :], BIG, NEG_X, ALU.mult, ALU.add))

            x_low(0)
            dve.wait_ge(sems["wa_hi_done"], 1)
            TT(wa_lo[:, :, D:3 * D], wa_raw[:, :, D:3 * D], wa_hi[:, :, D:3 * D].bitcast(F32), ALU.subtract
               ).then_inc(sems["wa_lo_kv"], 1)
            x_low(1)
            dve.wait_ge(sems["xt_lo"], 2)
            dve.wait_ge(sems["in_small"], 16 * 7)
            dve.wait_ge(sems["ones_ready"], 1)

            def a0_keys_values(h):
                for t in range(HT):
                    T = HT * h + t
                    dve.wait_ge(sems["a0_kv_ps"], T + 1)
                    TT(k_tok[:, T, :], bank[4 + t][:, 0:D], brow[:, 0:D], ALU.add)
                    TT(v_buf[:, T, :, 0:P], bank[4 + t][:, D:2 * D].rearrange("p (c d) -> p c d", c=KC),
                       brow[:, D:2 * D].rearrange("p (c d) -> p c d", c=KC), ALU.add).then_inc(sems["a0_kv"], 1)

            def a0_key_features(h):
                ks, es = (b[:, HT * h:HT * (h + 1), :].rearrange("p t d -> p (t d)") for b in (k_tok, ek))
                dve.wait_ge(sems["a0_ek"], h + 1)
                link(TS(es, es, 1.0, None, ALU.min))
                STT(ks, ks, 0.0, es, ALU.max, ALU.add).then_inc(sems["a0_kp"], 1)

            def a0_query_features(h):
                q = slice(h * 512, (h + 1) * 512)
                for c in range(KC):
                    dve.wait_ge(sems["a0_eq"], KC * h + c + 1)
                    m = TS(q_buf[:, c, q], bank[2 * h + c][:, :], bcol[:, c:c + 1], 0.0, ALU.add, ALU.max)
                link(m)
                for c in range(KC):
                    STT(q_buf[:, c, q], eq[:, c, q], 1.0, q_buf[:, c, q], ALU.min, ALU.add).then_inc(sems["a0_q"], 1)

            def a0_state(h):
                for b in range(2):
                    dve.wait_ge(sems["a0_st_ps"], 2 * h + b + 1)
                    for c in range(KC):
                        n = KC * (2 * h + b) + c
                        src = bank[2 * h + b]
                        TT(state[:, n, 0:P], src[:, c * 256:c * 256 + P], headmask, ALU.mult)
                        m = TS(state[:, n, P:BLK], head8, src[:, c * 256 + P:c * 256 + P + 1], None, ALU.mult)
                    m.then_inc(sems["a0_state"], 1)

            def a0_divide(h):
                t0, t1 = HT * h, HT * (h + 1)
                for t in range(HT):
                    dve.wait_ge(sems["a0_at_ps"], t0 + t + 1)
                    src = bank[4 + t][:, :].rearrange("p (c n) -> p c n", c=KC)
                    m = TS(mx[:, t0 + t, :].rearrange("p (c h) -> p c h", c=KC), src[:, :, P:BLK], 1e-6, None, ALU.add)
                link(m)
                link(dve.reciprocal(rs[:, t0:t1, :], mx[:, t0:t1, :]))
                for t in range(HT):
                    T = t0 + t
                    src = bank[4 + t][:, :].rearrange("p (c n) -> p c n", c=KC)
                    TT(ek[:, T, :].rearrange("p (c h d) -> p c h d", c=KC, d=HD),
                       src[:, :, 0:P].rearrange("p c (h d) -> p c h d", d=HD),
                       rs[:, T, :].rearrange("p (c h) -> p c h", c=KC).unsqueeze(3).to_broadcast([P, KC, HC, HD]),
                       ALU.mult).then_inc(sems["a0_attn"], 1)

            def a0_low(h):
                for c in range(KC):
                    dve.wait_ge(sems["a0_aT_hi"], KC * h + c + 1)
                    q = slice(c * 512, (c + 1) * 512)
                    TT(h_lo[:, h, q], bank[2 * h + c][:, :], h_hi[:, h, q].bitcast(F32), ALU.subtract
                       ).then_inc(sems["a0_aT_lo"], 1)

            def a0_residual(h):
                for j in range(2):
                    dve.wait_ge(sems["a0_o_ps"], 2 * h + j + 1)
                    T = HT * h + 2 * j
                    v = x_tok[:, T:T + 2, :].rearrange("p t d -> p (t d)")
                    TT(v, bank[4 + 2 * h + j][:, :], v, ALU.add).then_inc(sems["a0_res"], 1)
                dve.wait_ge(sems["a0_res"], 2 * (h + 1))

            a0_keys_values(0)
            a0_key_features(0)
            a0_query_features(0)
            a0_keys_values(1)
            a0_state(0)
            a0_key_features(1)
            a0_query_features(1)
            a0_divide(0)
            a0_state(1)
            a0_low(0)
            a0_divide(1)
            first_constants()
            dve.wait_ge(sems["a0_xb"], 1)
            a0_low(1)
            a0_residual(0)
            norm(0)
            a0_residual(1)
            xT_low(0)
            norm(1)

            def ffn_mul(kind, sbase, i, k, parts=None):
                chunks = 1 if kind == "f1" else KC
                for c in parts or range(chunks):
                    s = i * (4 * chunks) + (sbase + chunks * k + c)
                    r = (chunks * k + c) % 2
                    if not isinstance(s, int) or s >= 2:
                        dve.wait_ge(sems["hid_lo"], s - 1)
                    if kind == "f1":
                        dve.wait_ge(sems["silu_done"], s + 1)
                        if routed(i, k):
                            dve.wait_ge(sems["cw_ready"], i * 4 + (k + 1 - U_S))
                            TT(sil[:, r, :], bank[(3 * k + 1) % 4][:, :], sil[:, r, :], ALU.mult
                               ).then_inc(sems["m1_done"], 1)
                            dve.wait_ge(sems["m1_done"], i * 4 + (k + 1 - U_S + M1_0))
                        dve.wait_ge(sems["up_ready"], 2 * 2 * PACKS_F0 + i * 4 + (k + 1))
                        other = bank[(3 * k + 2) % 4]
                    elif kind == "f0":
                        dve.wait_ge(sems["silu_done"], s + 1)
                        dve.wait_ge(sems["up_ready"], i * 8 + (2 * k + c + 1))
                        other = bank[2 * c + 1]
                    else:
                        dve.wait_ge(sems["silu_done"], s + 1)
                        other = bank[2 * c]
                    TT(hraw[:, r, :], other[:, :], sil[:, r, :], ALU.mult).then_inc(sems["hid_mul"], 1)

            def ffn_add(weights, ubase, i, k, expert, tiles=range(HT)):
                u = i * 4 + (ubase + k)
                h = k % 2
                if k >= 2 or not isinstance(i, int) or i > 0:
                    dve.wait_ge(sems["acc_done"], (u - 1) * 4)
                for t in tiles:
                    T = HT * h + t
                    if t % 2 == 0:
                        dve.wait_ge(sems["out_ready"], u * 2 + (t // 2 + 1))
                    STT(x_tok[:, T, :], bank[4 + 2 * h + t // 2][:, (t % 2) * D:(t % 2 + 1) * D],
                        weights[:, T, expert], x_tok[:, T, :], ALU.mult, ALU.add).then_inc(sems["acc_done"], 1)

            def ffn(kind, weights, ubase, sbase, steps, norms, before_second, before_add=None):
                ffn_mul(kind, sbase, 0, 0)
                before_second()

                def body(i, last):
                    for k in range(4):
                        early = last and k == 2
                        if k < 3:
                            ffn_mul(kind, sbase, i, k + 1, (0,) if early else None)
                        elif not last:
                            ffn_mul(kind, sbase, i + 1, 0)
                        if before_add and isinstance(i, int) and 4 * i + k == 0:
                            before_add()
                        e = i * 2 + k // 2
                        ffn_add(weights, ubase, i, k, bass.ds(e, 1), (0, 1) if early else range(HT))
                        if early:
                            ffn_mul(kind, sbase, i, k + 1, (1,))
                            ffn_add(weights, ubase, i, k, bass.ds(e, 1), (2, 3))
                            dve.wait_ge(sems["acc_done"], 4 * (4 * i + ubase + k + 1))
                            norm(norms)
                steps_of(dve, kind, steps, body)
                dve.wait_ge(sems["acc_done"], 4 * (4 * steps + ubase))

            dve.wait_ge(sems["ln_done"], 8)
            ffn("x0", route0, 0, 0, PACKS_X0 // 2, 2, lambda: xT_low(1))
            xT_low(2)
            norm(3)

            def logits(m, scale_ap):
                h = m % 2
                dve.wait_ge(sems["rt_ps"], m + 1)
                t0 = HT * h
                src = bank[4 + 2 * h][:, 0:HT * 2 * E0].rearrange("p (t a e) -> p t e a", t=HT, a=2)
                if scale_ap is None:
                    dve.tensor_reduce(lg[:, t0:t0 + HT, :], src, axis=AXX, op=ALU.add).then_inc(sems["rt_lg"], 1)
                else:
                    link(dve.tensor_reduce(lg[:, t0:t0 + HT, :], src, axis=AXX, op=ALU.add))
                    TS(lg[:, t0:t0 + HT, :], lg[:, t0:t0 + HT, :], scale_ap, None, ALU.mult
                       ).then_inc(sems["rt_lg"], 1)

            def second_f0():
                xT_low(3)
                logits(0, temp[:, 1:2])
                logits(1, temp[:, 1:2])
                dve.wait_ge(sems["rt_sig"], 1)
                link(TS(zone[:, :, :], inh[:, :, :], -1.0, float(GOLD_C), ALU.mult, ALU.add))
                STT(dist[:, :, :], inh[:, :, :], float(GOLD_C), zone[:, :, :], ALU.subtract, ALU.max
                    ).then_inc(sems["rt_dist"], 1)

            def gold_weights():
                dve.wait_ge(sems["rt_dist"], 1)
                link(TS(zone[:, :, :], inh[:, :, :], float(GOLD_LO), None, ALU.is_ge))
                link(STT(pick[:, :, :], inh[:, :, :], float(GOLD_HI), zone[:, :, :], ALU.is_le, ALU.mult))
                dve.wait_ge(sems["rt_exp"], 1)
                link(TT(wz[:, :, :], wz[:, :, :], pick[:, :, :], ALU.mult))
                total(s1[:, :], wz[:, :, :])
                link(TS(none_in[:, :], s1[:, :], 1e-8, None, ALU.is_lt))
                top2(fb)
                link(TT(fb[:, :, :], fb[:, :, :], pick[:, :, :], ALU.mult))
                total(s2[:, :], fb[:, :, :])
                link(TS(s2[:, :], s2[:, :], 1e-8, None, ALU.max))
                link(dve.reciprocal(s1[:, :], s2[:, :]))
                link(TT(fb[:, :, :], fb[:, :, :], per_token(s1[:, :]), ALU.mult))
                link(TT(fb[:, :, :], fb[:, :, :], per_token(none_in[:, :]), ALU.mult))
                link(TS(s2[:, :], none_in[:, :], -1.0, 1.0, ALU.mult, ALU.add))
                link(TT(wz[:, :, :], wz[:, :, :], per_token(s2[:, :]), ALU.mult))
                link(TT(wz[:, :, :], wz[:, :, :], fb[:, :, :], ALU.add))
                total(s1[:, :], wz[:, :, :])
                link(TS(s1[:, :], s1[:, :], 1e-8, None, ALU.max))
                link(dve.reciprocal(s2[:, :], s1[:, :]))
                link(TT(gold[:, :, :], wz[:, :, :], per_token(s2[:, :]), ALU.mult))
                dve.wait_ge(sems["ln_done"], 16)

            ffn("f0", gold, 2 * PACKS_X0, 4 * PACKS_X0, PACKS_F0 // 2, 4, second_f0, gold_weights)

            def a1_queries(h):
                for c in range(KC):
                    dve.wait_ge(sems["a1_q_ps"], KC * h + c + 1)
                    TS(q_buf[:, c, h * 512:(h + 1) * 512], bank[2 + c][:, :], bcol[:, 2 + c:3 + c], None, ALU.add
                       ).then_inc(sems["a1_q"], 1)

            def a1_values(h):
                for t in range(HT):
                    T = HT * h + t
                    dve.wait_ge(sems["a1_v_ps"], T + 1)
                    src = bank[4 + 2 * h + t % 2]
                    for c in range(KC):
                        m = TT(v1[:, T, c * HC:(c + 1) * HC, 0:HD],
                               src[:, c * (D + P):c * (D + P) + P].rearrange("p (h d) -> p h d", d=HD),
                               brow[:, 3 * D + c * P:3 * D + (c + 1) * P].rearrange("p (h d) -> p h d", d=HD),
                               ALU.add)
                    m.then_inc(sems["a1_v"], 1)

            xT_low(4, wrap=True)
            norm(5)
            a1_queries(0)
            xT_low(5, wrap=True)
            a1_values(0)

            def a1_soft(T):
                dve.wait_ge(sems["a1_s_ps"], T + 1)
                v = sm[:, T % 4, :].rearrange("p (h k) -> p h k", h=HEADS)
                STT(v, bank[T % 2][:, :].rearrange("p (h k) -> p h k", h=HEADS), HD ** -0.5,
                    causal.unsqueeze(1).to_broadcast([P, HEADS, GS]), ALU.mult, ALU.add).then_inc(sems["a1_s"], 1)
                dve.wait_ge(sems["a1_s"], T + 1)
                dve.tensor_reduce(mx[:, T, :], v, axis=AXX, op=ALU.max).then_inc(sems["a1_max"], 1)

            def a1_turn(T):
                dve.wait_ge(sems["a1_exp"], T + 1)
                if T >= 2:
                    dve.wait_ge(sems["a1_o_ps"], T - 1)
                dve.transpose(pT[:, T % 2, :], sm[:, T % 4, :]).then_inc(sems["a1_pT"], 1)

            def a1_out(T):
                dve.wait_ge(sems["a1_o_ps"], T + 1)
                h, t = T // HT, T % HT
                o = bank[4 + 2 * h + t % 2][:, 0:HEADS * (HD + 1)].rearrange("p (h d) -> p h d", d=HD + 1)
                link(dve.reciprocal(rs[:, T, :], o[:, :, HD]))
                TT(o_tok[:, T, :].rearrange("p (h d) -> p h d", h=HEADS), o[:, :, 0:HD],
                   rs[:, T, :].unsqueeze(2).to_broadcast([P, HEADS, HD]), ALU.mult).then_inc(sems["a1_o"], 1)

            for T in range(TILES + LAG_A1 + 1):
                if T < TILES:
                    a1_soft(T)
                if 1 <= T <= TILES:
                    a1_turn(T - 1)
                if T == 0:
                    a1_queries(1)
                if T > LAG_A1:
                    a1_out(T - LAG_A1 - 1)
                if T == 2:
                    a1_values(1)
                if T == TILES - 2:
                    later_constants()
                if T == TILES:
                    dve.wait_ge(sems["a1_res"], 2)
                    norm(6)
            xT_low(6)

            def x1_mask(T):
                dve.wait_ge(sems["x1_s_ps"], T + 1)
                if T >= 4:
                    dve.wait_ge(sems["x1_pT_ps"], T - 3)
                STT(sm[:, T % 4, 0:D], bank[T % 2][:, 0:D], D ** -0.5, cap[:, T // 2, :], ALU.mult, ALU.min
                    ).then_inc(sems["x1_s"], 1)
                dve.wait_ge(sems["x1_s"], T + 1)
                dve.tensor_reduce(mx[:, T, 0:1], sm[:, T % 4, 0:D], axis=AXX, op=ALU.max, negate=True
                                  ).then_inc(sems["x1_max"], 1)

            def x1_low(T):
                dve.wait_ge(sems["x1_pT_hi"], T + 1)
                TT(h_lo[:, T % 2, 0:D], bank[2 + T % 2][:, 0:D], h_hi[:, T % 2, 0:D].bitcast(F32), ALU.subtract
                   ).then_inc(sems["x1_pT_lo"], 1)
                link(dve.reciprocal(rs[:, T, 1:2], rs[:, T, 0:1]))
                TT(rs[:, T, 2:3], rs[:, T, 1:2], valid[:, T // 2:T // 2 + 1], ALU.mult).then_inc(sems["x1_w"], 1)

            def x1_add(T):
                h, t = T // HT, T % HT
                dve.wait_ge(sems["x1_o_ps"], T + 1)
                dve.wait_ge(sems["x1_w"], T + 1)
                STT(x_tok[:, T, :], bank[4 + 2 * h + t % 2][:, 0:D], rs[:, T, 2:3], x_tok[:, T, :],
                    ALU.mult, ALU.add).then_inc(sems["x1_out"], 1)

            for T in range(TILES + LAG_X1):
                if T < TILES:
                    x1_mask(T)
                if T == 1:
                    dve.wait_ge(sems["a1_res"], 4)
                    norm(7)
                if LAG_PT <= T < TILES + LAG_PT:
                    x1_low(T - LAG_PT)
                if T == 2:
                    xT_low(7)
                if T == LAG_X1:
                    dve.wait_ge(sems["ln_done"], 32)
                if T >= LAG_X1:
                    x1_add(T - LAG_X1)
                if T == TILES:
                    dve.wait_ge(sems["x1_out"], HT)
                    norm_stats(8)
                if T == TILES + 1:
                    norm_apply(8)
            dve.wait_ge(sems["x1_out"], TILES)
            norm_stats(9)
            xT_low(8)
            norm_apply(9)

            f1_base = 4 * (PACKS_X0 + PACKS_F0)
            ffn_mul("f1", f1_base, 0, 0)
            xT_low(9)
            logits(2, None)
            logits(3, None)
            dve.wait_ge(sems["rt_lg"], 4)
            link(dve.tensor_reduce(s1[:, :], lg[:, :, :], axis=AXX, op=ALU.max))
            TT(inh[:, :, :], lg[:, :, :], per_token(s1[:, :]), ALU.subtract).then_inc(sems["rt_dist"], 1)
            ffn_mul("f1", f1_base, 0, 1)
            dve.wait_ge(sems["rt_exp1"], 1)
            total(s2[:, :], fb[:, :, :])
            link(dve.reciprocal(s1[:, :], s2[:, :]))
            link(TT(fb[:, :, :], fb[:, :, :], per_token(s1[:, :]), ALU.mult))
            ffn_mul("f1", f1_base, 0, 2)
            top2(fb)
            link(TT(fb[:, :, :], fb[:, :, :], pick[:, :, :], ALU.mult))
            link(dve.tensor_copy(cw_r[:, :, :], fb[:, :, :]))
            dve.tensor_copy(stack[:, :, 0:E1], cw_r[:, :, :].bitcast(F32))
            TT(stack[:, :, E1:2 * E1], fb[:, :, :], cw_r[:, :, :].bitcast(F32), ALU.subtract
               ).then_inc(sems["rt_stack"], 1)
            ffn_mul("f1", f1_base, 0, 3)
            for k in range(4):
                ffn_mul("f1", f1_base, 1, k)
            with dve.Fori(2, PACKS_F1 // 2 - 1) as i:
                for k in range(4):
                    ffn_mul("f1", f1_base, i, k)
            for k in range(3):
                ffn_mul("f1", f1_base, PACKS_F1 // 2 - 1, k)

            def last_add(h):
                dve.wait_ge(sems["down_done"], DOWN_0 + 2 * PACKS_F1 - 1 + h)
                for j in range(2):
                    T = HT * h + 2 * j
                    v = x_tok[:, T:T + 2, :].rearrange("p t d -> p (t d)")
                    m = TT(v, bank[4 + 2 * h + j][:, :], v, ALU.add)
                link(m)

            ffn_mul("f1", f1_base, PACKS_F1 // 2 - 1, 3)
            last_add(0)
            norm(10)
            last_add(1)
            norm(11)


def kernel(**inputs):
    import concourse.bacc as bacc
    from concourse.bass_utils import run_bass_kernel_spmd

    a = {k: np.asarray(v) for k, v in inputs.items()}
    f = np.float32

    def chunked(w):
        return np.ascontiguousarray(w.reshape(KC, P, -1).transpose(1, 0, 2))

    x = a["x"].reshape(B * S, D)
    ids = np.ascontiguousarray(a["itok_BxS_13_99985"].reshape(TILES, P).T)
    pad = a["mask_BxS2_bk0"].reshape(1, B * S).view(np.uint32)
    w0 = chunked(np.concatenate([a[f"L0_attn_{n}_w"].T for n in "qkvo"], 1))
    w1 = chunked(np.concatenate([a[f"L1_attn_W{n}"].T for n in "qkv"], 1))
    bcol = np.concatenate([a[n].reshape(KC, P).T for n in ("L0_attn_q_b", "L1_attn_bq", "L1_attn_bk")], 1)
    brow = np.concatenate([a[n] for n in ("L0_attn_k_b", "L0_attn_v_b", "L0_attn_o_b", "L1_attn_bv")]).reshape(1, -1)
    wr = chunked(np.concatenate([a["L0_ffn_Wr"], a["L1_ffn_gate_weight"].T], 1))

    p = np.arange(P)
    con = np.zeros((P, CONST_W), f)
    con[:, 0:P] = np.eye(P)
    con[:, P:2 * P] = (p[:, None] // HD == p[None, :] // HD)
    con[:, 2 * P:2 * P + HC] = (p[:, None] // HD == np.arange(HC)[None, :])
    con[:, P + BLK:P + BLK + GS] = np.where(np.arange(GS)[None, :] > p[:, None] % GS, NEG, 0.0)
    con[:, P + BLK + GS:P + BLK + GS + 8] = np.arange(8)[None, :]

    ctx_ = a["ctx_2048"]
    pk_x0 = np.stack([chunked(ctx_[e].T).reshape(P, -1) for e in range(EX)])
    pk_x1 = np.stack([np.concatenate([chunked(ctx_[b].T).reshape(P, -1), chunked(ctx_[b]).reshape(P, -1)], 1)
                      for b in range(B)])
    pk_f0 = np.stack([np.concatenate([chunked(a[f"L0_ffn_W{n}"][e]).reshape(P, -1) for n in "gud"], 1)
                      for e in range(E0)])
    rows = (CH_R + CH_S) * P
    gate, up, down = (np.zeros((rows, D), f) for _ in range(3))
    ns, nr = CH_S * P, E1 * F1
    gu, dn = a["L1_ffn_gate_up_weights"], a["L1_ffn_down_weights"]
    sgu, sdn = a["L1_ffn_shared_gate_up"], a["L1_ffn_shared_down"]
    gate[0:FS] = sgu[0:FS]
    up[0:FS] = sgu[FS:]
    down[0:FS] = sdn.T
    gate[ns:] = gu[:, 0:F1].reshape(nr, D)
    up[ns:] = gu[:, F1:].reshape(nr, D)
    down[ns:] = dn.transpose(0, 2, 1).reshape(nr, D)
    sel = np.zeros((rows // P, P, P), f)
    for n in range(nr):
        j, q = divmod(ns + n, P)
        sel[j, n // F1, q] = sel[j, E1 + n // F1, q] = 1.0
    pk_f1 = np.stack([np.concatenate([chunked(gate[j * P:(j + 1) * P].T).reshape(P, -1),
                                      chunked(up[j * P:(j + 1) * P].T).reshape(P, -1),
                                      down[j * P:(j + 1) * P], sel[j]], 1) for j in range(rows // P)])

    arrays = {"x_rows": x, "x_cols": x.T, "ids": ids, "pad_mask": pad, "w_attn0": w0, "w_attn1": w1,
              "bias_cols": bcol, "bias_rows": brow, "w_route": wr,
              "temperature": a["L0_ffn_temperature"].reshape(1, 1), "consts": con,
              "pk_x0": pk_x0, "pk_f0": pk_f0, "pk_x1": pk_x1, "pk_f1": pk_f1}
    arrays = {k: np.ascontiguousarray(v) for k, v in arrays.items()}
    nc = bacc.Bacc("TRN2", target_bir_lowering=False, num_devices=1)
    args = [nc.dram_tensor(f"{k}_dram", v.shape, mybir.dt.from_np(v.dtype), kind="ExternalInput").ap()
            for k, v in arrays.items()]
    out = nc.dram_tensor("out_dram", (B * S, D), F32, kind="ExternalOutput").ap()
    decoder_program(nc, *args, out)
    r = run_bass_kernel_spmd(nc, [{f"{k}_dram": v for k, v in arrays.items()}], core_ids=[0])
    return r.results[0]["out_dram"].reshape(B, S, D)
```
